# Optimizing a Trainium2 kernel written in Bass

```python
import numpy as np
import jax
import jax.numpy as jnp

def _softmax(x, axis=-1):
    return jax.nn.softmax(x, axis=axis)

def _gelu(x):
    return jax.nn.gelu(x, approximate=True)

def _silu(x):
    return jax.nn.silu(x)

def _sigmoid(x):
    return jax.nn.sigmoid(x)

def _layernorm(x, axis=-1, eps=1e-05):
    m = jnp.mean(x, axis=axis, keepdims=True)
    v = jnp.var(x, axis=axis, keepdims=True)
    return (x - m) / jnp.sqrt(v + eps)

def _scatter_add(tgt, idx, src, axis=0):
    return tgt.at[idx].add(src)

def _segment_sum(src, seg, n):
    return jax.ops.segment_sum(src, seg, n)
kernel_name = 'mk_conv_seq_d4_conv_nchw96_r2_73770f'

def setup_inputs(seed: int=0):
    np.random.seed(seed)
    _w = jnp.asarray

    def _rec_inputs():
        import jax
        import jax.numpy as jnp
        _gk = jax.random.key(seed)
        x = -0.0004039 + 1 * jax.random.normal(jax.random.fold_in(_gk, 1), (8, 48, 64, 64), jnp.float32)
        return x
    x = _rec_inputs()

    def _L0_conv_setup():
        import jax, jax.numpy as jnp
        import numpy as np
        EPS = 1e-05

        def _shift1d(x, s, axis):
            n = x.shape[axis]
            f = jnp.floor(s)
            frac = (s - f).astype(x.dtype)
            fi = f.astype(jnp.int32)

            def gather(off):
                idx = jnp.arange(n) + fi + off
                mask = (idx >= 0) & (idx < n)
                v = jnp.take(x, jnp.clip(idx, 0, n - 1), axis=axis)
                mshape = [1] * x.ndim
                mshape[axis] = n
                return v * mask.reshape(mshape).astype(x.dtype)
            return (1 - frac) * gather(0) + frac * gather(1)

        def _axial_dw(x, w_h, w_w, r):
            r = jnp.maximum(r, 1.0)
            c = x.shape[1]
            kh = w_h.shape[1]
            kw = w_w.shape[1]
            acc_h = jnp.zeros_like(x)
            for i, off in enumerate(range(-(kh // 2), kh // 2 + 1)):
                acc_h = acc_h + _shift1d(x, off * r, 2) * w_h[:, i].reshape(1, c, 1, 1)
            acc_w = jnp.zeros_like(x)
            for i, off in enumerate(range(-(kw // 2), kw // 2 + 1)):
                acc_w = acc_w + _shift1d(x, off * r, 3) * w_w[:, i].reshape(1, c, 1, 1)
            return x + acc_h + acc_w

        def _bn(x, g, b, m, v):
            sh = (1, -1, 1, 1)
            scale = g.reshape(sh) * jax.lax.rsqrt(v.reshape(sh) + EPS)
            return (x - m.reshape(sh)) * scale + b.reshape(sh)

        def _prelu(x, a):
            return jnp.where(x >= 0, x, a.reshape(1, -1, 1, 1) * x)

        def _pw(w, x):
            return jnp.einsum('oc,bchw->bohw', w, x)

        def _dwconv3(x, w, axis):
            c = x.shape[1]
            n = x.shape[axis]
            pad = [(0, 0)] * 4
            pad[axis] = (1, 1)
            xp = jnp.pad(x, pad)
            out = jnp.zeros_like(x)
            for i in range(3):
                out = out + jax.lax.slice_in_dim(xp, i, i + n, axis=axis) * w[:, i].reshape(1, c, 1, 1)
            return out

        def _coord_att(x, w1, bn1, a1, wh, ww):
            n, c, h, w = x.shape
            xh = x.mean(axis=3, keepdims=True)
            xw = jnp.transpose(x.mean(axis=2, keepdims=True), (0, 1, 3, 2))
            y = jnp.concatenate([xh, xw], axis=2)
            y = _prelu(_bn(_pw(w1, y), *bn1), a1)
            yh, yw = (y[:, :, :h], jnp.transpose(y[:, :, h:], (0, 1, 3, 2)))
            a_h = jax.nn.sigmoid(_pw(wh, yh))
            a_w = jax.nn.sigmoid(_pw(ww, yw))
            return x * a_w * a_h

        def _forward(x, r_m, wh_m, ww_m, r_l, wh_l, ww_l, w_fuse, bnf_g, bnf_b, bnf_m, bnf_v, dg_wh, dg_ww, dg_g, dg_b, dg_m, dg_v, act_a, ca_w1, ca_g, ca_b, ca_m, ca_v, ca_a, ca_wh, ca_ww):
            m = _axial_dw(x, wh_m, ww_m, r_m)
            l = _axial_dw(x, wh_l, ww_l, r_l)
            fused = _bn(_pw(w_fuse, m + l), bnf_g, bnf_b, bnf_m, bnf_v)
            edges = _dwconv3(x, dg_wh, 2) + _dwconv3(x, dg_ww, 3)
            anchor = _bn(x + edges, dg_g, dg_b, dg_m, dg_v)
            out = _prelu(fused + anchor, act_a)
            return _coord_att(out, ca_w1, (ca_g, ca_b, ca_m, ca_v), ca_a, ca_wh, ca_ww)
        key = jax.random.key(seed)
        ks = jax.random.split(key, 16)
        B, C, H, W = (8, 48, 64, 64)
        K = 5
        MIP = 8

        def rn(k, shape, scale=1.0):
            return jax.random.normal(k, shape, dtype=jnp.float32) * scale
        f32 = jnp.float32
        return {'x': rn(ks[0], (B, C, H, W)), 'r_m': jnp.array(4.0, f32), 'wh_m': rn(ks[1], (C, K), 0.2), 'ww_m': rn(ks[2], (C, K), 0.2), 'r_l': jnp.array(8.0, f32), 'wh_l': rn(ks[3], (C, K), 0.2), 'ww_l': rn(ks[4], (C, K), 0.2), 'w_fuse': rn(ks[5], (C, C), 0.1), 'bnf_g': jnp.ones((C,), f32), 'bnf_b': jnp.zeros((C,), f32), 'bnf_m': jnp.zeros((C,), f32), 'bnf_v': jnp.ones((C,), f32), 'dg_wh': rn(ks[6], (C, 3), 0.3), 'dg_ww': rn(ks[7], (C, 3), 0.3), 'dg_g': jnp.ones((C,), f32), 'dg_b': jnp.zeros((C,), f32), 'dg_m': jnp.zeros((C,), f32), 'dg_v': jnp.ones((C,), f32), 'act_a': jnp.full((C,), 0.25, f32), 'ca_w1': rn(ks[8], (MIP, C), 0.1), 'ca_g': jnp.ones((MIP,), f32), 'ca_b': jnp.zeros((MIP,), f32), 'ca_m': jnp.zeros((MIP,), f32), 'ca_v': jnp.ones((MIP,), f32), 'ca_a': jnp.full((MIP,), 0.25, f32), 'ca_wh': rn(ks[9], (C, MIP), 0.3), 'ca_ww': rn(ks[10], (C, MIP), 0.3)}
    _L0_conv_all = _L0_conv_setup()
    _L0_conv_in = {k: v for k, v in _L0_conv_all.items() if k in ('r_m', 'wh_m', 'ww_m', 'r_l', 'wh_l', 'ww_l', 'w_fuse', 'bnf_g', 'bnf_b', 'bnf_m', 'bnf_v', 'dg_wh', 'dg_ww', 'dg_g', 'dg_b', 'dg_m', 'dg_v', 'act_a', 'ca_w1', 'ca_g', 'ca_b', 'ca_m', 'ca_v', 'ca_a', 'ca_wh', 'ca_ww')}
    del _L0_conv_all

    def _L1_conv_setup():
        import jax, jax.numpy as jnp
        import numpy as np
        from jax import lax
        B, C, H, W = (8, 48, 96, 96)
        HC = 48
        EPS = 1e-05

        def _convlstm_scan(x_rows, w_mid, b, reverse):
            hc = w_mid.shape[0] // 4
            dn = ('NCH', 'OIH', 'NCH')

            def step(carry, xr):
                h, c = carry
                inp = jnp.concatenate([xr, h], axis=1)
                gates = lax.conv_general_dilated(inp, w_mid, (1,), 'SAME', dimension_numbers=dn) + b[None, :, None]
                i, f, g, o = jnp.split(gates, 4, axis=1)
                c2 = jax.nn.sigmoid(f) * c + jax.nn.sigmoid(i) * jnp.tanh(g)
                h2 = jax.nn.sigmoid(o) * jnp.tanh(c2)
                return ((h2, c2), h2)
            z = jnp.zeros((x_rows.shape[1], hc, x_rows.shape[3]), x_rows.dtype)
            _, hs = lax.scan(step, (z, z), x_rows, reverse=reverse)
            return hs
        key = jax.random.key(seed)
        ks = jax.random.split(key, 6)
        s = 0.05
        x = jax.random.normal(ks[0], (B, C, H, W), jnp.float32)
        w_f = jax.random.normal(ks[1], (4 * HC, C + HC, 3, 3), jnp.float32) * s
        b_f = jnp.zeros((4 * HC,), jnp.float32)
        w_b = jax.random.normal(ks[2], (4 * HC, C + HC, 3, 3), jnp.float32) * s
        b_b = jnp.zeros((4 * HC,), jnp.float32)
        w_proj = jax.random.normal(ks[3], (C, 2 * HC), jnp.float32) * s
        gamma = jnp.ones((C,), jnp.float32)
        beta = jnp.zeros((C,), jnp.float32)
        return {'x': x, 'w_f': w_f, 'b_f': b_f, 'w_b': w_b, 'b_b': b_b, 'w_proj': w_proj, 'gamma': gamma, 'beta': beta}
    _L1_conv_all = _L1_conv_setup()
    _L1_conv_in = {k: v for k, v in _L1_conv_all.items() if k in ('w_f', 'b_f', 'w_b', 'b_b', 'w_proj', 'gamma', 'beta')}
    del _L1_conv_all

    def _L2_conv_setup():
        import jax, jax.numpy as jnp
        import numpy as np
        from jax import lax
        B, C, H, W = (8, 48, 96, 96)
        HC = 48
        EPS = 1e-05

        def _convlstm_scan(x_rows, w_mid, b, reverse):
            hc = w_mid.shape[0] // 4
            dn = ('NCH', 'OIH', 'NCH')

            def step(carry, xr):
                h, c = carry
                inp = jnp.concatenate([xr, h], axis=1)
                gates = lax.conv_general_dilated(inp, w_mid, (1,), 'SAME', dimension_numbers=dn) + b[None, :, None]
                i, f, g, o = jnp.split(gates, 4, axis=1)
                c2 = jax.nn.sigmoid(f) * c + jax.nn.sigmoid(i) * jnp.tanh(g)
                h2 = jax.nn.sigmoid(o) * jnp.tanh(c2)
                return ((h2, c2), h2)
            z = jnp.zeros((x_rows.shape[1], hc, x_rows.shape[3]), x_rows.dtype)
            _, hs = lax.scan(step, (z, z), x_rows, reverse=reverse)
            return hs
        key = jax.random.key(seed)
        ks = jax.random.split(key, 6)
        s = 0.05
        x = jax.random.normal(ks[0], (B, C, H, W), jnp.float32)
        w_f = jax.random.normal(ks[1], (4 * HC, C + HC, 3, 3), jnp.float32) * s
        b_f = jnp.zeros((4 * HC,), jnp.float32)
        w_b = jax.random.normal(ks[2], (4 * HC, C + HC, 3, 3), jnp.float32) * s
        b_b = jnp.zeros((4 * HC,), jnp.float32)
        w_proj = jax.random.normal(ks[3], (C, 2 * HC), jnp.float32) * s
        gamma = jnp.ones((C,), jnp.float32)
        beta = jnp.zeros((C,), jnp.float32)
        return {'x': x, 'w_f': w_f, 'b_f': b_f, 'w_b': w_b, 'b_b': b_b, 'w_proj': w_proj, 'gamma': gamma, 'beta': beta}
    _L2_conv_all = _L2_conv_setup()
    _L2_conv_in = {k: v for k, v in _L2_conv_all.items() if k in ('w_f', 'b_f', 'w_b', 'b_b', 'w_proj', 'gamma', 'beta')}
    del _L2_conv_all

    def _L3_conv_setup():
        import jax, jax.numpy as jnp
        import numpy as np
        B, C, H, W = (32, 48, 56, 56)
        HID, OUP = (288, 48)
        EPS = 1e-05

        def _bn(x, g, b, m, v):
            scale = (g * jax.lax.rsqrt(v + EPS)).reshape(1, -1, 1, 1)
            shift = (b - m * g * jax.lax.rsqrt(v + EPS)).reshape(1, -1, 1, 1)
            return x * scale + shift
        key = jax.random.key(seed)
        ks = jax.random.split(key, 16)
        n = lambda k, s, sc=1.0: jax.random.normal(k, s, dtype=jnp.float32) * sc
        u = lambda k, s: jax.random.uniform(k, s, dtype=jnp.float32, minval=0.5, maxval=1.5)
        return {'x': n(ks[0], (B, C, H, W)), 'w1': n(ks[1], (HID, C), 0.05), 'g1': u(ks[2], (HID,)), 'b1': n(ks[3], (HID,), 0.1), 'm1': n(ks[4], (HID,), 0.1), 'v1': u(ks[5], (HID,)), 'wd': n(ks[6], (HID, 1, 3, 3), 0.05), 'gd': u(ks[7], (HID,)), 'bd': n(ks[8], (HID,), 0.1), 'md': n(ks[9], (HID,), 0.1), 'vd': u(ks[10], (HID,)), 'w2': n(ks[11], (OUP, HID), 0.05), 'g2': u(ks[12], (OUP,)), 'b2': n(ks[13], (OUP,), 0.1), 'm2': n(ks[14], (OUP,), 0.1), 'v2': u(ks[15], (OUP,))}
    _L3_conv_all = _L3_conv_setup()
    _L3_conv_in = {k: v for k, v in _L3_conv_all.items() if k in ('w1', 'g1', 'b1', 'm1', 'v1', 'wd', 'gd', 'bd', 'md', 'vd', 'w2', 'g2', 'b2', 'm2', 'v2')}
    del _L3_conv_all
    return {'x': x, 'L0_conv_r_m': _L0_conv_in['r_m'], 'L0_conv_wh_m': _L0_conv_in['wh_m'], 'L0_conv_ww_m': _L0_conv_in['ww_m'], 'L0_conv_r_l': _L0_conv_in['r_l'], 'L0_conv_wh_l': _L0_conv_in['wh_l'], 'L0_conv_ww_l': _L0_conv_in['ww_l'], 'L0_conv_w_fuse': _L0_conv_in['w_fuse'], 'L0_conv_bnf_g': _L0_conv_in['bnf_g'], 'L0_conv_bnf_b': _L0_conv_in['bnf_b'], 'L0_conv_bnf_m': _L0_conv_in['bnf_m'], 'L0_conv_bnf_v': _L0_conv_in['bnf_v'], 'L0_conv_dg_wh': _L0_conv_in['dg_wh'], 'L0_conv_dg_ww': _L0_conv_in['dg_ww'], 'L0_conv_dg_g': _L0_conv_in['dg_g'], 'L0_conv_dg_b': _L0_conv_in['dg_b'], 'L0_conv_dg_m': _L0_conv_in['dg_m'], 'L0_conv_dg_v': _L0_conv_in['dg_v'], 'L0_conv_act_a': _L0_conv_in['act_a'], 'L0_conv_ca_w1': _L0_conv_in['ca_w1'], 'L0_conv_ca_g': _L0_conv_in['ca_g'], 'L0_conv_ca_b': _L0_conv_in['ca_b'], 'L0_conv_ca_m': _L0_conv_in['ca_m'], 'L0_conv_ca_v': _L0_conv_in['ca_v'], 'L0_conv_ca_a': _L0_conv_in['ca_a'], 'L0_conv_ca_wh': _L0_conv_in['ca_wh'], 'L0_conv_ca_ww': _L0_conv_in['ca_ww'], 'L1_conv_w_f': _L1_conv_in['w_f'], 'L1_conv_b_f': _L1_conv_in['b_f'], 'L1_conv_w_b': _L1_conv_in['w_b'], 'L1_conv_b_b': _L1_conv_in['b_b'], 'L1_conv_w_proj': _L1_conv_in['w_proj'], 'L1_conv_gamma': _L1_conv_in['gamma'], 'L1_conv_beta': _L1_conv_in['beta'], 'L2_conv_w_f': _L2_conv_in['w_f'], 'L2_conv_b_f': _L2_conv_in['b_f'], 'L2_conv_w_b': _L2_conv_in['w_b'], 'L2_conv_b_b': _L2_conv_in['b_b'], 'L2_conv_w_proj': _L2_conv_in['w_proj'], 'L2_conv_gamma': _L2_conv_in['gamma'], 'L2_conv_beta': _L2_conv_in['beta'], 'L3_conv_w1': _L3_conv_in['w1'], 'L3_conv_g1': _L3_conv_in['g1'], 'L3_conv_b1': _L3_conv_in['b1'], 'L3_conv_m1': _L3_conv_in['m1'], 'L3_conv_v1': _L3_conv_in['v1'], 'L3_conv_wd': _L3_conv_in['wd'], 'L3_conv_gd': _L3_conv_in['gd'], 'L3_conv_bd': _L3_conv_in['bd'], 'L3_conv_md': _L3_conv_in['md'], 'L3_conv_vd': _L3_conv_in['vd'], 'L3_conv_w2': _L3_conv_in['w2'], 'L3_conv_g2': _L3_conv_in['g2'], 'L3_conv_b2': _L3_conv_in['b2'], 'L3_conv_m2': _L3_conv_in['m2'], 'L3_conv_v2': _L3_conv_in['v2']}

def reference(x, L0_conv_r_m, L0_conv_wh_m, L0_conv_ww_m, L0_conv_r_l, L0_conv_wh_l, L0_conv_ww_l, L0_conv_w_fuse, L0_conv_bnf_g, L0_conv_bnf_b, L0_conv_bnf_m, L0_conv_bnf_v, L0_conv_dg_wh, L0_conv_dg_ww, L0_conv_dg_g, L0_conv_dg_b, L0_conv_dg_m, L0_conv_dg_v, L0_conv_act_a, L0_conv_ca_w1, L0_conv_ca_g, L0_conv_ca_b, L0_conv_ca_m, L0_conv_ca_v, L0_conv_ca_a, L0_conv_ca_wh, L0_conv_ca_ww, L1_conv_w_f, L1_conv_b_f, L1_conv_w_b, L1_conv_b_b, L1_conv_w_proj, L1_conv_gamma, L1_conv_beta, L2_conv_w_f, L2_conv_b_f, L2_conv_w_b, L2_conv_b_b, L2_conv_w_proj, L2_conv_gamma, L2_conv_beta, L3_conv_w1, L3_conv_g1, L3_conv_b1, L3_conv_m1, L3_conv_v1, L3_conv_wd, L3_conv_gd, L3_conv_bd, L3_conv_md, L3_conv_vd, L3_conv_w2, L3_conv_g2, L3_conv_b2, L3_conv_m2, L3_conv_v2):
    import jax
    import jax.numpy as jnp

    def _L0_conv_ref(x, r_m, wh_m, ww_m, r_l, wh_l, ww_l, w_fuse, bnf_g, bnf_b, bnf_m, bnf_v, dg_wh, dg_ww, dg_g, dg_b, dg_m, dg_v, act_a, ca_w1, ca_g, ca_b, ca_m, ca_v, ca_a, ca_wh, ca_ww):
        import jax, jax.numpy as jnp
        import numpy as np
        EPS = 1e-05

        def _shift1d(x, s, axis):
            n = x.shape[axis]
            f = jnp.floor(s)
            frac = (s - f).astype(x.dtype)
            fi = f.astype(jnp.int32)

            def gather(off):
                idx = jnp.arange(n) + fi + off
                mask = (idx >= 0) & (idx < n)
                v = jnp.take(x, jnp.clip(idx, 0, n - 1), axis=axis)
                mshape = [1] * x.ndim
                mshape[axis] = n
                return v * mask.reshape(mshape).astype(x.dtype)
            return (1 - frac) * gather(0) + frac * gather(1)

        def _axial_dw(x, w_h, w_w, r):
            r = jnp.maximum(r, 1.0)
            c = x.shape[1]
            kh = w_h.shape[1]
            kw = w_w.shape[1]
            acc_h = jnp.zeros_like(x)
            for i, off in enumerate(range(-(kh // 2), kh // 2 + 1)):
                acc_h = acc_h + _shift1d(x, off * r, 2) * w_h[:, i].reshape(1, c, 1, 1)
            acc_w = jnp.zeros_like(x)
            for i, off in enumerate(range(-(kw // 2), kw // 2 + 1)):
                acc_w = acc_w + _shift1d(x, off * r, 3) * w_w[:, i].reshape(1, c, 1, 1)
            return x + acc_h + acc_w

        def _bn(x, g, b, m, v):
            sh = (1, -1, 1, 1)
            scale = g.reshape(sh) * jax.lax.rsqrt(v.reshape(sh) + EPS)
            return (x - m.reshape(sh)) * scale + b.reshape(sh)

        def _prelu(x, a):
            return jnp.where(x >= 0, x, a.reshape(1, -1, 1, 1) * x)

        def _pw(w, x):
            return jnp.einsum('oc,bchw->bohw', w, x)

        def _dwconv3(x, w, axis):
            c = x.shape[1]
            n = x.shape[axis]
            pad = [(0, 0)] * 4
            pad[axis] = (1, 1)
            xp = jnp.pad(x, pad)
            out = jnp.zeros_like(x)
            for i in range(3):
                out = out + jax.lax.slice_in_dim(xp, i, i + n, axis=axis) * w[:, i].reshape(1, c, 1, 1)
            return out

        def _coord_att(x, w1, bn1, a1, wh, ww):
            n, c, h, w = x.shape
            xh = x.mean(axis=3, keepdims=True)
            xw = jnp.transpose(x.mean(axis=2, keepdims=True), (0, 1, 3, 2))
            y = jnp.concatenate([xh, xw], axis=2)
            y = _prelu(_bn(_pw(w1, y), *bn1), a1)
            yh, yw = (y[:, :, :h], jnp.transpose(y[:, :, h:], (0, 1, 3, 2)))
            a_h = jax.nn.sigmoid(_pw(wh, yh))
            a_w = jax.nn.sigmoid(_pw(ww, yw))
            return x * a_w * a_h

        def _forward(x, r_m, wh_m, ww_m, r_l, wh_l, ww_l, w_fuse, bnf_g, bnf_b, bnf_m, bnf_v, dg_wh, dg_ww, dg_g, dg_b, dg_m, dg_v, act_a, ca_w1, ca_g, ca_b, ca_m, ca_v, ca_a, ca_wh, ca_ww):
            m = _axial_dw(x, wh_m, ww_m, r_m)
            l = _axial_dw(x, wh_l, ww_l, r_l)
            fused = _bn(_pw(w_fuse, m + l), bnf_g, bnf_b, bnf_m, bnf_v)
            edges = _dwconv3(x, dg_wh, 2) + _dwconv3(x, dg_ww, 3)
            anchor = _bn(x + edges, dg_g, dg_b, dg_m, dg_v)
            out = _prelu(fused + anchor, act_a)
            return _coord_att(out, ca_w1, (ca_g, ca_b, ca_m, ca_v), ca_a, ca_wh, ca_ww)
        return _forward(x, r_m, wh_m, ww_m, r_l, wh_l, ww_l, w_fuse, bnf_g, bnf_b, bnf_m, bnf_v, dg_wh, dg_ww, dg_g, dg_b, dg_m, dg_v, act_a, ca_w1, ca_g, ca_b, ca_m, ca_v, ca_a, ca_wh, ca_ww)

    def _L1_conv_ref(x, w_f, b_f, w_b, b_b, w_proj, gamma, beta):
        import jax, jax.numpy as jnp
        import numpy as np
        from jax import lax
        B, C, H, W = (8, 48, 96, 96)
        HC = 48
        EPS = 1e-05

        def _convlstm_scan(x_rows, w_mid, b, reverse):
            hc = w_mid.shape[0] // 4
            dn = ('NCH', 'OIH', 'NCH')

            def step(carry, xr):
                h, c = carry
                inp = jnp.concatenate([xr, h], axis=1)
                gates = lax.conv_general_dilated(inp, w_mid, (1,), 'SAME', dimension_numbers=dn) + b[None, :, None]
                i, f, g, o = jnp.split(gates, 4, axis=1)
                c2 = jax.nn.sigmoid(f) * c + jax.nn.sigmoid(i) * jnp.tanh(g)
                h2 = jax.nn.sigmoid(o) * jnp.tanh(c2)
                return ((h2, c2), h2)
            z = jnp.zeros((x_rows.shape[1], hc, x_rows.shape[3]), x_rows.dtype)
            _, hs = lax.scan(step, (z, z), x_rows, reverse=reverse)
            return hs
        xr = jnp.transpose(x, (2, 0, 1, 3))
        hs_f = _convlstm_scan(xr, w_f[:, :, 1, :], b_f, reverse=False)
        hs_b = _convlstm_scan(xr, w_b[:, :, 1, :], b_b, reverse=True)
        feats = jnp.concatenate([hs_f, hs_b], axis=2)
        feats = jnp.transpose(feats, (1, 2, 0, 3))
        y = jnp.einsum('oc,bchw->bohw', w_proj, feats)
        mu = jnp.mean(y, axis=(0, 2, 3))
        var = jnp.var(y, axis=(0, 2, 3))
        yn = (y - mu[None, :, None, None]) * lax.rsqrt(var + EPS)[None, :, None, None]
        y = gamma[None, :, None, None] * yn + beta[None, :, None, None]
        return jax.nn.relu(y) + x

    def _L2_conv_ref(x, w_f, b_f, w_b, b_b, w_proj, gamma, beta):
        import jax, jax.numpy as jnp
        import numpy as np
        from jax import lax
        B, C, H, W = (8, 48, 96, 96)
        HC = 48
        EPS = 1e-05

        def _convlstm_scan(x_rows, w_mid, b, reverse):
            hc = w_mid.shape[0] // 4
            dn = ('NCH', 'OIH', 'NCH')

            def step(carry, xr):
                h, c = carry
                inp = jnp.concatenate([xr, h], axis=1)
                gates = lax.conv_general_dilated(inp, w_mid, (1,), 'SAME', dimension_numbers=dn) + b[None, :, None]
                i, f, g, o = jnp.split(gates, 4, axis=1)
                c2 = jax.nn.sigmoid(f) * c + jax.nn.sigmoid(i) * jnp.tanh(g)
                h2 = jax.nn.sigmoid(o) * jnp.tanh(c2)
                return ((h2, c2), h2)
            z = jnp.zeros((x_rows.shape[1], hc, x_rows.shape[3]), x_rows.dtype)
            _, hs = lax.scan(step, (z, z), x_rows, reverse=reverse)
            return hs
        xr = jnp.transpose(x, (2, 0, 1, 3))
        hs_f = _convlstm_scan(xr, w_f[:, :, 1, :], b_f, reverse=False)
        hs_b = _convlstm_scan(xr, w_b[:, :, 1, :], b_b, reverse=True)
        feats = jnp.concatenate([hs_f, hs_b], axis=2)
        feats = jnp.transpose(feats, (1, 2, 0, 3))
        y = jnp.einsum('oc,bchw->bohw', w_proj, feats)
        mu = jnp.mean(y, axis=(0, 2, 3))
        var = jnp.var(y, axis=(0, 2, 3))
        yn = (y - mu[None, :, None, None]) * lax.rsqrt(var + EPS)[None, :, None, None]
        y = gamma[None, :, None, None] * yn + beta[None, :, None, None]
        return jax.nn.relu(y) + x

    def _L3_conv_ref(x, w1, g1, b1, m1, v1, wd, gd, bd, md, vd, w2, g2, b2, m2, v2):
        import jax, jax.numpy as jnp
        import numpy as np
        B, C, H, W = (32, 48, 56, 56)
        HID, OUP = (288, 48)
        EPS = 1e-05

        def _bn(x, g, b, m, v):
            scale = (g * jax.lax.rsqrt(v + EPS)).reshape(1, -1, 1, 1)
            shift = (b - m * g * jax.lax.rsqrt(v + EPS)).reshape(1, -1, 1, 1)
            return x * scale + shift
        h = jnp.einsum('oc,bchw->bohw', w1, x)
        h = jax.nn.relu(_bn(h, g1, b1, m1, v1))
        h = jax.lax.conv_general_dilated(h, wd, window_strides=(1, 1), padding=((1, 1), (1, 1)), feature_group_count=HID, dimension_numbers=('NCHW', 'OIHW', 'NCHW'))
        h = jax.nn.relu(_bn(h, gd, bd, md, vd))
        h = jnp.einsum('oc,bchw->bohw', w2, h)
        h = _bn(h, g2, b2, m2, v2)
        return x + h

    def _gn(v, G=32, eps=1e-05):
        B_, C_, H_, W_ = v.shape
        g = v.reshape(B_, G, C_ // G, H_, W_)
        m = jnp.mean(g, axis=(2, 3, 4), keepdims=True)
        s = jnp.var(g, axis=(2, 3, 4), keepdims=True)
        return ((g - m) / jnp.sqrt(s + eps)).reshape(v.shape)

    def _ln_c(v, eps=1e-06):
        m = jnp.mean(v, axis=1, keepdims=True)
        s = jnp.var(v, axis=1, keepdims=True)
        return (v - m) / jnp.sqrt(s + eps)

    def _ln_t(v, eps=1e-05):
        m = jnp.mean(v, axis=-1, keepdims=True)
        s = jnp.var(v, axis=-1, keepdims=True)
        return (v - m) / jnp.sqrt(s + eps)

    def _to_tokens(v):
        B_, C_, H_, W_ = v.shape
        return v.reshape(B_, C_, H_ * W_).transpose(0, 2, 1)

    def _from_tokens(t, like):
        B_, C_, H_, W_ = like.shape
        return t.transpose(0, 2, 1).reshape(B_, C_, H_, W_)
    x = _L0_conv_ref(x, L0_conv_r_m, L0_conv_wh_m, L0_conv_ww_m, L0_conv_r_l, L0_conv_wh_l, L0_conv_ww_l, L0_conv_w_fuse, L0_conv_bnf_g, L0_conv_bnf_b, L0_conv_bnf_m, L0_conv_bnf_v, L0_conv_dg_wh, L0_conv_dg_ww, L0_conv_dg_g, L0_conv_dg_b, L0_conv_dg_m, L0_conv_dg_v, L0_conv_act_a, L0_conv_ca_w1, L0_conv_ca_g, L0_conv_ca_b, L0_conv_ca_m, L0_conv_ca_v, L0_conv_ca_a, L0_conv_ca_wh, L0_conv_ca_ww)
    x = _L1_conv_ref(x, L1_conv_w_f, L1_conv_b_f, L1_conv_w_b, L1_conv_b_b, L1_conv_w_proj, L1_conv_gamma, L1_conv_beta)
    x = _L2_conv_ref(x, L2_conv_w_f, L2_conv_b_f, L2_conv_w_b, L2_conv_b_b, L2_conv_w_proj, L2_conv_gamma, L2_conv_beta)
    x = _L3_conv_ref(x, L3_conv_w1, L3_conv_g1, L3_conv_b1, L3_conv_m1, L3_conv_v1, L3_conv_wd, L3_conv_gd, L3_conv_bd, L3_conv_md, L3_conv_vd, L3_conv_w2, L3_conv_g2, L3_conv_b2, L3_conv_m2, L3_conv_v2)
    return x

_drawn_inputs = setup_inputs


def setup_inputs(seed=0):
    import zlib

    import numpy as np

    out = dict(_drawn_inputs(seed))
    spreads = {'L0_conv_bnf_g': (1.0, 0.2),
     'L0_conv_bnf_b': (0.0, 0.1),
     'L0_conv_bnf_m': (0.0, 0.1),
     'L0_conv_bnf_v': (1.0, 0.2),
     'L0_conv_dg_g': (1.0, 0.2),
     'L0_conv_dg_b': (0.0, 0.1),
     'L0_conv_dg_m': (0.0, 0.1),
     'L0_conv_dg_v': (1.0, 0.2),
     'L0_conv_act_a': (0.25, 0.2),
     'L0_conv_ca_g': (1.0, 0.2),
     'L0_conv_ca_b': (0.0, 0.1),
     'L0_conv_ca_m': (0.0, 0.1),
     'L0_conv_ca_v': (1.0, 0.6),
     'L0_conv_ca_a': (0.25, 0.6),
     'L1_conv_b_f': (0.0, 0.1),
     'L1_conv_b_b': (0.0, 0.1),
     'L1_conv_gamma': (1.0, 0.2),
     'L1_conv_beta': (0.0, 0.1),
     'L2_conv_b_f': (0.0, 0.1),
     'L2_conv_b_b': (0.0, 0.1),
     'L2_conv_gamma': (1.0, 0.2),
     'L2_conv_beta': (0.0, 0.1)}
    factors = {'L3_conv_g1': 41.536,
     'L3_conv_b1': 8.0,
     'L3_conv_m1': 24.349,
     'L3_conv_v1': 200.0,
     'L3_conv_gd': 82.217,
     'L3_conv_vd': 200.0,
     'L3_conv_v2': 128.352,
     'L3_conv_w1': 4.512,
     'L3_conv_bd': 5.624,
     'L3_conv_g2': 6.186,
     'L3_conv_m2': 3.043}
    for name, (base, spread) in spreads.items():
        noise = np.random.default_rng([zlib.crc32(name.encode()), seed]).standard_normal(out[name].shape)
        drawn = base * np.exp(spread * noise) if base else spread * noise
        out[name] = jnp.asarray(drawn.astype(out[name].dtype))
    for name, factor in factors.items():
        out[name] = (out[name] * factor).astype(out[name].dtype)
    return out
```

```python
import concourse.bass as bass
from concourse import mybir
from contextlib import ExitStack
import numpy as np

F32 = mybir.dt.float32
F32R = mybir.dt.float32r
I32 = mybir.dt.int32
ALU = mybir.AluOpType
ACT = mybir.ActivationFunctionType
AX = mybir.AxisListType

B, C, H, W = 8, 48, 64, 64
P = 128
HALF = 64
HB = B // 2
PAIRS = C // 2
BW = B * W
WP = W + 2
ROW = B * WP
HID = 6 * C
GROUPS, GC = 3, HID // 3
EPS = 1e-5
BANKS = 8

K_AX, K_DG = 5, 3
TAPS = 2 * K_AX + 1 + K_DG
OFFSETS = [*range(-2, 3), *range(-2, 3), 0, -1, 0, 1]
SPAN = 2 * H - 1
SETS = PAIRS + C
COLS = 2 * SETS
PER_BANK = 3


def wait(eng, sem, value):
    if isinstance(value, int) and value <= 0:
        return
    eng.wait_ge(sem, value)


def release(nc, sems):
    nc.clear_and_free_semaphores(sems)
    nc.all_engine_barrier()


def held(eng, value):
    return value if isinstance(value, int) else eng.snap(value)


def peeled(eng, count, body):
    body(0)
    with eng.Fori(1, count) as k:
        body(k)


def axial_filters(nc, D, ctx_hs):
    ctx = ExitStack()
    with ctx:
        sems = []
        ctx.callback(release, nc, sems)

        def sb(name, shape, dt=F32):
            return ctx.enter_context(nc.sbuf_tensor(name, shape, dt))

        def sem(name):
            sems.append(nc.alloc_semaphore(name))
            return sems[-1]

        hs = ctx_hs
        taps = sb("taps", [TAPS, 2, COLS])
        tapc = sb("tapc", [TAPS, 2])
        shift = sb("shift", [TAPS, 1])
        radius = sb("radius", [TAPS, 1])
        disti = sb("disti", [TAPS, SPAN], I32)
        dist = sb("dist", [TAPS, 3, SPAN])
        hat = sb("hat", [TAPS, SPAN])
        filt = sb("filt", [P, COLS, H])
        fy = sb("fy", [P, 2, 2, P])
        fx = sb("fx", [P, 2, 2, 2, P])
        xr = sb("xr", [P, 2, BW])
        xc = sb("xc", [P, 2, 2, HB, H])
        stage = sb("stage", [P, 4, BW])
        ps = [ctx.enter_context(nc.psum_tensor(f"axps{i}", [P, BW], F32)) for i in range(BANKS)]

        loaded = sem("a_loaded")
        iota_done = sem("a_iota")
        hat_steps = sem("a_hat_steps")
        hat_ready = sem("a_hat_ready")
        built = sem("a_built")
        kept_a = sem("a_kept_act")
        kept_d = sem("a_kept_dve")
        x_in = [sem(f"a_x_in{s}") for s in range(2)]
        pair_copied = sem("a_pair_copied")
        filtered = sem("a_filtered")
        staged_a = sem("a_staged_act")
        staged_d = sem("a_staged_dve")
        stored = [sem(f"a_stored{s}") for s in range(4)]
        zeroed = sem("a_zeroed")

        groups = [list(range(i, min(i + PER_BANK, H))) for i in range(0, H, PER_BANK)]
        NG = len(groups)
        n_act, n_dve = (NG + 1) // 2, NG // 2

        with nc.Block() as block:
            @block.sync
            def _(sp):
                sp.dma_start(taps[:, :, :], D["tap_table"]).then_inc(loaded, 16)
                sp.dma_start(tapc[:, :], D["tap_consts"]).then_inc(loaded, 16)

                def load(pair, s):
                    sp.dma_start(xr[:, s, :], D["x_rows"][pair]).then_inc(x_in[s], 16)
                    sp.dma_start(xc[:, s], D["x_cols"][pair].rearrange("p (a b y) -> p a b y", a=2, b=HB)
                                 ).then_inc(x_in[s], 16)

                def step(k, last=False):
                    for s in range(2):
                        pair = held(sp, 2 * k + s)
                        ahead = held(sp, 2 * k + s + 2)
                        done = held(sp, 2 * k + s + 1)
                        sp.wait_ge(staged_a, done)
                        sp.wait_ge(staged_d, done)
                        sp.dma_start(D["mixed"][pair], stage[:, 2 * s, :]).then_inc(stored[2 * s], 16)
                        sp.dma_start(D["edged"][pair], stage[:, 2 * s + 1, :]).then_inc(stored[2 * s + 1], 16)
                        if not last:
                            load(ahead, s)
                for s in range(2):
                    load(s, s)
                with sp.Fori(0, PAIRS // 2 - 1) as k:
                    step(k)
                step(PAIRS // 2 - 1, last=True)
                for s in range(4):
                    sp.wait_ge(stored[s], 16 * (PAIRS // 2))

            @block.gpsimd
            def _(pool):
                pool.iota(disti[:, :], [[1, SPAN]], base=-(H - 1), channel_multiplier=0).then_inc(iota_done, 1)
                pool.memset(hs[32:64, :, :], 0.0).then_inc(zeroed, 1)

            @block.scalar
            def _(act):
                for n in range(0, NG, 2):
                    act.wait_ge(built, n + 1)
                    g = groups[n]
                    nc.scalar.activation(filt[:, :, g[0]:g[0] + len(g)],
                                         ps[n % BANKS][:, 0:COLS * len(g)].rearrange("p (i c) -> p c i", c=COLS),
                                         ACT.Copy).then_inc(kept_a, 1)

                def step(k):
                    for s in range(2):
                        act.wait_ge(filtered, 4 * k + 2 * s + 1)
                        wait(act, stored[2 * s], 16 * k)
                        nc.scalar.activation(stage[:, 2 * s, :], ps[2 * s][:, :], ACT.Copy).then_inc(staged_a, 1)
                peeled(act, PAIRS // 2, step)

            @block.vector
            def _(dve):
                nc.vector.memset(fy[:, :, :, :], 0.0).then_inc(hat_steps, 1)
                nc.vector.memset(fx[:, :, :, :, :], 0.0).then_inc(hat_steps, 1)
                dve.wait_ge(loaded, 32)
                dve.wait_ge(iota_done, 1)
                nc.vector.tensor_copy(dist[:, 0, :], disti[:, :]).then_inc(hat_steps, 1)
                nc.vector.tensor_scalar(radius[:, :], tapc[:, 1:2], 1.0, None, ALU.max).then_inc(hat_steps, 1)
                dve.wait_ge(hat_steps, 4)
                nc.vector.tensor_tensor(shift[:, :], radius[:, :], tapc[:, 0:1], ALU.mult).then_inc(hat_steps, 1)
                dve.wait_ge(hat_steps, 5)
                nc.vector.tensor_scalar(dist[:, 1, :], dist[:, 0, :], shift[:, 0:1], None, ALU.subtract).then_inc(hat_steps, 1)
                dve.wait_ge(hat_steps, 6)
                nc.vector.tensor_scalar(dist[:, 0, :], dist[:, 1, :], -1.0, 1.0, ALU.mult, ALU.add).then_inc(hat_steps, 1)
                nc.vector.tensor_scalar(dist[:, 2, :], dist[:, 1, :], 1.0, None, ALU.add).then_inc(hat_steps, 1)
                dve.wait_ge(hat_steps, 8)
                nc.vector.tensor_tensor(dist[:, 1, :], dist[:, 0, :], dist[:, 2, :], ALU.min).then_inc(hat_steps, 1)
                dve.wait_ge(hat_steps, 9)
                nc.vector.tensor_scalar(hat[:, :], dist[:, 1, :], 0.0, None, ALU.max).then_inc(hat_ready, 1)
                for n in range(1, NG, 2):
                    dve.wait_ge(built, n + 1)
                    g = groups[n]
                    nc.vector.tensor_copy(filt[:, :, g[0]:g[0] + len(g)],
                                          ps[n % BANKS][:, 0:COLS * len(g)].rearrange("p (i c) -> p c i", c=COLS)
                                          ).then_inc(kept_d, 1)
                dve.wait_ge(kept_a, n_act)
                dve.wait_ge(kept_d, n_dve)

                def copy_pair(pair, s):
                    for q in range(2):
                        for h in range(2):
                            lo = h * HALF
                            nc.vector.tensor_copy(fy[lo:lo + HALF, s, q, lo:lo + HALF].unsqueeze(1),
                                                  filt[lo:lo + HALF, bass.ds(pair + q * SETS, 1), :])
                            last = nc.vector.tensor_copy(fx[lo:lo + HALF, s, q, :, lo:lo + HALF],
                                                         filt[lo:lo + HALF, bass.ds(2 * pair + (q * SETS + PAIRS), 2), :])
                    last.then_inc(pair_copied, 1)

                def step(k):
                    for s in range(2):
                        wait(dve, filtered, 4 * k - 4 + 2 * s + 2)
                        copy_pair(2 * k + s, s)
                    for s in range(2):
                        dve.wait_ge(filtered, 4 * k + 2 * s + 2)
                        wait(dve, stored[2 * s + 1], 16 * k)
                        nc.vector.tensor_copy(stage[:, 2 * s + 1, :], ps[2 * s + 1][:, :]).then_inc(staged_d, 1)
                peeled(dve, PAIRS // 2, step)

            @block.tensor
            def _(pe):
                pe.wait_ge(loaded, 32)
                pe.wait_ge(hat_ready, 1)
                for n, g in enumerate(groups):
                    if n >= BANKS:
                        m = n - BANKS
                        pe.wait_ge(kept_d if m % 2 else kept_a, m // 2 + 1)
                    for r, i in enumerate(g):
                        for h in range(2):
                            mm = nc.tensor.matmul(ps[n % BANKS][h * HALF:(h + 1) * HALF, r * COLS:(r + 1) * COLS],
                                                  hat[:, H - 1 - i:2 * H - 1 - i], taps[:, h, :], start=(r == 0), stop=True,
                                                  skip_group_check=True)
                    mm.then_inc(built, 1)
                pe.wait_ge(kept_a, n_act)
                pe.wait_ge(kept_d, n_dve)

                def step(k):
                    for s in range(2):
                        wait(pe, x_in[s], 32 * k + 32)
                        wait(pe, pair_copied, 2 * k + s + 1)
                        for q in range(2):
                            bank = ps[2 * s + q]
                            wait(pe, staged_d if q else staged_a, 2 * k + s - 1)
                            nc.tensor.matmul(bank[:, :], fy[:, s, q, :], xr[:, s, :],
                                             start=True, stop=False, skip_group_check=True)
                            for b in range(HB):
                                for h in range(2):
                                    mm = nc.tensor.matmul(bank[h * HALF:(h + 1) * HALF, b * P:(b + 1) * P],
                                                          xc[:, s, h, b, :], fx[:, s, q, h, :],
                                                          start=False, stop=True, skip_group_check=True)
                            mm.then_inc(filtered, 1)
                peeled(pe, PAIRS // 2, step)



def mix_channels(nc, D, hs):
    ctx = ExitStack()
    UNIT = 4
    UC = UNIT * HB * W
    with ctx:
        sems = []
        ctx.callback(release, nc, sems)

        def sb(name, shape, dt=F32):
            return ctx.enter_context(nc.sbuf_tensor(name, shape, dt))

        def sem(name):
            sems.append(nc.alloc_semaphore(name))
            return sems[-1]

        kept = hs[:, 0:H // 2, :].rearrange("p a n -> p (a n)").rearrange("p (u n) -> p u n", n=UC)
        mixed = sb("mixed_sb", [P, 2, UC])
        edged = sb("edged_sb", [P, 2, UC])
        scaled = sb("scaled", [P, 2, UC])
        total = sb("total", [P, 2, UC])
        minus = sb("minus", [P, 2, UC])
        wf = sb("wf", [P, P])
        par = sb("par", [P, 9])
        half_power = sb("half_power", [P, 2])
        var = sb("var", [P, 2])
        rs = sb("rs", [P, 2])
        scale = sb("scale", [P, 2])
        shift = sb("shift_bn", [P, 4])
        slope = sb("slope", [P, 1])
        ps = [ctx.enter_context(nc.psum_tensor(f"mxps{i}", [P, BW], F32)) for i in range(4)]

        loaded = sem("m_loaded")
        steps = sem("m_steps")
        consts = sem("m_consts")
        x_in = [sem(f"m_x_in{s}") for s in range(2)]
        zeroed = sem("m_zeroed")
        multiplied = sem("m_multiplied")
        affine = sem("m_affine")
        added = sem("m_added")
        negs = sem("m_negs")
        done = sem("m_done")

        with nc.Block() as block:
            @block.sync
            def _(sp):
                sp.dma_start(wf[:, :], D["w_fuse_T"]).then_inc(loaded, 16)
                sp.dma_start(par[:, :], D["mix_params"]).then_inc(loaded, 16)
                sp.wait_ge(zeroed, 2)

                def load(u, s):
                    for q, tile in (("mixed", mixed), ("edged", edged)):
                        src = D[q].rearrange("k (a y) (h n) -> k a y h n", a=2, h=2)
                        src = D[q + "_c"]
                        for h in range(2):
                            sp.dma_start(tile[h * HALF:h * HALF + C, s, :].rearrange("p (y n) -> p y n", y=UNIT),
                                         src[:, u, :, h, :]).then_inc(x_in[s], 16)

                def step(k):
                    for s in range(2):
                        u = held(sp, 2 * k + s)
                        used = held(sp, 2 * k + s - 1)
                        wait(sp, done, used)
                        load(u, s)
                peeled(sp, H // UNIT // 2, step)

            @block.gpsimd
            def _(pool):
                pool.memset(edged[:, :, :], 0.0).then_inc(zeroed, 1)
                pool.memset(mixed[:, :, :], 0.0).then_inc(zeroed, 1)
                pool.memset(half_power[:, :], -0.5).then_inc(steps, 1)
                pool.wait_ge(loaded, 32)
                pool.tensor_scalar(var[:, :], par[:, 3:8:4], EPS, 0.0, ALU.add, ALU.add).then_inc(steps, 1)
                pool.wait_ge(steps, 2)
                pool.tensor_tensor(rs[:, :], var[:, :], half_power[:, :], ALU.pow).then_inc(steps, 1)
                pool.wait_ge(steps, 3)
                pool.tensor_tensor(scale[:, :], rs[:, :], par[:, 0:5:4], ALU.mult).then_inc(steps, 1)
                pool.wait_ge(steps, 4)
                pool.tensor_tensor(shift[:, 0:2], par[:, 2:7:4], scale[:, :], ALU.mult).then_inc(steps, 1)
                pool.wait_ge(steps, 5)
                pool.tensor_tensor(shift[:, 2:4], par[:, 1:6:4], shift[:, 0:2], ALU.subtract).then_inc(steps, 1)
                pool.wait_ge(steps, 6)
                pool.tensor_tensor(shift[:, 0:1], shift[:, 2:3], shift[:, 3:4], ALU.add).then_inc(consts, 1)
                pool.tensor_scalar(slope[:, :], par[:, 8:9], -1.0, 0.0, ALU.add, ALU.add).then_inc(consts, 1)

            @block.tensor
            def _(pe):
                pe.wait_ge(loaded, 32)

                def step(k):
                    for s in range(2):
                        wait(pe, x_in[s], 64 * k + 64)
                        wait(pe, affine, 4 * k + 2 * s - 2)
                        for j in range(2):
                            nc.tensor.matmul(ps[2 * s + j][:, :], wf[0:HALF + C, :],
                                             mixed[0:HALF + C, s, j * BW:(j + 1) * BW],
                                             start=True, stop=True).then_inc(multiplied, 1)
                peeled(pe, H // UNIT // 2, step)

            @block.scalar
            def _(act):
                act.wait_ge(consts, 2)

                def step(k):
                    for s in range(2):
                        wait(act, done, 2 * k + s - 1)
                        for j in range(2):
                            act.wait_ge(multiplied, 4 * k + 2 * s + j + 1)
                            nc.scalar.activation(scaled[:, s, j * BW:(j + 1) * BW], ps[2 * s + j][:, :], ACT.Identity,
                                                 bias=shift[:, 0:1], scale=scale[:, 0:1]).then_inc(affine, 1)
                peeled(act, H // UNIT // 2, step)

            @block.vector
            def _(dve):
                dve.wait_ge(consts, 2)
                dve.wait_ge(zeroed, 2)

                def step(k):
                    for s in range(2):
                        dve.wait_ge(affine, 4 * k + 2 * s + 2)
                        dve.wait_ge(x_in[s], 64 * k + 64)
                        nc.vector.scalar_tensor_tensor(total[:, s, :], edged[:, s, :], scale[:, 1:2], scaled[:, s, :],
                                                       ALU.mult, ALU.add).then_inc(added, 1)
                        dve.wait_ge(added, 2 * k + s + 1)
                        nc.vector.tensor_scalar(minus[:, s, :], total[:, s, :], 0.0, slope[:, 0:1], ALU.min, ALU.mult
                                                ).then_inc(negs, 1)
                        dve.wait_ge(negs, 2 * k + s + 1)
                        nc.vector.tensor_tensor(kept[:, bass.ds(2 * k + s, 1), :].rearrange("p a n -> p (a n)"),
                                                minus[:, s, :], total[:, s, :], ALU.add).then_inc(done, 1)
                peeled(dve, H // UNIT // 2, step)


def coordinate_attention(nc, D, hs, out_rows):
    ctx = ExitStack()
    UNIT = 4
    with ctx:
        sems = []
        ctx.callback(release, nc, sems)

        def sb(name, shape, dt=F32):
            return ctx.enter_context(nc.sbuf_tensor(name, shape, dt))

        def sem(name):
            sems.append(nc.alloc_semaphore(name))
            return sems[-1]

        kept = hs[:, 0:H // 2, :].rearrange("p a n -> p (a n)").rearrange("p (y b w) -> p y b w", b=HB, w=W)
        means = sb("means", [P, 2, H * HB])
        w1 = sb("ca_w1", [P, HALF])
        wg = sb("ca_wg", [P, 2, HALF])
        par = sb("ca_par", [P, 5])
        power = sb("ca_power", [P, 1])
        tmp = sb("ca_tmp", [P, 4])
        cs = sb("ca_cs", [P, 3])
        z = sb("ca_z", [P, 3, BW])
        gate = sb("ca_gate", [P, 2, H * HB])
        xa = sb("ca_xa", [P, 2, UNIT, HB * W])
        xg = sb("ca_xg", [P, 2, UNIT, HB * W])
        parts = sb("ca_parts", [P, 2, 2, UNIT, HB, WP], F32R)
        ps = [ctx.enter_context(nc.psum_tensor(f"caps{i}", [P, BW], F32)) for i in range(2)]

        loaded = sem("c_loaded")
        steps = sem("c_steps")
        consts = sem("c_consts")
        summed = sem("c_summed")
        squeezed = sem("c_squeezed")
        normed = sem("c_normed")
        zneg = sem("c_zneg")
        zdone = sem("c_zdone")
        widened = sem("c_widened")
        gated = sem("c_gated")
        bordered = sem("c_bordered")
        times_w = sem("c_times_w")
        times_h = sem("c_times_h")
        hi_done = sem("c_hi")
        lo_done = sem("c_lo")
        stored = [sem(f"c_stored{s}") for s in range(2)]

        with nc.Block() as block:
            @block.sync
            def _(sp):
                sp.dma_start(w1[:, :], D["ca_w1_T"]).then_inc(loaded, 16)
                sp.dma_start(wg[:, :, :], D["ca_wg_T"]).then_inc(loaded, 16)
                sp.dma_start(par[:, :], D["ca_params"]).then_inc(loaded, 16)

                def step(k):
                    for s in range(2):
                        u = held(sp, 2 * k + s)
                        ready = held(sp, 2 * k + s + 1)
                        sp.wait_ge(lo_done, ready)
                        for h in range(2):
                            for part in range(2):
                                sp.dma_start(out_rows[u, :, :, part, h, :],
                                             parts[h * HALF:h * HALF + C, s, part].rearrange("p y b w -> p y (b w)").bitcast(F32)
                                             ).then_inc(stored[s], 16)
                peeled(sp, H // UNIT // 2, step)
                for s in range(2):
                    sp.wait_ge(stored[s], 64 * (H // UNIT // 2))

            @block.gpsimd
            def _(pool):
                pool.memset(parts[:, :, :, :, :, 0:1].bitcast(F32), 0.0).then_inc(bordered, 1)
                pool.memset(parts[:, :, :, :, :, WP - 1:WP].bitcast(F32), 0.0).then_inc(bordered, 1)
                pool.memset(power[:, :], -0.5).then_inc(steps, 1)
                pool.wait_ge(loaded, 48)
                pool.tensor_scalar(tmp[:, 0:1], par[:, 3:4], EPS, 0.0, ALU.add, ALU.add).then_inc(steps, 1)
                pool.wait_ge(steps, 2)
                pool.tensor_tensor(tmp[:, 1:2], tmp[:, 0:1], power[:, :], ALU.pow).then_inc(steps, 1)
                pool.wait_ge(steps, 3)
                pool.tensor_tensor(tmp[:, 2:3], tmp[:, 1:2], par[:, 0:1], ALU.mult).then_inc(steps, 1)
                pool.wait_ge(steps, 4)
                pool.tensor_tensor(tmp[:, 3:4], par[:, 2:3], tmp[:, 2:3], ALU.mult).then_inc(steps, 1)
                pool.tensor_scalar(cs[:, 0:1], tmp[:, 2:3], 1.0 / W, 0.0, ALU.mult, ALU.add).then_inc(consts, 1)
                pool.wait_ge(steps, 5)
                pool.tensor_tensor(cs[:, 1:2], par[:, 1:2], tmp[:, 3:4], ALU.subtract).then_inc(consts, 1)
                pool.tensor_scalar(cs[:, 2:3], par[:, 4:5], -1.0, 0.0, ALU.add, ALU.add).then_inc(consts, 1)

            @block.tensor
            def _(pe):
                pe.wait_ge(loaded, 48)
                pe.wait_ge(summed, 2)
                for h in range(2):
                    lo = h * HALF
                    mm = nc.tensor.matmul(ps[0][lo:lo + HALF, :], w1[lo:lo + C, :],
                                          means[lo:lo + C, :, :].rearrange("p a n -> p (a n)"), start=True, stop=True)
                mm.then_inc(squeezed, 1)
                pe.wait_ge(zdone, 1)
                for a in range(2):
                    for h in range(2):
                        lo = h * HALF
                        mm = nc.tensor.matmul(ps[1][lo:lo + HALF, a * H * HB:(a + 1) * H * HB],
                                              wg[lo:lo + HALF, a, :], z[lo:lo + HALF, 2, a * H * HB:(a + 1) * H * HB],
                                              start=(a == 0), stop=True, skip_group_check=True)
                mm.then_inc(widened, 1)

            @block.scalar
            def _(act):
                act.wait_ge(consts, 3)
                act.wait_ge(squeezed, 1)
                nc.scalar.activation(z[:, 0, :], ps[0][:, :], ACT.Identity, bias=cs[:, 1:2], scale=cs[:, 0:1]).then_inc(normed, 1)
                act.wait_ge(widened, 1)
                nc.scalar.activation(gate[:, :, :], ps[1][:, :].rearrange("p (a n) -> p a n", a=2), ACT.Sigmoid).then_inc(gated, 1)
                act.wait_ge(bordered, 2)

                def step(k):
                    for s in range(2):
                        act.wait_ge(times_h, 2 * k + s + 1)
                        wait(act, stored[s], 64 * k)
                        nc.scalar.activation(parts[:, s, 0, :, :, 1:W + 1],
                                             xg[:, s].rearrange("p y (b w) -> p y b w", b=HB), ACT.Copy).then_inc(hi_done, 1)
                peeled(act, H // UNIT // 2, step)

            @block.vector
            def _(dve):
                nc.vector.tensor_reduce(means[:, 0, :].rearrange("p (y b) -> p y b", b=HB), kept, AX.X, ALU.add).then_inc(summed, 1)
                nc.vector.tensor_reduce(means[:, 1, :].rearrange("p (b w) -> p b w", b=HB),
                                        kept.rearrange("p y b w -> p b w y"), AX.X, ALU.add).then_inc(summed, 1)
                dve.wait_ge(normed, 1)
                nc.vector.tensor_scalar(z[:, 1, :], z[:, 0, :], 0.0, cs[:, 2:3], ALU.min, ALU.mult).then_inc(zneg, 1)
                dve.wait_ge(zneg, 1)
                nc.vector.tensor_tensor(z[:, 2, :], z[:, 0, :], z[:, 1, :], ALU.add).then_inc(zdone, 1)
                dve.wait_ge(gated, 1)
                a_h = gate[:, 0, :].rearrange("p (u y b) -> p u (y b)", b=HB, y=UNIT)
                a_w = gate[:, 1, :]
                flat = hs[:, 0:H // 2, :].rearrange("p a n -> p (a n)").rearrange("p (u y n) -> p u y n", y=UNIT, n=HB * W)

                def step(k):
                    for s in range(2):
                        u = dve.snap(2 * k + s) if not isinstance(k, int) else 2 * k + s
                        nc.vector.tensor_tensor(xa[:, s], flat[:, bass.ds(u, 1)].rearrange("p a y n -> p (a y) n"),
                                                a_w.unsqueeze(1).broadcast_to([P, UNIT, HB * W]), ALU.mult).then_inc(times_w, 1)
                        dve.wait_ge(times_w, 2 * k + s + 1)
                        nc.vector.tensor_tensor(xg[:, s].rearrange("p y (b w) -> p (y b) w", b=HB),
                                                xa[:, s].rearrange("p y (b w) -> p (y b) w", b=HB),
                                                a_h[:, bass.ds(u, 1), :].rearrange("p a n -> p (a n)").unsqueeze(2).broadcast_to([P, UNIT * HB, W]),
                                                ALU.mult).then_inc(times_h, 1)
                        dve.wait_ge(hi_done, 2 * k + s + 1)
                        nc.vector.tensor_tensor(parts[:, s, 1, :, :, 1:W + 1].rearrange("p y b w -> p (y b) w"),
                                                xg[:, s].rearrange("p y (b w) -> p (y b) w", b=HB),
                                                parts[:, s, 0, :, :, 1:W + 1].rearrange("p y b w -> p (y b) w").bitcast(F32),
                                                ALU.subtract).then_inc(lo_done, 1)
                peeled(dve, H // UNIT // 2, step)


def lstm_scans(nc, D, hs, rows_in, weights, tag):
    ctx = ExitStack()
    near, far = (0, HALF), (HALF, 0)
    K = HALF + C
    with ctx:
        sems = []
        ctx.callback(release, nc, sems)

        def sb(name, shape, dt=F32):
            return ctx.enter_context(nc.sbuf_tensor(name + tag, shape, dt))

        def sem(name):
            sems.append(nc.alloc_semaphore(name + tag))
            return sems[-1]

        NW = 2 * 2 * 3 * K
        w = sb("w", [K, NW])
        w_hi = sb("w_hi", [K, 2, 2, 3, K], F32R)
        w_lo = sb("w_lo", [K, 2, 2, 3, K], F32R)
        xh = sb("xh", [P, 2, 2, 2, B, WP], F32R)
        gate_if = sb("gate_if", [P, 2, BW])
        gate_g = sb("gate_g", [P, 2, BW])
        keep = sb("keep", [P, 2, BW])
        add = sb("add", [P, 2, BW])
        cell = sb("cell", [P, 2, BW])
        tanh_c = sb("tanh_c", [P, 2, BW])
        ps = [[ctx.enter_context(nc.psum_tensor(f"gates{d}{m}" + tag, [P, BW], F32)) for m in range(2)] for d in range(2)]

        w_loaded = sem("w_loaded")
        w_split = sem("w_split")
        cleared = sem("cleared")
        x_in = [[sem(f"x_in{d}{s}") for s in range(2)] for d in range(2)]
        gates = [[sem(f"gates_if{d}"), sem(f"gates_go{d}")] for d in range(2)]
        sig_if = [sem(f"sig_if{d}") for d in range(2)]
        tanh_g = [sem(f"tanh_g{d}") for d in range(2)]
        tanhs = [sem(f"tanhs{d}") for d in range(2)]
        kept = [sem(f"kept{d}") for d in range(2)]
        added = [sem(f"added{d}") for d in range(2)]
        cells = [sem(f"cells{d}") for d in range(2)]
        h_hi = [sem(f"h_hi{d}") for d in range(2)]
        h_full = [sem(f"h_full{d}") for d in range(2)]
        h_lo = [sem(f"h_lo{d}") for d in range(2)]

        with nc.Block() as block:
            @block.sync
            def _(sp):
                sp.dma_start(w[:, :], D[weights]).then_inc(w_loaded, 16)
                sp.wait_ge(cleared, 3)

                def load(row, d, s):
                    sp.dma_start(xh[far[d]:far[d] + C, d, s].rearrange("p q b w -> p (q b w)").bitcast(F32),
                                 rows_in[row].rearrange("c q n -> c (q n)")).then_inc(x_in[d][s], 16)
                for s in range(2):
                    load(s, 0, s)
                    load(H - 1 - s, 1, s)
                with sp.Fori(0, H // 2 - 1) as k:
                    for s in range(2):
                        row_f = sp.snap(2 * k + s + 2)
                        row_b = sp.snap(k * -2 + (H - 3 - s))
                        done = sp.snap(2 * k + s + 1)
                        sp.wait_ge(gates[0][1], done)
                        load(row_f, 0, s)
                        sp.wait_ge(gates[1][1], done)
                        load(row_b, 1, s)

            @block.gpsimd
            def _(pool):
                pool.memset(xh[:, :, :, :, :, :].bitcast(F32), 0.0).then_inc(cleared, 1)
                pool.wait_ge(cleared, 1)
                pool.memset(xh[32:64, :, :, 0].bitcast(F32), 1.0).then_inc(cleared, 1)
                pool.wait_ge(cleared, 2)
                pool.memset(xh[32:C, 0, :, 0].bitcast(F32), 0.0).then_inc(cleared, 1)
                with pool.Fori(0, H // 2) as k:
                    for s in range(2):
                        for d in range(2):
                            pool.wait_ge(tanhs[d], 2 * k + s + 1)
                            row = 2 * k + s if d == 0 else k * -2 + (H - 1 - s)
                            pool.tensor_tensor(hs[near[d]:near[d] + C, bass.ds(row, 1), :].rearrange("p a n -> p (a n)"),
                                               gate_g[far[d]:far[d] + C, d, :], tanh_c[far[d]:far[d] + C, d, :],
                                               ALU.mult).then_inc(h_full[d], 1)

            @block.tensor
            def _(pe):
                pe.wait_ge(w_split, 2)
                with pe.Fori(0, H // 2) as k:
                    for s in range(2):
                        for d in range(2):
                            pe.wait_ge(x_in[d][s], 16 * k + 16)
                            pe.wait_ge(h_hi[d], 2 * k + s + 1)
                            for m in range(2):
                                def taps(weight, part, first, last):
                                    for t in range(3):
                                        mm = nc.tensor.matmul(ps[d][m][0:K, :], weight[:, d, m, t, :],
                                                              xh[0:K, d, s, part, :, t:t + W],
                                                              start=(first and t == 0), stop=(last and t == 2))
                                    return mm
                                taps(w_hi, 0, True, False)
                                taps(w_lo, 0, False, False)
                                if m == 0:
                                    pe.wait_ge(h_lo[d], 2 * k + s + 1)
                                taps(w_hi, 1, False, True).then_inc(gates[d][m], 1)

            @block.scalar
            def _(act):
                with act.Fori(0, H // 2) as k:
                    for s in range(2):
                        for d in range(2):
                            n, f = near[d], far[d]
                            act.wait_ge(gates[d][0], 2 * k + s + 1)
                            nc.scalar.activation(gate_if[0:K, d, :], ps[d][0][0:K, :], ACT.Sigmoid).then_inc(sig_if[d], 1)
                            act.wait_ge(gates[d][1], 2 * k + s + 1)
                            nc.scalar.activation(gate_g[n:n + C, d, :], ps[d][1][n:n + C, :], ACT.Tanh).then_inc(tanh_g[d], 1)
                            nc.scalar.activation(gate_g[f:f + C, d, :], ps[d][1][f:f + C, :], ACT.Sigmoid).then_inc(tanh_g[d], 1)
                            act.wait_ge(cells[d], 2 * k + s + 2)
                            nc.scalar.activation(tanh_c[f:f + C, d, :], cell[f:f + C, d, :], ACT.Tanh).then_inc(tanhs[d], 1)

            @block.vector
            def _(dve):
                for d in range(2):
                    nc.vector.memset(cell[:, d, :], 0.0).then_inc(cells[d], 1)
                dve.wait_ge(w_loaded, 16)
                flat_hi = w_hi[:, :, :, :, :].rearrange("p a b c n -> p (a b c n)")
                flat_lo = w_lo[:, :, :, :, :].rearrange("p a b c n -> p (a b c n)")
                nc.vector.tensor_copy(flat_hi, w[:, :]).then_inc(w_split, 1)
                dve.wait_ge(w_split, 1)
                nc.vector.tensor_tensor(flat_lo, w[:, :], flat_hi.bitcast(F32), ALU.subtract).then_inc(w_split, 1)
                dve.wait_ge(cleared, 3)
                for d in range(2):
                    nc.vector.memset(keep[:, d, :], 0.0).then_inc(h_hi[d], 1)
                    nc.vector.memset(add[:, d, :], 0.0).then_inc(h_lo[d], 1)
                with dve.Fori(0, H // 2) as k:
                    for s in range(2):
                        for d in range(2):
                            n, f = near[d], far[d]
                            dve.wait_ge(cells[d], 2 * k + s + 1)
                            dve.wait_ge(sig_if[d], 2 * k + s + 1)
                            nc.vector.tensor_tensor(keep[n:n + C, d, :], gate_if[f:f + C, d, :], cell[f:f + C, d, :],
                                                    ALU.mult).then_inc(kept[d], 1)
                            dve.wait_ge(tanh_g[d], 4 * k + 2 * s + 1)
                            nc.vector.tensor_tensor(add[n:n + C, d, :], gate_if[n:n + C, d, :], gate_g[n:n + C, d, :],
                                                    ALU.mult).then_inc(added[d], 1)
                            dve.wait_ge(kept[d], 2 * k + s + 1)
                            dve.wait_ge(added[d], 2 * k + s + 1)
                            nc.vector.tensor_tensor(cell[f:f + C, d, :], keep[n:n + C, d, :], add[n:n + C, d, :],
                                                    ALU.add).then_inc(cells[d], 1)
                            dve.wait_ge(tanhs[d], 2 * k + s + 1)
                            hi = xh[n:n + C, d, 1 - s, 0, :, 1:W + 1]
                            nc.vector.tensor_tensor(hi, gate_g[f:f + C, d, :].rearrange("p (b w) -> p b w", b=B),
                                                    tanh_c[f:f + C, d, :].rearrange("p (b w) -> p b w", b=B),
                                                    ALU.mult).then_inc(h_hi[d], 1)
                            dve.wait_ge(h_hi[d], 2 * k + s + 2)
                            dve.wait_ge(h_full[d], 2 * k + s + 1)
                            row = 2 * k + s if d == 0 else k * -2 + (H - 1 - s)
                            nc.vector.tensor_tensor(xh[n:n + C, d, 1 - s, 1, :, 1:W + 1],
                                                    hs[n:n + C, bass.ds(row, 1), :].rearrange("p a (b w) -> p (a b) w", b=B),
                                                    hi.bitcast(F32), ALU.subtract).then_inc(h_lo[d], 1)


def project_and_norm(nc, D, hs, rows_in, rows_out, weights, params, tag):
    ctx = ExitStack()
    K = HALF + C
    HH = H // 2
    with ctx:
        sems = []
        ctx.callback(release, nc, sems)

        def sb(name, shape, dt=F32):
            return ctx.enter_context(nc.sbuf_tensor(name + tag, shape, dt))

        def sem(name):
            sems.append(nc.alloc_semaphore(name + tag))
            return sems[-1]

        w = sb("pw", [K, HALF])
        par = sb("ppar", [P, 2])
        sumdif = sb("sumdif", [P, 2, P])
        stats = sb("stats", [P, HH, 6])
        mv = sb("mv", [P, 2])
        tot = sb("tot", [P, 4])
        tmp = sb("ptmp", [P, 6])
        cs = sb("pcs", [P, 2])
        res_in = sb("res_in", [P, 2, 2, B, WP])
        res = sb("res", [P, 2, BW])
        act_out = sb("act_out", [P, 2, BW])
        val = sb("val", [P, 2, BW])
        parts = sb("pparts", [P, 2, 2, B, WP], F32R)
        ps = [ctx.enter_context(nc.psum_tensor(f"pps{i}" + tag, [P, BW], F32)) for i in range(BANKS - 1)]
        ps_stat = ctx.enter_context(nc.psum_tensor("ps_stat" + tag, [P, BW], F32))
        NB = BANKS - 1

        loaded = sem("p_loaded")
        cleared = sem("p_cleared")
        projected = sem("projected")
        kept = sem("y_kept")
        counted = sem("counted")
        aggregated = sem("aggregated")
        shared = sem("shared")
        steps = sem("p_steps")
        consts = sem("p_consts")
        r_in = [sem(f"r_in{s}") for s in range(2)]
        summed = sem("r_summed")
        normed = sem("p_normed")
        valued = sem("valued")
        hi_done = sem("p_hi")
        lo_done = sem("p_lo")
        stored = [sem(f"p_stored{s}") for s in range(2)]

        with nc.Block() as block:
            @block.sync
            def _(sp):
                sp.dma_start(w[:, :], D[weights]).then_inc(loaded, 16)
                sp.dma_start(par[:, :], D[params]).then_inc(loaded, 16)
                sp.dma_start(sumdif[:, :, :], D["sum_dif"]).then_inc(loaded, 16)
                sp.wait_ge(cleared, 3)

                def load(y, y2, s):
                    for h, row in enumerate((y, y2)):
                        sp.dma_start(res_in[h * HALF:h * HALF + C, s].rearrange("p q b w -> p (q b w)"),
                                     rows_in[row].rearrange("c q n -> c (q n)")).then_inc(r_in[s], 16)

                def store(y, y2, s):
                    for h, row in enumerate((y, y2)):
                        sp.dma_start(rows_out[row].rearrange("c q n -> c (q n)"),
                                     parts[h * HALF:h * HALF + C, s].rearrange("p q b w -> p (q b w)").bitcast(F32)
                                     ).then_inc(stored[s], 16)
                for s in range(2):
                    load(s, s + HH, s)

                def step(k, last=False):
                    for s in range(2):
                        y, y2 = held(sp, 2 * k + s), held(sp, 2 * k + (s + HH))
                        a, a2 = held(sp, 2 * k + (s + 2)), held(sp, 2 * k + (s + 2 + HH))
                        ready = held(sp, 2 * k + s + 1)
                        sp.wait_ge(lo_done, ready)
                        store(y, y2, s)
                        if not last:
                            load(a, a2, s)
                with sp.Fori(0, HH // 2 - 1) as k:
                    step(k)
                step(HH // 2 - 1, last=True)
                for s in range(2):
                    sp.wait_ge(stored[s], 32 * (HH // 2))

            @block.gpsimd
            def _(pool):
                pool.memset(res_in[:, :, :, :, :], 0.0).then_inc(cleared, 1)
                pool.memset(parts[:, :, :, :, :].bitcast(F32), 0.0).then_inc(cleared, 1)
                pool.memset(tmp[:, 5:6], -0.5).then_inc(cleared, 1)
                pool.wait_ge(cleared, 3)
                pool.wait_ge(steps, 2)
                pool.tensor_tensor(tmp[:, 1:2], tmp[:, 0:1], tmp[:, 5:6], ALU.pow).then_inc(steps, 1)
                pool.wait_ge(steps, 3)
                pool.tensor_tensor(cs[:, 0:1], tmp[:, 1:2], par[:, 0:1], ALU.mult).then_inc(steps, 1)
                pool.wait_ge(steps, 4)
                pool.tensor_tensor(tmp[:, 2:3], tot[:, 0:1], cs[:, 0:1], ALU.mult).then_inc(steps, 1)
                pool.wait_ge(steps, 5)
                pool.tensor_tensor(cs[:, 1:2], par[:, 1:2], tmp[:, 2:3], ALU.subtract).then_inc(consts, 1)

                def step(k):
                    for s in range(2):
                        pool.wait_ge(r_in[s], 32 * k + 32)
                        wait(pool, valued, 2 * k + s - 1)
                        pool.tensor_tensor(res[:, s, :].rearrange("p (b w) -> p b w", b=B),
                                           res_in[:, s, 0, :, 1:W + 1], res_in[:, s, 1, :, 1:W + 1], ALU.add).then_inc(summed, 1)
                peeled(pool, HH // 2, step)

            @block.tensor
            def _(pe):
                pe.wait_ge(loaded, 48)
                for y in range(HH):
                    if y >= NB:
                        pe.wait_ge(kept, y - NB + 1)
                    for h in range(2):
                        mm = nc.tensor.matmul(ps[y % NB][h * HALF:(h + 1) * HALF, :], w[:, :], hs[0:K, y + h * HH, :],
                                              start=True, stop=True)
                    mm.then_inc(projected, 1)
                pe.wait_ge(aggregated, 1)
                for a in range(2):
                    mm = nc.tensor.matmul(ps_stat[:, 2 * a:2 * a + 2], sumdif[:, a, :], mv[:, :],
                                          start=(a == 0), stop=True, skip_group_check=True)
                mm.then_inc(shared, 1)

            @block.scalar
            def _(act):
                for y in range(HH):
                    act.wait_ge(projected, y + 1)
                    nc.scalar.activation(hs[:, y, :], ps[y % NB][:, :], ACT.Copy).then_inc(kept, 1)
                act.wait_ge(consts, 1)

                def step(k):
                    for s in range(2):
                        wait(act, valued, 2 * k + s - 1)
                        y = 2 * k + s
                        nc.scalar.activation(act_out[:, s, :], hs[:, bass.ds(y, 1), :].rearrange("p a n -> p (a n)"), ACT.Relu,
                                             bias=cs[:, 1:2], scale=cs[:, 0:1]).then_inc(normed, 1)
                    for s in range(2):
                        act.wait_ge(valued, 2 * k + s + 1)
                        wait(act, stored[s], 32 * k)
                        nc.scalar.activation(parts[:, s, 0, :, 1:W + 1], val[:, s, :].rearrange("p (b w) -> p b w", b=B),
                                             ACT.Copy).then_inc(hi_done, 1)
                peeled(act, HH // 2, step)

            @block.vector
            def _(dve):
                for y in range(HH):
                    dve.wait_ge(kept, y + 1)
                    nc.vector.bn_stats(stats[:, y, :], hs[:, y, :]).then_inc(counted, 1)
                dve.wait_ge(counted, HH)
                nc.vector.bn_aggr(mv[:, :], stats[:, :, :].rearrange("p a n -> p (a n)")).then_inc(aggregated, 1)
                dve.wait_ge(shared, 1)
                nc.vector.tensor_copy(tot[:, :], ps_stat[:, 0:4]).then_inc(shared, 1)
                dve.wait_ge(shared, 2)
                nc.vector.scalar_tensor_tensor(tmp[:, 3:4], tot[:, 2:3], tot[:, 2:3], tot[:, 1:2], ALU.mult, ALU.add).then_inc(steps, 1)
                dve.wait_ge(steps, 1)
                nc.vector.tensor_scalar(tmp[:, 0:1], tmp[:, 3:4], EPS, None, ALU.add).then_inc(steps, 1)
                dve.wait_ge(cleared, 3)

                def step(k):
                    for s in range(2):
                        dve.wait_ge(normed, 2 * k + s + 1)
                        dve.wait_ge(summed, 2 * k + s + 1)
                        wait(dve, lo_done, 2 * k + s - 1)
                        nc.vector.tensor_tensor(val[:, s, :], act_out[:, s, :], res[:, s, :], ALU.add).then_inc(valued, 1)
                    for s in range(2):
                        dve.wait_ge(hi_done, 2 * k + s + 1)
                        nc.vector.tensor_tensor(parts[:, s, 1, :, 1:W + 1], val[:, s, :].rearrange("p (b w) -> p b w", b=B),
                                                parts[:, s, 0, :, 1:W + 1].bitcast(F32), ALU.subtract).then_inc(lo_done, 1)
                peeled(dve, HH // 2, step)


def inverted_residual(nc, D, rows_in, out):
    ctx = ExitStack()
    K = HALF + C
    NV = 5
    NT = B - NV
    RING = 4
    with ctx:
        sems = []
        ctx.callback(release, nc, sems)

        def sb(name, shape, dt=F32):
            return ctx.enter_context(nc.sbuf_tensor(name, shape, dt))

        def sem(name):
            sems.append(nc.alloc_semaphore(name))
            return sems[-1]

        w1 = sb("b_w1", [K, HID])
        w1_hi = sb("b_w1_hi", [K, HID], F32R)
        w1_lo = sb("b_w1_lo", [K, HID], F32R)
        wd = sb("b_wd", [GC, GROUPS, 9])
        w2 = sb("b_w2", [GC, GROUPS, HALF])
        bn_hid = sb("b_bn_hid", [GC, 4, 2, GROUPS])
        bn_out = sb("b_bn_out", [P, 4])
        eye = sb("b_eye", [GC, GC])
        diag = sb("b_diag", [GC, 2, 9, GC])
        diag_hi = sb("b_diag_hi", [GC, 2, 9, GC], F32R)
        diag_lo = sb("b_diag_lo", [GC, 2, 9, GC], F32R)
        cs = sb("b_cs", [GC, 2, 2, GROUPS])
        cso = sb("b_cso", [P, 2])
        tmp = sb("b_tmp", [P, 4, 2 * GROUPS])
        x3 = sb("b_x3", [P, RING, B, WP], F32R)
        hv0 = sb("b_hv0", [GC, RING, B, WP])
        hv1 = sb("b_hv1", [GC, RING, NV, WP])
        ht1 = sb("b_ht1", [GC, RING, 2, NT, WP], F32R)
        ht2 = sb("b_ht2", [GC, RING, 2, B, WP], F32R)
        full1 = sb("b_full1", [GC, 2, NT, W])
        full2 = sb("b_full2", [GC, 2, B, W])
        acc = sb("b_acc", [GC, 2, (B + NV) * W])
        h2 = sb("b_h2", [GC, 2, GROUPS, BW])
        res_in = sb("b_res_in", [P, 2, 2, B, WP])
        res = sb("b_res", [P, 2, BW])
        scaled = sb("b_scaled", [P, 2, BW])
        o = sb("b_o", [P, 2, BW])
        ps1 = [ctx.enter_context(nc.psum_tensor(f"b_ps1{i}", [P, BW], F32)) for i in range(GROUPS)]
        ps2 = [ctx.enter_context(nc.psum_tensor(f"b_ps2{i}", [P, BW], F32)) for i in range(2)]
        ps3 = [ctx.enter_context(nc.psum_tensor(f"b_ps3{i}", [P, BW], F32)) for i in range(2)]

        loaded = sem("b_loaded")
        cleared = sem("b_cleared")
        steps = sem("b_steps")
        consts = sem("b_consts")
        diags = sem("b_diags")
        w_split = sem("b_w_split")
        x_in = [sem(f"b_x_in{s}") for s in range(RING)]
        r_in = [sem(f"b_r_in{s}") for s in range(2)]
        expanded = sem("b_expanded")
        rows_v = sem("b_rows_v")
        rows_hi = sem("b_rows_hi")
        rows_full = sem("b_rows_full")
        rows_lo = sem("b_rows_lo")
        depth_t = sem("b_depth_t")
        taps_v = sem("b_taps_v")
        diag_steps = sem("b_diag_steps")
        squashed = sem("b_squashed")
        reduced = sem("b_reduced")
        affine = sem("b_affine")
        r_sum = sem("b_r_sum")
        final = sem("b_final")
        stored = [sem(f"b_stored{s}") for s in range(2)]

        def slot(y):
            return y % RING

        with nc.Block() as block:
            @block.sync
            def _(sp):
                for tile, name in ((w1, "b_w1_T"), (wd, "b_wd"), (w2, "b_w2_T"), (bn_hid, "b_bn_hid"), (bn_out, "b_bn_out")):
                    ap = tile[tuple(slice(None) for _ in tile.shape)]
                    sp.dma_start(ap, D[name]).then_inc(loaded, 16)
                sp.wait_ge(cleared, 4)

                def load_x(row, s):
                    for part in range(2):
                        sp.dma_start(x3[part * HALF:part * HALF + C, s].rearrange("p b w -> p (b w)").bitcast(F32),
                                     rows_in[row][:, part, :]).then_inc(x_in[s], 16)

                def load_r(y, y1, s):
                    for h, row in enumerate((y, y1)):
                        sp.dma_start(res_in[h * HALF:h * HALF + C, s].rearrange("p q b w -> p (q b w)"),
                                     rows_in[row].rearrange("c q n -> c (q n)")).then_inc(r_in[s], 16)

                for y in range(RING):
                    load_x(y, y)
                for s in range(2):
                    load_r(2 * s, 2 * s + 1, s)

                def store(y, y1, s):
                    for h, row in enumerate((y, y1)):
                        sp.dma_start(out[row].rearrange("c b w -> c (b w)"),
                                     o[h * HALF:h * HALF + C, s, :]).then_inc(stored[s], 16)

                def step(k, last=False):
                    for u in range(RING):
                        s = u // 2
                        ahead = held(sp, k * RING + (u + RING))
                        used = held(sp, k * RING + (u + 1))
                        done = held(sp, k * 2 + (s - 1))
                        y, y1 = held(sp, k * RING + (2 * s - 4)), held(sp, k * RING + (2 * s - 3))
                        r, r1 = held(sp, k * RING + 2 * s), held(sp, k * RING + (2 * s + 1))
                        if not last:
                            sp.wait_ge(expanded, used)
                            load_x(ahead, u)
                        if u % 2 and not (isinstance(k, int) and k == 0):
                            sp.wait_ge(final, done)
                            store(y, y1, s)
                            load_r(r, r1, s)
                step(0)
                with sp.Fori(1, H // RING - 1) as k:
                    step(k)
                step(H // RING - 1, last=True)
                for s in range(2):
                    sp.wait_ge(final, H // 2 - 1 + s)
                    store(H - 4 + 2 * s, H - 3 + 2 * s, s)
                for s in range(2):
                    sp.wait_ge(stored[s], 32 * (H // RING))

            @block.gpsimd
            def _(pool):
                pool.memset(x3[:, :, :, :].bitcast(F32), 0.0).then_inc(cleared, 1)
                pool.memset(eye[:, :], 0.0).then_inc(cleared, 1)
                pool.wait_ge(cleared, 2)
                pool.affine_select(out=eye[:, :], in_=eye[:, :], compare_op=ALU.not_equal, fill=1.0, base=0,
                                   pattern=[[-1, GC]], channel_multiplier=1).then_inc(cleared, 1)
                pool.memset(tmp[:, 3, :], -0.5).then_inc(steps, 1)
                pool.memset(res_in[:, :, :, :, :], 0.0).then_inc(cleared, 1)
                for t in (hv0, hv1):
                    pool.memset(t[:, :, :, :], 0.0).then_inc(cleared, 1)
                for t in (ht1, ht2):
                    pool.memset(t[:, :, :, :, :].bitcast(F32), 0.0).then_inc(cleared, 1)
                pool.wait_ge(loaded, 80)
                pool.wait_ge(steps, 1)
                n = 2 * GROUPS

                def flat(i):
                    return bn_hid[:, i].rearrange("p a g -> p (a g)")
                pool.tensor_scalar(tmp[0:GC, 0, :], flat(3), EPS, 0.0, ALU.add, ALU.add).then_inc(steps, 1)
                pool.wait_ge(steps, 2)
                pool.tensor_tensor(tmp[0:GC, 1, :], tmp[0:GC, 0, :], tmp[0:GC, 3, :], ALU.pow).then_inc(steps, 1)
                pool.wait_ge(steps, 3)
                pool.tensor_tensor(cs[:, 0].rearrange("p a g -> p (a g)"), tmp[0:GC, 1, :], flat(0), ALU.mult).then_inc(steps, 1)
                pool.wait_ge(steps, 4)
                pool.tensor_tensor(tmp[0:GC, 2, :], flat(2), cs[:, 0].rearrange("p a g -> p (a g)"), ALU.mult).then_inc(steps, 1)
                pool.wait_ge(steps, 5)
                pool.tensor_tensor(cs[:, 1].rearrange("p a g -> p (a g)"), flat(1), tmp[0:GC, 2, :], ALU.subtract).then_inc(consts, 1)
                pool.tensor_scalar(tmp[:, 0, 0:1], bn_out[:, 3:4], EPS, 0.0, ALU.add, ALU.add).then_inc(steps, 1)
                pool.wait_ge(steps, 6)
                pool.tensor_tensor(tmp[:, 1, 0:1], tmp[:, 0, 0:1], tmp[:, 3, 0:1], ALU.pow).then_inc(steps, 1)
                pool.wait_ge(steps, 7)
                pool.tensor_tensor(cso[:, 0:1], tmp[:, 1, 0:1], bn_out[:, 0:1], ALU.mult).then_inc(steps, 1)
                pool.wait_ge(steps, 8)
                pool.tensor_tensor(tmp[:, 2, 0:1], bn_out[:, 2:3], cso[:, 0:1], ALU.mult).then_inc(steps, 1)
                pool.wait_ge(steps, 9)
                pool.tensor_tensor(cso[:, 1:2], bn_out[:, 1:2], tmp[:, 2, 0:1], ALU.subtract).then_inc(consts, 1)

                def low_parts(s, count):
                    pool.wait_ge(rows_full, count)
                    for ht, full in ((ht1, full1), (ht2, full2)):
                        pool.tensor_tensor(ht[:, s, 1, :, 1:W + 1], full[:, s % 2], ht[:, s, 0, :, 1:W + 1].bitcast(F32),
                                           ALU.subtract).then_inc(rows_lo, 1)

                def residual(k, s):
                    pool.wait_ge(r_in[s], 32 * k + 32)
                    wait(pool, final, 2 * k + s - 1)
                    pool.tensor_tensor(res[:, s, :].rearrange("p (b w) -> p b w", b=B),
                                       res_in[:, s, 0, :, 1:W + 1], res_in[:, s, 1, :, 1:W + 1], ALU.add).then_inc(r_sum, 1)
                for r in range(2):
                    low_parts(r, 2 * r + 2)

                def step(k, last=False):
                    for u in range(RING):
                        if last and u == 2:
                            pool.wait_ge(depth_t, 2 * (H - 2))
                            pool.wait_ge(taps_v, 18 * (H - 2))
                            for t, done in ((hv0, rows_v), (hv1, rows_v)):
                                pool.memset(t[:, 0], 0.0).then_inc(done, 1)
                            for t in (ht1, ht2):
                                pool.memset(t[:, 0, 0].bitcast(F32), 0.0).then_inc(rows_hi, 1)
                                pool.memset(t[:, 0, 1].bitcast(F32), 0.0).then_inc(rows_lo, 1)
                        elif not last or u < 2:
                            low_parts((u + 2) % RING, 2 * RING * k + 2 * (u + 3))
                        if u % 2:
                            residual(k, u // 2)
                step(0)
                with pool.Fori(1, H // RING - 1) as k:
                    step(k)
                step(H // RING - 1, last=True)

            @block.tensor
            def _(pe):
                pe.wait_ge(w_split, 2)
                pe.wait_ge(cleared, 8)

                def expand(y, k, s):
                    pe.wait_ge(x_in[s], 32 * k + 32)
                    wait(pe, rows_full, 2 * y)
                    for g in range(GROUPS):
                        for n, w in enumerate((w1_hi, w1_lo)):
                            mm = nc.tensor.matmul(ps1[g][0:GC, :], w[:, g * GC:(g + 1) * GC],
                                                  x3[0:K, s, :, 1:W + 1], start=(n == 0), stop=(n == 1))
                    mm.then_inc(expanded, 1)

                def depthwise(y, s):
                    pe.wait_ge(rows_hi, 2 * y + 4)
                    for g, ht in enumerate((ht1, ht2)):
                        n = ht.shape[3]
                        wait(pe, squashed, 4 * y + (g - 3))
                        for part, d in ((0, diag_hi), (0, diag_lo), (1, diag_hi)):
                            if part and g == 0:
                                pe.wait_ge(rows_lo, 2 * y + 4)
                            for t in range(9):
                                dy, dx = t // 3 - 1, t % 3
                                mm = nc.tensor.matmul(ps2[g][0:GC, 0:n * W], d[:, g, t, :],
                                                      ht[:, slot(s + dy), part, :, dx:dx + W],
                                                      start=(d is diag_hi and part == 0 and t == 0), stop=(part == 1 and t == 8))
                        mm.then_inc(depth_t, 1)

                def reduce_row(y, v):
                    pe.wait_ge(squashed, y * 4 + 4)
                    for g in range(GROUPS):
                        mm = nc.tensor.matmul(ps3[v // 2][(v % 2) * HALF:(v % 2 + 1) * HALF, :], w2[:, g, :],
                                              h2[:, v % 2, g, :], start=(g == 0), stop=(g == GROUPS - 1))
                    mm.then_inc(reduced, 1)
                for r in range(2):
                    expand(r, 0, r)
                pe.wait_ge(diags, 2)

                def step(k, first=False, last=False):
                    for u in range(RING):
                        if not last or u < 2:
                            expand(k * RING + (u + 2), k + (u + 2) // RING, (u + 2) % RING)
                        depthwise(k * RING + u, u)
                        if not (first and u == 0):
                            v = (u - 1) % RING
                            if not first and v % 2 == 0:
                                wait(pe, affine, 2 * k - 1 + (0 if u == 1 else 1))
                            reduce_row(k * RING + (u - 1), v)

                step(0, first=True)
                with pe.Fori(1, H // RING - 1) as k:
                    step(k)
                step(H // RING - 1, last=True)
                reduce_row(H - 1, RING - 1)

            @block.scalar
            def _(act):
                act.wait_ge(consts, 2)
                act.wait_ge(cleared, 8)

                def hidden(y, s):
                    act.wait_ge(expanded, y + 1)
                    wait(act, depth_t, 2 * y - 4)
                    wait(act, taps_v, 18 * y - 36)
                    wait(act, rows_lo, 2 * y - 2)

                    def relu(dst, g, b0, b1, done):
                        nc.scalar.activation(dst, ps1[g][0:GC, b0 * W:b1 * W].rearrange("p (b w) -> p b w", w=W), ACT.Relu,
                                             bias=cs[:, 1, 0, g:g + 1], scale=cs[:, 0, 0, g:g + 1]).then_inc(done, 1)
                    relu(hv0[:, s, :, 1:W + 1], 0, 0, B, rows_v)
                    relu(hv1[:, s, :, 1:W + 1], 1, 0, NV, rows_v)
                    relu(ht1[:, s, 0, :, 1:W + 1], 1, NV, B, rows_hi)
                    relu(ht2[:, s, 0, :, 1:W + 1], 2, 0, B, rows_hi)
                    relu(full1[:, s % 2], 1, NV, B, rows_full)
                    relu(full2[:, s % 2], 2, 0, B, rows_full)

                def squash(y, s):
                    def relu(dst, src, g):
                        nc.scalar.activation(dst, src, ACT.Relu, bias=cs[:, 1, 1, g:g + 1],
                                             scale=cs[:, 0, 1, g:g + 1]).then_inc(squashed, 1)
                    wait(act, reduced, y - 1)
                    act.wait_ge(depth_t, 2 * y + 2)
                    relu(h2[:, s % 2, 1, NV * W:], ps2[0][0:GC, 0:NT * W], 1)
                    relu(h2[:, s % 2, 2, :], ps2[1][0:GC, :], 2)
                    act.wait_ge(taps_v, 18 * y + 18)
                    relu(h2[:, s % 2, 0, :], acc[:, s % 2, 0:BW], 0)
                    relu(h2[:, s % 2, 1, 0:NV * W], acc[:, s % 2, BW:BW + NV * W], 1)

                def affine_rows(j, s):
                    act.wait_ge(reduced, 2 * j + 2)
                    wait(act, final, j - 1)
                    nc.scalar.activation(scaled[:, s, :], ps3[s][:, :], ACT.Identity, bias=cso[:, 1:2],
                                         scale=cso[:, 0:1]).then_inc(affine, 1)
                for r in range(2):
                    hidden(r, r)

                def step(k, first=False, last=False):
                    for u in range(RING):
                        if not last or u < 2:
                            hidden(k * RING + (u + 2), (u + 2) % RING)
                        squash(k * RING + u, u)
                        if u % 2 == 0 and not (first and u == 0):
                            affine_rows(k * 2 + (u // 2 - 1), (u // 2 - 1) % 2)
                step(0, first=True)
                with act.Fori(1, H // RING - 1) as k:
                    step(k)
                step(H // RING - 1, last=True)
                affine_rows(H // 2 - 1, 1)

            @block.vector
            def _(dve):
                dve.wait_ge(loaded, 80)
                nc.vector.tensor_copy(w1_hi[:, :], w1[:, :]).then_inc(w_split, 1)
                dve.wait_ge(w_split, 1)
                nc.vector.tensor_tensor(w1_lo[:, :], w1[:, :], w1_hi[:, :].bitcast(F32), ALU.subtract).then_inc(w_split, 1)
                dve.wait_ge(cleared, 8)
                for g in range(2):
                    for t in range(9):
                        last_one = nc.vector.tensor_scalar(diag[:, g, t, :], eye[:, :], wd[:, g + 1, t:t + 1], None, ALU.mult)
                        last_one.then_inc(diag_steps, 1)
                dve.wait_ge(diag_steps, 18)

                def flat(t):
                    return t[:, :, :, :].rearrange("p a b n -> p (a b n)")
                nc.vector.tensor_copy(flat(diag_hi), flat(diag)).then_inc(diags, 1)
                dve.wait_ge(diags, 1)
                nc.vector.tensor_tensor(flat(diag_lo), flat(diag), flat(diag_hi).bitcast(F32), ALU.subtract).then_inc(diags, 1)

                def depthwise(y, s):
                    dve.wait_ge(rows_v, 2 * y + 4)
                    wait(dve, squashed, 4 * y - 4)
                    parts = ((hv0, 0, 0, B), (hv1, 1, BW, NV))
                    for t in range(9):
                        dy, dx = t // 3 - 1, t % 3
                        for i, (hv, g, at, n) in enumerate(parts):
                            sums = acc[:, s % 2, at:at + n * W].rearrange("p (b w) -> p b w", w=W)
                            src = hv[:, slot(s + dy), :, dx:dx + W]
                            if t:
                                dve.wait_ge(taps_v, 18 * y + (2 * t - 1 + i))
                                nxt = nc.vector.scalar_tensor_tensor(sums, src, wd[:, g, t:t + 1], sums, ALU.mult, ALU.add)
                            else:
                                nxt = nc.vector.tensor_scalar(sums, src, wd[:, g, t:t + 1], None, ALU.mult)
                            nxt.then_inc(taps_v, 1)

                def finish(j, s, earlier):
                    dve.wait_ge(affine, j + 1)
                    dve.wait_ge(r_sum, j + 1)
                    wait(dve, stored[s], 32 * earlier)
                    nc.vector.tensor_tensor(o[:, s, :], scaled[:, s, :], res[:, s, :], ALU.add).then_inc(final, 1)

                def step(k):
                    for u in range(RING):
                        depthwise(k * RING + u, u)
                        if u == 1 and not (isinstance(k, int) and k == 0):
                            finish(k * 2 - 1, 1, k - 1)
                        if u == 3:
                            finish(k * 2, 0, k)
                step(0)
                step(1)
                with dve.Fori(2, H // RING) as k:
                    step(k)
                finish(H // 2 - 1, 1, H // RING - 1)


def build(nc, D, out, stop=99):
    ctx = ExitStack()
    with ctx:
        hs_ctx = ctx.enter_context(ExitStack())
        hs = hs_ctx.enter_context(nc.sbuf_tensor("hs", [P, H, BW], F32))
        mixed = nc.dram_tensor("mixed", (PAIRS, P, BW), F32, kind="Internal").ap()
        edged = nc.dram_tensor("edged", (PAIRS, P, BW), F32, kind="Internal").ap()
        D = dict(D, mixed=mixed, edged=edged)
        for q in ("mixed", "edged"):
            D[q + "_c"] = D[q].rearrange("k (a u y) (h n) -> (k a) u y h n", a=2, y=4, h=2)
        rows = [nc.dram_tensor(f"rows{i}", (H, C, 2, ROW), F32, kind="Internal").ap() for i in range(3)]
        units = rows[0].rearrange("(u y) c q (h n) -> u c y q h n", y=4, h=2)
        axial_filters(nc, D, hs)
        if stop >= 2:
            mix_channels(nc, D, hs)
        if stop >= 3:
            coordinate_attention(nc, D, hs, units)
        for n, layer in enumerate(("l1", "l2")):
            if stop >= 4 + n:
                lstm_scans(nc, D, hs, rows[n], layer + "_w", "_" + layer)
                project_and_norm(nc, D, hs, rows[n], rows[n + 1], layer + "_proj_T", layer + "_params", "_" + layer)
        if stop == 99:
            hs_ctx.close()
            inverted_residual(nc, D, rows[2], out)
        if stop < 99:
            d = ctx.enter_context(nc.semaphore("dbg"))
            with nc.Block() as block:
                @block.sync
                def _(sp):
                    if stop == 1:
                        sp.dma_start(out.rearrange("a c b w -> (a c b w)"), mixed.rearrange("a b c -> (a b c)")).then_inc(d, 16)
                    if stop == 2:
                        of = out.rearrange("a c b w -> (a c b w)").rearrange("(c n) -> c n", c=2 * C)
                        for h in range(2):
                            sp.dma_start(of[h * C:(h + 1) * C], hs[h * HALF:h * HALF + C, 0:H // 2, :].rearrange("p a n -> p (a n)")).then_inc(d, 16)
                    if stop >= 3:
                        sp.dma_start(out.rearrange("y c b w -> (y c) b w"),
                                     rows[stop - 3].rearrange("y c q (b w) -> (y c) q b w", b=B)[:, 0, :, 1:W + 1]).then_inc(d, 16)
                    sp.wait_ge(d, 32 if stop == 2 else 16)


def halves(rows, n=HALF):
    rows = np.asarray(rows)
    out = np.zeros((P,) + rows.shape[1:], rows.dtype)
    out[0:rows.shape[0]] = rows
    out[HALF:HALF + rows.shape[0]] = rows
    return out


def layout(inputs):
    g = {k: np.asarray(v) for k, v in inputs.items()}
    f = np.float32
    x = g["x"]
    A = {}
    A["x_rows"] = x.reshape(B, PAIRS, 2, H, W).transpose(1, 2, 3, 0, 4).reshape(PAIRS, P, BW)
    A["x_cols"] = x.reshape(HB, 2, PAIRS, 2, H, W).transpose(2, 1, 5, 3, 0, 4).reshape(PAIRS, P, 2 * HB * H)
    L = {k[8:]: v for k, v in g.items() if k.startswith("L0_conv_")}
    table = np.zeros((TAPS, 2, COLS), f)
    for h in range(2):
        ay, ax = slice(0, PAIRS), slice(PAIRS, SETS)
        ey, ex = slice(SETS, SETS + PAIRS), slice(SETS + PAIRS, COLS)
        table[0:5, h, ay] = L["wh_m"][h::2].T
        table[5:10, h, ay] = L["wh_l"][h::2].T
        table[0:5, h, ax] = L["ww_m"].T
        table[5:10, h, ax] = L["ww_l"].T
        table[10, h, ay] = 2.0
        table[10, h, ey] = 1.0
        table[11:14, h, ey] = L["dg_wh"][h::2].T
        table[11:14, h, ex] = L["dg_ww"].T
    A["tap_table"] = table
    consts = np.zeros((TAPS, 2), f)
    consts[:, 0] = OFFSETS
    consts[:, 1] = 1.0
    consts[0:5, 1] = L["r_m"]
    consts[5:10, 1] = L["r_l"]
    A["tap_consts"] = consts
    wf = np.zeros((P, P), f)
    for lo in (0, HALF):
        wf[lo:lo + C, lo:lo + C] = L["w_fuse"].T
    A["w_fuse_T"] = wf
    A["mix_params"] = halves(np.stack([L[k] for k in ("bnf_g", "bnf_b", "bnf_m", "bnf_v", "dg_g", "dg_b", "dg_m", "dg_v", "act_a")], 1))
    w1 = np.zeros((C, HALF), f)
    w1[:, 0:8] = L["ca_w1"].T
    A["ca_w1_T"] = halves(w1)
    wg = np.zeros((8, 2, HALF), f)
    wg[:, 0, 0:C] = L["ca_wh"].T
    wg[:, 1, 0:C] = L["ca_ww"].T
    A["ca_wg_T"] = halves(wg)
    A["ca_params"] = halves(np.stack([L[k] for k in ("ca_g", "ca_b", "ca_m", "ca_v", "ca_a")], 1))
    for layer in ("l1", "l2"):
        Q = {k[8:]: v for k, v in g.items() if k.startswith(layer.upper() + "_conv_")}
        K = HALF + C
        w = np.zeros((K, 2, 2, 3, K), f)
        for d, (wd, bd, near, far) in enumerate(((Q["w_f"], Q["b_f"], 0, HALF), (Q["w_b"], Q["b_b"], HALF, 0))):
            mid = wd[:, :, 1, :].reshape(4, C, 2 * C, 3)
            for m, (a, b) in enumerate(((0, 1), (2, 3))):
                for gate, col in ((a, near), (b, far)):
                    w[near:near + C, d, m, :, col:col + C] = mid[gate, :, C:].transpose(1, 2, 0)
                    w[far:far + C, d, m, :, col:col + C] = mid[gate, :, :C].transpose(1, 2, 0)
                    w[C, d, m, 1, col:col + C] = bd.reshape(4, C)[gate]
        A[layer + "_w"] = w.reshape(K, -1)
        wp = np.zeros((K, HALF), f)
        wp[0:C, 0:C] = Q["w_proj"][:, 0:C].T
        wp[HALF:K, 0:C] = Q["w_proj"][:, C:].T
        A[layer + "_proj_T"] = wp
        A[layer + "_params"] = halves(np.stack([Q["gamma"], Q["beta"]], 1))
    Q = {k[8:]: v for k, v in g.items() if k.startswith("L3_conv_")}
    w1 = np.zeros((HALF + C, HID), f)
    w1[0:C] = w1[HALF:] = Q["w1"].T
    A["b_w1_T"] = w1
    A["b_wd"] = Q["wd"].reshape(GROUPS, GC, 9).transpose(1, 0, 2)
    w2 = np.zeros((GC, GROUPS, HALF), f)
    w2[:, :, 0:C] = Q["w2"].reshape(C, GROUPS, GC).transpose(2, 1, 0)
    A["b_w2_T"] = w2
    A["b_bn_hid"] = np.stack([np.stack([Q[p + n].reshape(GROUPS, GC).T for n in "1d"], 1) for p in "gbmv"], 1)
    A["b_bn_out"] = halves(np.stack([Q[p + "2"] for p in "gbmv"], 1))
    sd = np.zeros((P, 2, P), f)
    for p in range(P):
        sd[p, 0, p] = sd[p, 0, (p + HALF) % P] = 0.5
        sd[p, 1, p], sd[p, 1, (p + HALF) % P] = 0.5, -0.5
    A["sum_dif"] = sd
    return {k: np.ascontiguousarray(v) for k, v in A.items()}


STOP = 99


def kernel(**inputs):
    import concourse.bacc as bacc
    from concourse.bass_utils import run_bass_kernel_spmd

    nc = bacc.Bacc("TRN2", target_bir_lowering=False, num_devices=1)
    arrays = layout(inputs)
    D = {k: nc.dram_tensor("in_" + k, a.shape, mybir.dt.from_np(a.dtype), kind="ExternalInput").ap() for k, a in arrays.items()}
    out = nc.dram_tensor("out_rows", (H, C, B, W), F32, kind="ExternalOutput").ap()
    build(nc, D, out, STOP)
    r = run_bass_kernel_spmd(nc, [{"in_" + k: a for k, a in arrays.items()}], core_ids=[0])
    return np.ascontiguousarray(r.results[0]["out_rows"].transpose(2, 1, 0, 3))
```

```python
import concourse.bass as bass
from concourse import mybir
from contextlib import ExitStack
import numpy as np

F32 = mybir.dt.float32
F32R = mybir.dt.float32r
I32 = mybir.dt.int32
ALU = mybir.AluOpType
ACT = mybir.ActivationFunctionType
AX = mybir.AxisListType

B, C, H, W = 8, 48, 64, 64
P = 128
HALF = 64
HB = B // 2
PAIRS = C // 2
BW = B * W
WP = W + 2
ROW = B * WP
HID = 6 * C
GROUPS, GC = 3, HID // 3
EPS = 1e-5
BANKS = 8

K_AX, K_DG = 5, 3
TAPS = 2 * K_AX + 1 + K_DG
OFFSETS = [*range(-2, 3), *range(-2, 3), 0, -1, 0, 1]
SPAN = 2 * H - 1
SETS = PAIRS + C
COLS = 2 * SETS
PER_BANK = 3


def wait(eng, sem, value):
    if isinstance(value, int) and value <= 0:
        return
    eng.wait_ge(sem, value)


def release(nc, sems):
    nc.clear_and_free_semaphores(sems)
    nc.all_engine_barrier()


def held(eng, value):
    return value if isinstance(value, int) else eng.snap(value)


def peeled(eng, count, body):
    body(0)
    with eng.Fori(1, count) as k:
        body(k)


def axial_filters(nc, D, ctx_hs):
    ctx = ExitStack()
    with ctx:
        sems = []
        ctx.callback(release, nc, sems)

        def sb(name, shape, dt=F32):
            return ctx.enter_context(nc.sbuf_tensor(name, shape, dt))

        def sem(name):
            sems.append(nc.alloc_semaphore(name))
            return sems[-1]

        hs = ctx_hs
        taps = sb("taps", [TAPS, 2, COLS])
        tapc = sb("tapc", [TAPS, 2])
        shift = sb("shift", [TAPS, 1])
        radius = sb("radius", [TAPS, 1])
        disti = sb("disti", [TAPS, SPAN], I32)
        dist = sb("dist", [TAPS, 3, SPAN])
        hat = sb("hat", [TAPS, SPAN])
        filt = sb("filt", [P, COLS, H])
        fy = sb("fy", [P, 2, 2, P])
        fx = sb("fx", [P, 2, 2, 2, P])
        xr = sb("xr", [P, 2, BW])
        xc = sb("xc", [P, 2, 2, HB, H])
        stage = sb("stage", [P, 4, BW])
        ps = [ctx.enter_context(nc.psum_tensor(f"axps{i}", [P, BW], F32)) for i in range(BANKS)]

        loaded = sem("a_loaded")
        iota_done = sem("a_iota")
        hat_steps = sem("a_hat_steps")
        hat_ready = sem("a_hat_ready")
        built = sem("a_built")
        kept_a = sem("a_kept_act")
        kept_d = sem("a_kept_dve")
        x_in = [sem(f"a_x_in{s}") for s in range(2)]
        pair_copied = sem("a_pair_copied")
        filtered = sem("a_filtered")
        staged_a = sem("a_staged_act")
        staged_d = sem("a_staged_dve")
        stored = [sem(f"a_stored{s}") for s in range(4)]
        zeroed = sem("a_zeroed")

        groups = [list(range(i, min(i + PER_BANK, H))) for i in range(0, H, PER_BANK)]
        NG = len(groups)
        n_act, n_dve = (NG + 1) // 2, NG // 2

        with nc.Block() as block:
            @block.sync
            def _(sp):
                sp.dma_start(taps[:, :, :], D["tap_table"]).then_inc(loaded, 16)
                sp.dma_start(tapc[:, :], D["tap_consts"]).then_inc(loaded, 16)

                def load(pair, s):
                    sp.dma_start(xr[:, s, :], D["x_rows"][pair]).then_inc(x_in[s], 16)
                    sp.dma_start(xc[:, s], D["x_cols"][pair].rearrange("p (a b y) -> p a b y", a=2, b=HB)
                                 ).then_inc(x_in[s], 16)

                def step(k, last=False):
                    for s in range(2):
                        pair = held(sp, 2 * k + s)
                        ahead = held(sp, 2 * k + s + 2)
                        done = held(sp, 2 * k + s + 1)
                        sp.wait_ge(staged_a, done)
                        sp.wait_ge(staged_d, done)
                        sp.dma_start(D["mixed"][pair], stage[:, 2 * s, :]).then_inc(stored[2 * s], 16)
                        sp.dma_start(D["edged"][pair], stage[:, 2 * s + 1, :]).then_inc(stored[2 * s + 1], 16)
                        if not last:
                            load(ahead, s)
                for s in range(2):
                    load(s, s)
                with sp.Fori(0, PAIRS // 2 - 1) as k:
                    step(k)
                step(PAIRS // 2 - 1, last=True)
                for s in range(4):
                    sp.wait_ge(stored[s], 16 * (PAIRS // 2))

            @block.gpsimd
            def _(pool):
                pool.iota(disti[:, :], [[1, SPAN]], base=-(H - 1), channel_multiplier=0).then_inc(iota_done, 1)
                pool.memset(hs[32:64, :, :], 0.0).then_inc(zeroed, 1)

            @block.scalar
            def _(act):
                for n in range(0, NG, 2):
                    act.wait_ge(built, n + 1)
                    g = groups[n]
                    nc.scalar.activation(filt[:, :, g[0]:g[0] + len(g)],
                                         ps[n % BANKS][:, 0:COLS * len(g)].rearrange("p (i c) -> p c i", c=COLS),
                                         ACT.Copy).then_inc(kept_a, 1)

                def step(k):
                    for s in range(2):
                        act.wait_ge(filtered, 4 * k + 2 * s + 1)
                        wait(act, stored[2 * s], 16 * k)
                        nc.scalar.activation(stage[:, 2 * s, :], ps[2 * s][:, :], ACT.Copy).then_inc(staged_a, 1)
                peeled(act, PAIRS // 2, step)

            @block.vector
            def _(dve):
                nc.vector.memset(fy[:, :, :, :], 0.0).then_inc(hat_steps, 1)
                nc.vector.memset(fx[:, :, :, :, :], 0.0).then_inc(hat_steps, 1)
                dve.wait_ge(loaded, 32)
                dve.wait_ge(iota_done, 1)
                nc.vector.tensor_copy(dist[:, 0, :], disti[:, :]).then_inc(hat_steps, 1)
                nc.vector.tensor_scalar(radius[:, :], tapc[:, 1:2], 1.0, None, ALU.max).then_inc(hat_steps, 1)
                dve.wait_ge(hat_steps, 4)
                nc.vector.tensor_tensor(shift[:, :], radius[:, :], tapc[:, 0:1], ALU.mult).then_inc(hat_steps, 1)
                dve.wait_ge(hat_steps, 5)
                nc.vector.tensor_scalar(dist[:, 1, :], dist[:, 0, :], shift[:, 0:1], None, ALU.subtract).then_inc(hat_steps, 1)
                dve.wait_ge(hat_steps, 6)
                nc.vector.tensor_scalar(dist[:, 0, :], dist[:, 1, :], -1.0, 1.0, ALU.mult, ALU.add).then_inc(hat_steps, 1)
                nc.vector.tensor_scalar(dist[:, 2, :], dist[:, 1, :], 1.0, None, ALU.add).then_inc(hat_steps, 1)
                dve.wait_ge(hat_steps, 8)
                nc.vector.tensor_tensor(dist[:, 1, :], dist[:, 0, :], dist[:, 2, :], ALU.min).then_inc(hat_steps, 1)
                dve.wait_ge(hat_steps, 9)
                nc.vector.tensor_scalar(hat[:, :], dist[:, 1, :], 0.0, None, ALU.max).then_inc(hat_ready, 1)
                for n in range(1, NG, 2):
                    dve.wait_ge(built, n + 1)
                    g = groups[n]
                    nc.vector.tensor_copy(filt[:, :, g[0]:g[0] + len(g)],
                                          ps[n % BANKS][:, 0:COLS * len(g)].rearrange("p (i c) -> p c i", c=COLS)
                                          ).then_inc(kept_d, 1)
                dve.wait_ge(kept_a, n_act)
                dve.wait_ge(kept_d, n_dve)

                def copy_pair(pair, s):
                    for q in range(2):
                        for h in range(2):
                            lo = h * HALF
                            nc.vector.tensor_copy(fy[lo:lo + HALF, s, q, lo:lo + HALF].unsqueeze(1),
                                                  filt[lo:lo + HALF, bass.ds(pair + q * SETS, 1), :])
                            last = nc.vector.tensor_copy(fx[lo:lo + HALF, s, q, :, lo:lo + HALF],
                                                         filt[lo:lo + HALF, bass.ds(2 * pair + (q * SETS + PAIRS), 2), :])
                    last.then_inc(pair_copied, 1)

                def step(k):
                    for s in range(2):
                        wait(dve, filtered, 4 * k - 4 + 2 * s + 2)
                        copy_pair(2 * k + s, s)
                    for s in range(2):
                        dve.wait_ge(filtered, 4 * k + 2 * s + 2)
                        wait(dve, stored[2 * s + 1], 16 * k)
                        nc.vector.tensor_copy(stage[:, 2 * s + 1, :], ps[2 * s + 1][:, :]).then_inc(staged_d, 1)
                peeled(dve, PAIRS // 2, step)

            @block.tensor
            def _(pe):
                pe.wait_ge(loaded, 32)
                pe.wait_ge(hat_ready, 1)
                for n, g in enumerate(groups):
                    if n >= BANKS:
                        m = n - BANKS
                        pe.wait_ge(kept_d if m % 2 else kept_a, m // 2 + 1)
                    for r, i in enumerate(g):
                        for h in range(2):
                            mm = nc.tensor.matmul(ps[n % BANKS][h * HALF:(h + 1) * HALF, r * COLS:(r + 1) * COLS],
                                                  hat[:, H - 1 - i:2 * H - 1 - i], taps[:, h, :], start=(r == 0), stop=True,
                                                  skip_group_check=True)
                    mm.then_inc(built, 1)
                pe.wait_ge(kept_a, n_act)
                pe.wait_ge(kept_d, n_dve)

                def step(k):
                    for s in range(2):
                        wait(pe, x_in[s], 32 * k + 32)
                        wait(pe, pair_copied, 2 * k + s + 1)
                        for q in range(2):
                            bank = ps[2 * s + q]
                            wait(pe, staged_d if q else staged_a, 2 * k + s - 1)
                            nc.tensor.matmul(bank[:, :], fy[:, s, q, :], xr[:, s, :],
                                             start=True, stop=False, skip_group_check=True)
                            for b in range(HB):
                                for h in range(2):
                                    mm = nc.tensor.matmul(bank[h * HALF:(h + 1) * HALF, b * P:(b + 1) * P],
                                                          xc[:, s, h, b, :], fx[:, s, q, h, :],
                                                          start=False, stop=True, skip_group_check=True)
                            mm.then_inc(filtered, 1)
                peeled(pe, PAIRS // 2, step)



def mix_channels(nc, D, hs):
    ctx = ExitStack()
    UNIT = 4
    UC = UNIT * HB * W
    with ctx:
        sems = []
        ctx.callback(release, nc, sems)

        def sb(name, shape, dt=F32):
            return ctx.enter_context(nc.sbuf_tensor(name, shape, dt))

        def sem(name):
            sems.append(nc.alloc_semaphore(name))
            return sems[-1]

        kept = hs[:, 0:H // 2, :].rearrange("p a n -> p (a n)").rearrange("p (u n) -> p u n", n=UC)
        mixed = sb("mixed_sb", [P, 2, UC])
        edged = sb("edged_sb", [P, 2, UC])
        scaled = sb("scaled", [P, 2, UC])
        total = sb("total", [P, 2, UC])
        minus = sb("minus", [P, 2, UC])
        wf = sb("wf", [P, P])
        par = sb("par", [P, 9])
        half_power = sb("half_power", [P, 2])
        var = sb("var", [P, 2])
        rs = sb("rs", [P, 2])
        scale = sb("scale", [P, 2])
        shift = sb("shift_bn", [P, 4])
        slope = sb("slope", [P, 1])
        ps = [ctx.enter_context(nc.psum_tensor(f"mxps{i}", [P, BW], F32)) for i in range(4)]

        loaded = sem("m_loaded")
        steps = sem("m_steps")
        consts = sem("m_consts")
        x_in = [sem(f"m_x_in{s}") for s in range(2)]
        zeroed = sem("m_zeroed")
        multiplied = sem("m_multiplied")
        affine = sem("m_affine")
        added = sem("m_added")
        negs = sem("m_negs")
        done = sem("m_done")

        with nc.Block() as block:
            @block.sync
            def _(sp):
                sp.dma_start(wf[:, :], D["w_fuse_T"]).then_inc(loaded, 16)
                sp.dma_start(par[:, :], D["mix_params"]).then_inc(loaded, 16)
                sp.wait_ge(zeroed, 2)

                def load(u, s):
                    for q, tile in (("mixed", mixed), ("edged", edged)):
                        src = D[q].rearrange("k (a y) (h n) -> k a y h n", a=2, h=2)
                        src = D[q + "_c"]
                        for h in range(2):
                            sp.dma_start(tile[h * HALF:h * HALF + C, s, :].rearrange("p (y n) -> p y n", y=UNIT),
                                         src[:, u, :, h, :]).then_inc(x_in[s], 16)

                def step(k):
                    for s in range(2):
                        u = held(sp, 2 * k + s)
                        used = held(sp, 2 * k + s - 1)
                        wait(sp, done, used)
                        load(u, s)
                peeled(sp, H // UNIT // 2, step)

            @block.gpsimd
            def _(pool):
                pool.memset(edged[:, :, :], 0.0).then_inc(zeroed, 1)
                pool.memset(mixed[:, :, :], 0.0).then_inc(zeroed, 1)
                pool.memset(half_power[:, :], -0.5).then_inc(steps, 1)
                pool.wait_ge(loaded, 32)
                pool.tensor_scalar(var[:, :], par[:, 3:8:4], EPS, 0.0, ALU.add, ALU.add).then_inc(steps, 1)
                pool.wait_ge(steps, 2)
                pool.tensor_tensor(rs[:, :], var[:, :], half_power[:, :], ALU.pow).then_inc(steps, 1)
                pool.wait_ge(steps, 3)
                pool.tensor_tensor(scale[:, :], rs[:, :], par[:, 0:5:4], ALU.mult).then_inc(steps, 1)
                pool.wait_ge(steps, 4)
                pool.tensor_tensor(shift[:, 0:2], par[:, 2:7:4], scale[:, :], ALU.mult).then_inc(steps, 1)
                pool.wait_ge(steps, 5)
                pool.tensor_tensor(shift[:, 2:4], par[:, 1:6:4], shift[:, 0:2], ALU.subtract).then_inc(steps, 1)
                pool.wait_ge(steps, 6)
                pool.tensor_tensor(shift[:, 0:1], shift[:, 2:3], shift[:, 3:4], ALU.add).then_inc(consts, 1)
                pool.tensor_scalar(slope[:, :], par[:, 8:9], -1.0, 0.0, ALU.add, ALU.add).then_inc(consts, 1)

            @block.tensor
            def _(pe):
                pe.wait_ge(loaded, 32)

                def step(k):
                    for s in range(2):
                        wait(pe, x_in[s], 64 * k + 64)
                        wait(pe, affine, 4 * k + 2 * s - 2)
                        for j in range(2):
                            nc.tensor.matmul(ps[2 * s + j][:, :], wf[0:HALF + C, :],
                                             mixed[0:HALF + C, s, j * BW:(j + 1) * BW],
                                             start=True, stop=True).then_inc(multiplied, 1)
                peeled(pe, H // UNIT // 2, step)

            @block.scalar
            def _(act):
                act.wait_ge(consts, 2)

                def step(k):
                    for s in range(2):
                        wait(act, done, 2 * k + s - 1)
                        for j in range(2):
                            act.wait_ge(multiplied, 4 * k + 2 * s + j + 1)
                            nc.scalar.activation(scaled[:, s, j * BW:(j + 1) * BW], ps[2 * s + j][:, :], ACT.Identity,
                                                 bias=shift[:, 0:1], scale=scale[:, 0:1]).then_inc(affine, 1)
                peeled(act, H // UNIT // 2, step)

            @block.vector
            def _(dve):
                dve.wait_ge(consts, 2)
                dve.wait_ge(zeroed, 2)

                def step(k):
                    for s in range(2):
                        dve.wait_ge(affine, 4 * k + 2 * s + 2)
                        dve.wait_ge(x_in[s], 64 * k + 64)
                        nc.vector.scalar_tensor_tensor(total[:, s, :], edged[:, s, :], scale[:, 1:2], scaled[:, s, :],
                                                       ALU.mult, ALU.add).then_inc(added, 1)
                        dve.wait_ge(added, 2 * k + s + 1)
                        nc.vector.tensor_scalar(minus[:, s, :], total[:, s, :], 0.0, slope[:, 0:1], ALU.min, ALU.mult
                                                ).then_inc(negs, 1)
                        dve.wait_ge(negs, 2 * k + s + 1)
                        nc.vector.tensor_tensor(kept[:, bass.ds(2 * k + s, 1), :].rearrange("p a n -> p (a n)"),
                                                minus[:, s, :], total[:, s, :], ALU.add).then_inc(done, 1)
                peeled(dve, H // UNIT // 2, step)


def coordinate_attention(nc, D, hs, out_rows):
    ctx = ExitStack()
    UNIT = 4
    with ctx:
        sems = []
        ctx.callback(release, nc, sems)

        def sb(name, shape, dt=F32):
            return ctx.enter_context(nc.sbuf_tensor(name, shape, dt))

        def sem(name):
            sems.append(nc.alloc_semaphore(name))
            return sems[-1]

        kept = hs[:, 0:H // 2, :].rearrange("p a n -> p (a n)").rearrange("p (y b w) -> p y b w", b=HB, w=W)
        means = sb("means", [P, 2, H * HB])
        w1 = sb("ca_w1", [P, HALF])
        wg = sb("ca_wg", [P, 2, HALF])
        par = sb("ca_par", [P, 5])
        power = sb("ca_power", [P, 1])
        tmp = sb("ca_tmp", [P, 4])
        cs = sb("ca_cs", [P, 3])
        z = sb("ca_z", [P, 3, BW])
        gate = sb("ca_gate", [P, 2, H * HB])
        xa = sb("ca_xa", [P, 2, UNIT, HB * W])
        xg = sb("ca_xg", [P, 2, UNIT, HB * W])
        ps = [ctx.enter_context(nc.psum_tensor(f"caps{i}", [P, BW], F32)) for i in range(2)]

        loaded = sem("c_loaded")
        steps = sem("c_steps")
        consts = sem("c_consts")
        summed = sem("c_summed")
        squeezed = sem("c_squeezed")
        normed = sem("c_normed")
        zneg = sem("c_zneg")
        zdone = sem("c_zdone")
        widened = sem("c_widened")
        gated = sem("c_gated")
        times_w = sem("c_times_w")
        times_h = sem("c_times_h")
        stored = [sem(f"c_stored{s}") for s in range(2)]

        with nc.Block() as block:
            @block.sync
            def _(sp):
                sp.dma_start(w1[:, :], D["ca_w1_T"]).then_inc(loaded, 16)
                sp.dma_start(wg[:, :, :], D["ca_wg_T"]).then_inc(loaded, 16)
                sp.dma_start(par[:, :], D["ca_params"]).then_inc(loaded, 16)

                def step(k):
                    for s in range(2):
                        u = held(sp, 2 * k + s)
                        ready = held(sp, 2 * k + s + 1)
                        sp.wait_ge(times_h, ready)
                        for h in range(2):
                            sp.dma_start(out_rows[u, :, :, h, :], xg[h * HALF:h * HALF + C, s]).then_inc(stored[s], 16)
                peeled(sp, H // UNIT // 2, step)
                for s in range(2):
                    sp.wait_ge(stored[s], 32 * (H // UNIT // 2))

            @block.gpsimd
            def _(pool):
                pool.memset(power[:, :], -0.5).then_inc(steps, 1)
                pool.wait_ge(loaded, 48)
                pool.tensor_scalar(tmp[:, 0:1], par[:, 3:4], EPS, 0.0, ALU.add, ALU.add).then_inc(steps, 1)
                pool.wait_ge(steps, 2)
                pool.tensor_tensor(tmp[:, 1:2], tmp[:, 0:1], power[:, :], ALU.pow).then_inc(steps, 1)
                pool.wait_ge(steps, 3)
                pool.tensor_tensor(tmp[:, 2:3], tmp[:, 1:2], par[:, 0:1], ALU.mult).then_inc(steps, 1)
                pool.wait_ge(steps, 4)
                pool.tensor_tensor(tmp[:, 3:4], par[:, 2:3], tmp[:, 2:3], ALU.mult).then_inc(steps, 1)
                pool.tensor_scalar(cs[:, 0:1], tmp[:, 2:3], 1.0 / W, 0.0, ALU.mult, ALU.add).then_inc(consts, 1)
                pool.wait_ge(steps, 5)
                pool.tensor_tensor(cs[:, 1:2], par[:, 1:2], tmp[:, 3:4], ALU.subtract).then_inc(consts, 1)
                pool.tensor_scalar(cs[:, 2:3], par[:, 4:5], -1.0, 0.0, ALU.add, ALU.add).then_inc(consts, 1)

            @block.tensor
            def _(pe):
                pe.wait_ge(loaded, 48)
                pe.wait_ge(summed, 2)
                for h in range(2):
                    lo = h * HALF
                    mm = nc.tensor.matmul(ps[0][lo:lo + HALF, :], w1[lo:lo + C, :],
                                          means[lo:lo + C, :, :].rearrange("p a n -> p (a n)"), start=True, stop=True)
                mm.then_inc(squeezed, 1)
                pe.wait_ge(zdone, 1)
                for a in range(2):
                    for h in range(2):
                        lo = h * HALF
                        mm = nc.tensor.matmul(ps[1][lo:lo + HALF, a * H * HB:(a + 1) * H * HB],
                                              wg[lo:lo + HALF, a, :], z[lo:lo + HALF, 2, a * H * HB:(a + 1) * H * HB],
                                              start=(a == 0), stop=True, skip_group_check=True)
                mm.then_inc(widened, 1)

            @block.scalar
            def _(act):
                act.wait_ge(consts, 3)
                act.wait_ge(squeezed, 1)
                nc.scalar.activation(z[:, 0, :], ps[0][:, :], ACT.Identity, bias=cs[:, 1:2], scale=cs[:, 0:1]).then_inc(normed, 1)
                act.wait_ge(widened, 1)
                nc.scalar.activation(gate[:, :, :], ps[1][:, :].rearrange("p (a n) -> p a n", a=2), ACT.Sigmoid).then_inc(gated, 1)

            @block.vector
            def _(dve):
                nc.vector.tensor_reduce(means[:, 0, :].rearrange("p (y b) -> p y b", b=HB), kept, AX.X, ALU.add).then_inc(summed, 1)
                nc.vector.tensor_reduce(means[:, 1, :].rearrange("p (b w) -> p b w", b=HB),
                                        kept.rearrange("p y b w -> p b w y"), AX.X, ALU.add).then_inc(summed, 1)
                dve.wait_ge(normed, 1)
                nc.vector.tensor_scalar(z[:, 1, :], z[:, 0, :], 0.0, cs[:, 2:3], ALU.min, ALU.mult).then_inc(zneg, 1)
                dve.wait_ge(zneg, 1)
                nc.vector.tensor_tensor(z[:, 2, :], z[:, 0, :], z[:, 1, :], ALU.add).then_inc(zdone, 1)
                dve.wait_ge(gated, 1)
                a_h = gate[:, 0, :].rearrange("p (u y b) -> p u (y b)", b=HB, y=UNIT)
                a_w = gate[:, 1, :]
                flat = hs[:, 0:H // 2, :].rearrange("p a n -> p (a n)").rearrange("p (u y n) -> p u y n", y=UNIT, n=HB * W)

                def step(k):
                    for s in range(2):
                        u = dve.snap(2 * k + s) if not isinstance(k, int) else 2 * k + s
                        nc.vector.tensor_tensor(xa[:, s], flat[:, bass.ds(u, 1)].rearrange("p a y n -> p (a y) n"),
                                                a_w.unsqueeze(1).broadcast_to([P, UNIT, HB * W]), ALU.mult).then_inc(times_w, 1)
                        dve.wait_ge(times_w, 2 * k + s + 1)
                        wait(dve, stored[s], 32 * k)
                        nc.vector.tensor_tensor(xg[:, s].rearrange("p y (b w) -> p (y b) w", b=HB),
                                                xa[:, s].rearrange("p y (b w) -> p (y b) w", b=HB),
                                                a_h[:, bass.ds(u, 1), :].rearrange("p a n -> p (a n)").unsqueeze(2).broadcast_to([P, UNIT * HB, W]),
                                                ALU.mult).then_inc(times_h, 1)
                peeled(dve, H // UNIT // 2, step)


def lstm_scans(nc, D, hs, rows_in, weights, tag):
    ctx = ExitStack()
    near, far = (0, HALF), (HALF, 0)
    K = HALF + C
    parts = [slice(j * HB * W, (j + 1) * HB * W) for j in range(2)]
    with ctx:
        sems = []
        ctx.callback(release, nc, sems)

        def sb(name, shape, dt=F32):
            return ctx.enter_context(nc.sbuf_tensor(name + tag, shape, dt))

        def sem(name):
            sems.append(nc.alloc_semaphore(name + tag))
            return sems[-1]

        NW = 2 * 2 * 3 * K
        w = sb("w", [K, NW])
        w_hi = sb("w_hi", [K, 2, 2, 3, K], F32R)
        w_lo = sb("w_lo", [K, 2, 2, 3, K], F32R)
        xf = sb("xf", [P, 2, BW])
        xh = sb("xh", [P, 2, 2, 2, B, WP], F32R)
        gate_if = sb("gate_if", [P, 2, BW])
        gate_g = sb("gate_g", [P, 2, BW])
        keep = sb("keep", [P, 2, BW])
        add = sb("add", [P, 2, BW])
        cell = sb("cell", [P, 2, BW])
        tanh_c = sb("tanh_c", [P, 2, BW])
        ps = [[ctx.enter_context(nc.psum_tensor(f"gates{d}{m}" + tag, [P, BW], F32)) for m in range(2)] for d in range(2)]

        w_loaded = sem("w_loaded")
        w_split = sem("w_split")
        cleared = sem("cleared")
        x_in = [[sem(f"x_in{d}{s}") for s in range(2)] for d in range(2)]
        x_hi = [sem(f"x_hi{d}") for d in range(2)]
        x_lo = [sem(f"x_lo{d}") for d in range(2)]
        gates = [[sem(f"gates_if{d}"), sem(f"gates_go{d}")] for d in range(2)]
        sig_if = [sem(f"sig_if{d}") for d in range(2)]
        tanh_g = [sem(f"tanh_g{d}") for d in range(2)]
        tanhs = [sem(f"tanhs{d}") for d in range(2)]
        kept = [sem(f"kept{d}") for d in range(2)]
        added = [sem(f"added{d}") for d in range(2)]
        cells = [sem(f"cells{d}") for d in range(2)]
        h_hi = [sem(f"h_hi{d}") for d in range(2)]
        h_full = [sem(f"h_full{d}") for d in range(2)]
        h_lo = [sem(f"h_lo{d}") for d in range(2)]

        with nc.Block() as block:
            @block.sync
            def _(sp):
                sp.dma_start(w[:, :], D[weights]).then_inc(w_loaded, 16)

                def load(row, d, s):
                    sp.dma_start(xf[far[d]:far[d] + C, s, :], rows_in[row]).then_inc(x_in[d][s], 16)
                for s in range(2):
                    load(s, 0, s)
                    load(H - 1 - s, 1, s)
                with sp.Fori(0, H // 2 - 1) as k:
                    for s in range(2):
                        row_f = sp.snap(2 * k + s + 2)
                        row_b = sp.snap(k * -2 + (H - 3 - s))
                        done = sp.snap(2 * k + s + 1)
                        sp.wait_ge(x_lo[0], done)
                        load(row_f, 0, s)
                        sp.wait_ge(x_lo[1], done)
                        load(row_b, 1, s)

            @block.gpsimd
            def _(pool):
                pool.memset(xh[:, :, :, :, :, :].bitcast(F32), 0.0).then_inc(cleared, 1)
                pool.wait_ge(cleared, 1)
                pool.memset(xh[32:64, :, :, 0].bitcast(F32), 1.0).then_inc(cleared, 1)
                pool.wait_ge(cleared, 2)
                pool.memset(xh[32:C, :, :, 0].bitcast(F32), 0.0).then_inc(cleared, 1)

                def step(k, last=False):
                    for s in range(2):
                        for d in range(2):
                            if d:
                                state_lo(2 * k + s, 2 * k + s, 0, s)
                            elif s:
                                state_lo(2 * k, k * -2 + (H - 1), 1, 0)
                            elif not (isinstance(k, int) and k == 0):
                                state_lo(2 * k - 1, k * -2 + H, 1, 1)
                            if not last:
                                split_lo(2 * k + s + 2, d, s)

                def state_lo(t, row, d, s):
                    n = near[d]
                    pool.wait_ge(h_full[d], t + 1)
                    pool.wait_ge(h_hi[d], t + 2)
                    whole = hs[n:n + C, bass.ds(row, 1), :].rearrange("p a (b w) -> p (a b) w", b=B)
                    pool.tensor_tensor(xh[n:n + C, d, 1 - s, 1, :, 1:W + 1], whole,
                                       xh[n:n + C, d, 1 - s, 0, :, 1:W + 1].bitcast(F32), ALU.subtract).then_inc(h_lo[d], 1)
                def split_lo(t, d, s):
                    pool.wait_ge(x_hi[d], t + 1)
                    pool.tensor_tensor(xh[far[d]:far[d] + C, d, s, 1, :, 1:W + 1],
                                       xf[far[d]:far[d] + C, s, :].rearrange("p (b w) -> p b w", b=B),
                                       xh[far[d]:far[d] + C, d, s, 0, :, 1:W + 1].bitcast(F32),
                                       ALU.subtract).then_inc(x_lo[d], 1)
                for s in range(2):
                    for d in range(2):
                        split_lo(s, d, s)
                step(0)
                with pool.Fori(1, H // 2 - 1) as k:
                    step(k)
                step(H // 2 - 1, last=True)

            @block.tensor
            def _(pe):
                pe.wait_ge(w_split, 2)
                with pe.Fori(0, H // 2) as k:
                    for s in range(2):
                        for d in range(2):
                            pe.wait_ge(x_lo[d], 2 * k + s + 1)
                            pe.wait_ge(h_hi[d], 2 * k + s + 1)

                            def taps(m, weight, part, first, last):
                                for t in range(3):
                                    mm = nc.tensor.matmul(ps[d][m][0:K, :], weight[:, d, m, t, :],
                                                          xh[0:K, d, s, part, :, t:t + W],
                                                          start=(first and t == 0), stop=(last and t == 2))
                                return mm
                            for m in range(2):
                                taps(m, w_hi, 0, True, False)
                                taps(m, w_lo, 0, False, False)
                            pe.wait_ge(h_lo[d], 2 * k + s + 1)
                            for m in range(2):
                                taps(m, w_hi, 1, False, True).then_inc(gates[d][m], 1)

            @block.scalar
            def _(act):
                act.wait_ge(cleared, 3)

                def split_hi(k, d, s):
                    act.wait_ge(x_in[d][s], 16 * k + 16)
                    nc.scalar.activation(xh[far[d]:far[d] + C, d, s, 0, :, 1:W + 1],
                                         xf[far[d]:far[d] + C, s, :].rearrange("p (b w) -> p b w", b=B),
                                         ACT.Copy).then_inc(x_hi[d], 1)
                for s in range(2):
                    for d in range(2):
                        split_hi(0, d, s)

                def step(k, last=False):
                    for s in range(2):
                        for d in range(2):
                            n, f = near[d], far[d]
                            act.wait_ge(gates[d][0], 2 * k + s + 1)
                            nc.scalar.activation(gate_if[0:K, d, :], ps[d][0][0:K, :], ACT.Sigmoid).then_inc(sig_if[d], 1)
                            act.wait_ge(gates[d][1], 2 * k + s + 1)
                            nc.scalar.activation(gate_g[n:n + C, d, :], ps[d][1][n:n + C, :], ACT.Tanh).then_inc(tanh_g[d], 1)
                            nc.scalar.activation(gate_g[f:f + C, d, :], ps[d][1][f:f + C, :], ACT.Sigmoid).then_inc(tanh_g[d], 1)
                            if not last:
                                split_hi(k + 1, d, s)
                            for j, part in enumerate(parts):
                                act.wait_ge(cells[d], 4 * k + 2 * s + (j + 3))
                                nc.scalar.activation(tanh_c[f:f + C, d, part], cell[f:f + C, d, part],
                                                     ACT.Tanh).then_inc(tanhs[d], 1)
                with act.Fori(0, H // 2 - 1) as k:
                    step(k)
                step(H // 2 - 1, last=True)

            @block.vector
            def _(dve):
                for d in range(2):
                    for part in parts:
                        nc.vector.memset(cell[:, d, part], 0.0).then_inc(cells[d], 1)
                dve.wait_ge(w_loaded, 16)
                flat_hi = w_hi[:, :, :, :, :].rearrange("p a b c n -> p (a b c n)")
                flat_lo = w_lo[:, :, :, :, :].rearrange("p a b c n -> p (a b c n)")
                nc.vector.tensor_copy(flat_hi, w[:, :]).then_inc(w_split, 1)
                dve.wait_ge(w_split, 1)
                nc.vector.tensor_tensor(flat_lo, w[:, :], flat_hi.bitcast(F32), ALU.subtract).then_inc(w_split, 1)
                dve.wait_ge(cleared, 3)
                for d in range(2):
                    nc.vector.memset(keep[:, d, :], 0.0).then_inc(h_hi[d], 1)
                    nc.vector.memset(add[:, d, :], 0.0).then_inc(h_lo[d], 1)

                def step(k, last=False):
                    for s in range(2):
                        for d in range(2):
                            n, f = near[d], far[d]
                            dve.wait_ge(cells[d], 4 * k + 2 * s + 2)
                            dve.wait_ge(sig_if[d], 2 * k + s + 1)
                            nc.vector.tensor_tensor(keep[n:n + C, d, :], gate_if[f:f + C, d, :], cell[f:f + C, d, :],
                                                    ALU.mult).then_inc(kept[d], 1)
                            dve.wait_ge(tanh_g[d], 4 * k + 2 * s + 1)
                            nc.vector.tensor_tensor(add[n:n + C, d, :], gate_if[n:n + C, d, :], gate_g[n:n + C, d, :],
                                                    ALU.mult).then_inc(added[d], 1)
                            dve.wait_ge(kept[d], 2 * k + s + 1)
                            dve.wait_ge(added[d], 2 * k + s + 1)
                            for part in parts:
                                nc.vector.tensor_tensor(cell[f:f + C, d, part], keep[n:n + C, d, part],
                                                        add[n:n + C, d, part], ALU.add).then_inc(cells[d], 1)
                            for j, part in enumerate(parts):
                                dve.wait_ge(tanhs[d], 4 * k + 2 * s + (j + 1))
                                hi = nc.vector.tensor_tensor(xh[n:n + C, d, 1 - s, 0, j * HB:(j + 1) * HB, 1:W + 1],
                                                             gate_g[f:f + C, d, part].rearrange("p (b w) -> p b w", b=HB),
                                                             tanh_c[f:f + C, d, part].rearrange("p (b w) -> p b w", b=HB),
                                                             ALU.mult)
                            hi.then_inc(h_hi[d], 1)
                            row = 2 * k + s if d == 0 else k * -2 + (H - 1 - s)
                            whole = hs[n:n + C, bass.ds(row, 1), :].rearrange("p a n -> p (a n)")
                            nc.vector.tensor_tensor(whole, gate_g[f:f + C, d, :], tanh_c[f:f + C, d, :],
                                                    ALU.mult).then_inc(h_full[d], 1)
                with dve.Fori(0, H // 2 - 1) as k:
                    step(k)
                step(H // 2 - 1, last=True)


def project_and_norm(nc, D, hs, rows_in, rows_out, weights, params, tag):
    ctx = ExitStack()
    K = HALF + C
    HH = H // 2
    NR = 4
    with ctx:
        sems = []
        ctx.callback(release, nc, sems)

        def sb(name, shape, dt=F32):
            return ctx.enter_context(nc.sbuf_tensor(name + tag, shape, dt))

        def sem(name):
            sems.append(nc.alloc_semaphore(name + tag))
            return sems[-1]

        w = sb("pw", [K, HALF])
        par = sb("ppar", [P, 2])
        sumdif = sb("sumdif", [P, 2, P])
        stats = sb("stats", [P, HH, 6])
        mv = sb("mv", [P, 2])
        tot = sb("tot", [P, 4])
        tmp = sb("ptmp", [P, 6])
        cs = sb("pcs", [P, 2])
        res = sb("res", [P, NR, BW])
        act_out = sb("act_out", [P, NR, BW])
        val = sb("val", [P, NR, BW])
        ps = [ctx.enter_context(nc.psum_tensor(f"pps{i}" + tag, [P, BW], F32)) for i in range(BANKS - 1)]
        ps_stat = ctx.enter_context(nc.psum_tensor("ps_stat" + tag, [P, BW], F32))
        NB = BANKS - 1

        loaded = sem("p_loaded")
        cleared = sem("p_cleared")
        projected = sem("projected")
        kept = sem("y_kept")
        counted = sem("counted")
        aggregated = sem("aggregated")
        shared = sem("shared")
        steps = sem("p_steps")
        consts = sem("p_consts")
        r_in = [sem(f"r_in{s}") for s in range(NR)]
        normed = sem("p_normed")
        valued = sem("valued")
        stored = [sem(f"p_stored{s}") for s in range(NR)]

        with nc.Block() as block:
            @block.sync
            def _(sp):
                sp.dma_start(w[:, :], D[weights]).then_inc(loaded, 16)
                sp.dma_start(par[:, :], D[params]).then_inc(loaded, 16)
                sp.dma_start(sumdif[:, :, :], D["sum_dif"]).then_inc(loaded, 16)
                sp.wait_ge(cleared, 2)

                def load(y, y2, s):
                    for h, row in enumerate((y, y2)):
                        sp.dma_start(res[h * HALF:h * HALF + C, s, :], rows_in[row]).then_inc(r_in[s], 16)

                def store(y, y2, s):
                    for h, row in enumerate((y, y2)):
                        sp.dma_start(rows_out[row], val[h * HALF:h * HALF + C, s, :]).then_inc(stored[s], 16)
                for s in range(NR):
                    load(s, s + HH, s)

                def step(k, last=False):
                    for s in range(NR):
                        y, y2 = held(sp, k * NR + s), held(sp, k * NR + (s + HH))
                        a, a2 = held(sp, k * NR + (s + NR)), held(sp, k * NR + (s + NR + HH))
                        ready = held(sp, k * NR + (s + 1))
                        sp.wait_ge(valued, ready)
                        store(y, y2, s)
                        if not last:
                            load(a, a2, s)
                with sp.Fori(0, HH // NR - 1) as k:
                    step(k)
                step(HH // NR - 1, last=True)
                for s in range(NR):
                    sp.wait_ge(stored[s], 32 * (HH // NR))

            @block.gpsimd
            def _(pool):
                pool.memset(res[:, :, :], 0.0).then_inc(cleared, 1)
                pool.memset(tmp[:, 5:6], -0.5).then_inc(cleared, 1)
                pool.wait_ge(cleared, 2)
                pool.wait_ge(steps, 2)
                pool.tensor_tensor(tmp[:, 1:2], tmp[:, 0:1], tmp[:, 5:6], ALU.pow).then_inc(steps, 1)
                pool.wait_ge(steps, 3)
                pool.tensor_tensor(cs[:, 0:1], tmp[:, 1:2], par[:, 0:1], ALU.mult).then_inc(steps, 1)
                pool.wait_ge(steps, 4)
                pool.tensor_tensor(tmp[:, 2:3], tot[:, 0:1], cs[:, 0:1], ALU.mult).then_inc(steps, 1)
                pool.wait_ge(steps, 5)
                pool.tensor_tensor(cs[:, 1:2], par[:, 1:2], tmp[:, 2:3], ALU.subtract).then_inc(consts, 1)

            @block.tensor
            def _(pe):
                pe.wait_ge(loaded, 48)
                for y in range(HH):
                    if y >= NB:
                        pe.wait_ge(kept, y - NB + 1)
                    for h in range(2):
                        mm = nc.tensor.matmul(ps[y % NB][h * HALF:(h + 1) * HALF, :], w[:, :], hs[0:K, y + h * HH, :],
                                              start=True, stop=True)
                    mm.then_inc(projected, 1)
                pe.wait_ge(aggregated, 1)
                for a in range(2):
                    mm = nc.tensor.matmul(ps_stat[:, 2 * a:2 * a + 2], sumdif[:, a, :], mv[:, :],
                                          start=(a == 0), stop=True, skip_group_check=True)
                mm.then_inc(shared, 1)

            @block.scalar
            def _(act):
                for y in range(HH):
                    act.wait_ge(projected, y + 1)
                    nc.scalar.activation(hs[:, y, :], ps[y % NB][:, :], ACT.Copy).then_inc(kept, 1)
                act.wait_ge(consts, 1)

                def step(k):
                    for s in range(NR):
                        wait(act, valued, k * NR + (s - NR + 1))
                        nc.scalar.activation(act_out[:, s, :], hs[:, bass.ds(k * NR + s, 1), :].rearrange("p a n -> p (a n)"),
                                             ACT.Relu, bias=cs[:, 1:2], scale=cs[:, 0:1]).then_inc(normed, 1)
                peeled(act, HH // NR, step)

            @block.vector
            def _(dve):
                for y in range(HH):
                    dve.wait_ge(kept, y + 1)
                    nc.vector.bn_stats(stats[:, y, :], hs[:, y, :]).then_inc(counted, 1)
                dve.wait_ge(counted, HH)
                nc.vector.bn_aggr(mv[:, :], stats[:, :, :].rearrange("p a n -> p (a n)")).then_inc(aggregated, 1)
                dve.wait_ge(shared, 1)
                nc.vector.tensor_copy(tot[:, :], ps_stat[:, 0:4]).then_inc(shared, 1)
                dve.wait_ge(shared, 2)
                nc.vector.scalar_tensor_tensor(tmp[:, 3:4], tot[:, 2:3], tot[:, 2:3], tot[:, 1:2], ALU.mult, ALU.add).then_inc(steps, 1)
                dve.wait_ge(steps, 1)
                nc.vector.tensor_scalar(tmp[:, 0:1], tmp[:, 3:4], EPS, None, ALU.add).then_inc(steps, 1)

                def step(k):
                    for s in range(NR):
                        dve.wait_ge(normed, k * NR + (s + 1))
                        dve.wait_ge(r_in[s], 32 * k + 32)
                        wait(dve, stored[s], 32 * k)
                        nc.vector.tensor_tensor(val[:, s, :], act_out[:, s, :], res[:, s, :], ALU.add).then_inc(valued, 1)
                peeled(dve, HH // NR, step)


def inverted_residual(nc, D, rows_in, out):
    ctx = ExitStack()
    K = HALF + C
    NV = 7
    NT = B - NV
    RING = 4
    with ctx:
        sems = []
        ctx.callback(release, nc, sems)

        def sb(name, shape, dt=F32):
            return ctx.enter_context(nc.sbuf_tensor(name, shape, dt))

        def sem(name):
            sems.append(nc.alloc_semaphore(name))
            return sems[-1]

        w1 = sb("b_w1", [K, HID])
        w1_hi = sb("b_w1_hi", [K, HID], F32R)
        w1_lo = sb("b_w1_lo", [K, HID], F32R)
        wd = sb("b_wd", [GC, GROUPS, 9])
        w2 = sb("b_w2", [GC, GROUPS, HALF])
        bn_hid = sb("b_bn_hid", [GC, 4, 2, GROUPS])
        bn_out = sb("b_bn_out", [P, 4])
        eye = sb("b_eye", [GC, GC])
        diag = sb("b_diag", [GC, 2, 9, GC])
        diag_hi = sb("b_diag_hi", [GC, 2, 9, GC], F32R)
        diag_lo = sb("b_diag_lo", [GC, 2, 9, GC], F32R)
        cs = sb("b_cs", [GC, 2, 2, GROUPS])
        cso = sb("b_cso", [P, 2])
        tmp = sb("b_tmp", [P, 4, 2 * GROUPS])
        xs = sb("b_xs", [P, RING, BW])
        x3 = sb("b_x3", [P, RING, B, WP], F32R)
        hv0 = sb("b_hv0", [GC, RING, B, WP])
        hv1 = sb("b_hv1", [GC, RING, NV, WP])
        ht1 = sb("b_ht1", [GC, RING, 2, NT, WP], F32R)
        ht2 = sb("b_ht2", [GC, RING, 2, B, WP], F32R)
        full1 = sb("b_full1", [GC, 2, NT, W])
        full2 = sb("b_full2", [GC, 2, B, W])
        acc = sb("b_acc", [GC, 2, (B + NV) * W])
        h2 = sb("b_h2", [GC, RING, GROUPS, BW])
        res = sb("b_res", [P, 2, BW])
        scaled = sb("b_scaled", [P, 2, BW])
        o = sb("b_o", [P, 2, BW])
        ps1 = [ctx.enter_context(nc.psum_tensor(f"b_ps1{i}", [P, BW], F32)) for i in range(GROUPS)]
        ps2 = [ctx.enter_context(nc.psum_tensor(f"b_ps2{i}", [P, BW], F32)) for i in range(2)]
        ps3 = [ctx.enter_context(nc.psum_tensor(f"b_ps3{i}", [P, BW], F32)) for i in range(2)]

        loaded = sem("b_loaded")
        cleared = sem("b_cleared")
        steps = sem("b_steps")
        consts = sem("b_consts")
        diags = sem("b_diags")
        w_split = sem("b_w_split")
        x_in = [sem(f"b_x_in{s}") for s in range(RING)]
        r_in = [sem(f"b_r_in{s}") for s in range(2)]
        expanded = sem("b_expanded")
        rows_v = sem("b_rows_v")
        rows_hi = sem("b_rows_hi")
        rows_full = sem("b_rows_full")
        rows_lo = sem("b_rows_lo")
        depth_t = sem("b_depth_t")
        taps_v = sem("b_taps_v")
        diag_steps = sem("b_diag_steps")
        squashed = sem("b_squashed")
        reduced = sem("b_reduced")
        affine = sem("b_affine")
        x_hi = sem("b_x_hi")
        x_lo = sem("b_x_lo")
        final = sem("b_final")
        stored = [sem(f"b_stored{s}") for s in range(2)]

        def slot(y):
            return y % RING

        with nc.Block() as block:
            @block.sync
            def _(sp):
                for tile, name in ((w1, "b_w1_T"), (wd, "b_wd"), (w2, "b_w2_T"), (bn_hid, "b_bn_hid"), (bn_out, "b_bn_out")):
                    ap = tile[tuple(slice(None) for _ in tile.shape)]
                    sp.dma_start(ap, D[name]).then_inc(loaded, 16)
                sp.wait_ge(cleared, 5)

                def load_x(row, s):
                    for part in range(2):
                        sp.dma_start(xs[part * HALF:part * HALF + C, s, :], rows_in[row]).then_inc(x_in[s], 16)

                def load_r(y, y1, s):
                    for h, row in enumerate((y, y1)):
                        sp.dma_start(res[h * HALF:h * HALF + C, s, :], rows_in[row]).then_inc(r_in[s], 16)

                for y in range(RING):
                    load_x(y, y)
                for s in range(2):
                    load_r(2 * s, 2 * s + 1, s)

                def store(y, y1, s):
                    for h, row in enumerate((y, y1)):
                        sp.dma_start(out[row].rearrange("c b w -> c (b w)"),
                                     o[h * HALF:h * HALF + C, s, :]).then_inc(stored[s], 16)

                def step(k, last=False):
                    for u in range(RING):
                        s = u // 2
                        ahead = held(sp, k * RING + (u + RING))
                        used = held(sp, k * RING + (u + 1))
                        done = held(sp, k * 2 + (s - 1))
                        y, y1 = held(sp, k * RING + (2 * s - 4)), held(sp, k * RING + (2 * s - 3))
                        r, r1 = held(sp, k * RING + 2 * s), held(sp, k * RING + (2 * s + 1))
                        if not last:
                            sp.wait_ge(x_lo, used)
                            load_x(ahead, u)
                        if u % 2 and not (isinstance(k, int) and k == 0):
                            sp.wait_ge(final, done)
                            store(y, y1, s)
                            load_r(r, r1, s)
                step(0)
                with sp.Fori(1, H // RING - 1) as k:
                    step(k)
                step(H // RING - 1, last=True)
                for s in range(2):
                    sp.wait_ge(final, H // 2 - 1 + s)
                    store(H - 4 + 2 * s, H - 3 + 2 * s, s)
                for s in range(2):
                    sp.wait_ge(stored[s], 32 * (H // RING))

            @block.gpsimd
            def _(pool):
                pool.memset(xs[:, :, :], 0.0).then_inc(cleared, 1)
                pool.memset(x3[:, :, :, :].bitcast(F32), 0.0).then_inc(cleared, 1)
                pool.memset(eye[:, :], 0.0).then_inc(cleared, 1)
                pool.wait_ge(cleared, 3)
                pool.affine_select(out=eye[:, :], in_=eye[:, :], compare_op=ALU.not_equal, fill=1.0, base=0,
                                   pattern=[[-1, GC]], channel_multiplier=1).then_inc(cleared, 1)
                pool.memset(tmp[:, 3, :], -0.5).then_inc(steps, 1)
                pool.memset(res[:, :, :], 0.0).then_inc(cleared, 1)
                for t in (hv0, hv1):
                    pool.memset(t[:, :, :, :], 0.0).then_inc(cleared, 1)
                for t in (ht1, ht2):
                    pool.memset(t[:, :, :, :, :].bitcast(F32), 0.0).then_inc(cleared, 1)
                pool.wait_ge(loaded, 80)
                pool.wait_ge(steps, 1)
                n = 2 * GROUPS

                def flat(i):
                    return bn_hid[:, i].rearrange("p a g -> p (a g)")
                pool.tensor_scalar(tmp[0:GC, 0, :], flat(3), EPS, 0.0, ALU.add, ALU.add).then_inc(steps, 1)
                pool.wait_ge(steps, 2)
                pool.tensor_tensor(tmp[0:GC, 1, :], tmp[0:GC, 0, :], tmp[0:GC, 3, :], ALU.pow).then_inc(steps, 1)
                pool.wait_ge(steps, 3)
                pool.tensor_tensor(cs[:, 0].rearrange("p a g -> p (a g)"), tmp[0:GC, 1, :], flat(0), ALU.mult).then_inc(steps, 1)
                pool.wait_ge(steps, 4)
                pool.tensor_tensor(tmp[0:GC, 2, :], flat(2), cs[:, 0].rearrange("p a g -> p (a g)"), ALU.mult).then_inc(steps, 1)
                pool.wait_ge(steps, 5)
                pool.tensor_tensor(cs[:, 1].rearrange("p a g -> p (a g)"), flat(1), tmp[0:GC, 2, :], ALU.subtract).then_inc(consts, 1)
                pool.tensor_scalar(tmp[:, 0, 0:1], bn_out[:, 3:4], EPS, 0.0, ALU.add, ALU.add).then_inc(steps, 1)
                pool.wait_ge(steps, 6)
                pool.tensor_tensor(tmp[:, 1, 0:1], tmp[:, 0, 0:1], tmp[:, 3, 0:1], ALU.pow).then_inc(steps, 1)
                pool.wait_ge(steps, 7)
                pool.tensor_tensor(cso[:, 0:1], tmp[:, 1, 0:1], bn_out[:, 0:1], ALU.mult).then_inc(steps, 1)
                pool.wait_ge(steps, 8)
                pool.tensor_tensor(tmp[:, 2, 0:1], bn_out[:, 2:3], cso[:, 0:1], ALU.mult).then_inc(steps, 1)
                pool.wait_ge(steps, 9)
                pool.tensor_tensor(cso[:, 1:2], bn_out[:, 1:2], tmp[:, 2, 0:1], ALU.subtract).then_inc(consts, 1)

                def low_parts(s, count, splits):
                    pool.wait_ge(x_lo, splits)
                    pool.wait_ge(rows_full, count)
                    for ht, full in ((ht1, full1), (ht2, full2)):
                        pool.tensor_tensor(ht[:, s, 1, :, 1:W + 1], full[:, s % 2], ht[:, s, 0, :, 1:W + 1].bitcast(F32),
                                           ALU.subtract).then_inc(rows_lo, 1)

                def split_lo(count, s, lows=0):
                    pool.wait_ge(x_hi, count)
                    wait(pool, rows_lo, lows)
                    half = slice(HALF, K)
                    pool.tensor_tensor(x3[half, s, :, 1:W + 1], xs[half, s, :].rearrange("p (b w) -> p b w", b=B),
                                       x3[half, s, :, 1:W + 1].bitcast(F32), ALU.subtract).then_inc(x_lo, 1)
                for r in range(RING):
                    split_lo(r + 1, r)
                for r in range(2):
                    low_parts(r, 2 * r + 2, RING)

                def step(k, last=False):
                    for u in range(RING):
                        if last and u == 2:
                            pool.wait_ge(depth_t, 2 * (H - 2))
                            pool.wait_ge(taps_v, 18 * (H - 2))
                            for t, done in ((hv0, rows_v), (hv1, rows_v)):
                                pool.memset(t[:, 0], 0.0).then_inc(done, 1)
                            for t in (ht1, ht2):
                                pool.memset(t[:, 0, 0].bitcast(F32), 0.0).then_inc(rows_hi, 1)
                                pool.memset(t[:, 0, 1].bitcast(F32), 0.0).then_inc(rows_lo, 1)
                        elif not last or u < 2:
                            low_parts((u + 2) % RING, 2 * RING * k + 2 * (u + 3), H if last else k * RING + (u + RING))
                        if not last:
                            split_lo(k * RING + (u + RING + 1), u, k * (2 * RING) + 2 * (u + 3))
                step(0)
                with pool.Fori(1, H // RING - 1) as k:
                    step(k)
                step(H // RING - 1, last=True)

            @block.tensor
            def _(pe):
                pe.wait_ge(w_split, 2)
                pe.wait_ge(cleared, 9)

                def expand(y, s):
                    pe.wait_ge(x_lo, y + 1)
                    wait(pe, rows_full, 2 * y)
                    for g in range(GROUPS):
                        for n, w in enumerate((w1_hi, w1_lo)):
                            mm = nc.tensor.matmul(ps1[g][0:GC, :], w[:, g * GC:(g + 1) * GC],
                                                  x3[0:K, s, :, 1:W + 1], start=(n == 0), stop=(n == 1))
                    mm.then_inc(expanded, 1)

                def depthwise(y, s):
                    pe.wait_ge(rows_hi, 2 * y + 4)
                    for g, ht in enumerate((ht1, ht2)):
                        n = ht.shape[3]
                        wait(pe, squashed, 4 * y + (g - 3))
                        for part, d in ((0, diag_hi), (0, diag_lo), (1, diag_hi)):
                            if part and g == 0:
                                pe.wait_ge(rows_lo, 2 * y + 4)
                            for t in range(9):
                                dy, dx = t // 3 - 1, t % 3
                                mm = nc.tensor.matmul(ps2[g][0:GC, 0:n * W], d[:, g, t, :],
                                                      ht[:, slot(s + dy), part, :, dx:dx + W],
                                                      start=(d is diag_hi and part == 0 and t == 0), stop=(part == 1 and t == 8))
                        mm.then_inc(depth_t, 1)

                def reduce_pair(j, s):
                    pe.wait_ge(squashed, j * 8 + 8)
                    wait(pe, affine, j - 1)
                    for g in range(GROUPS):
                        for h in range(2):
                            mm = nc.tensor.matmul(ps3[s][h * HALF:(h + 1) * HALF, :], w2[:, g, :],
                                                  h2[:, 2 * s + h, g, :], start=(g == 0), stop=(g == GROUPS - 1),
                                                  skip_group_check=True)
                    mm.then_inc(reduced, 1)
                for r in range(2):
                    expand(r, r)
                pe.wait_ge(diags, 2)

                def step(k, first=False, last=False):
                    for u in range(RING):
                        if not last or u < 2:
                            expand(k * RING + (u + 2), (u + 2) % RING)
                        depthwise(k * RING + u, u)
                        if u == 0 and not first:
                            reduce_pair(k * 2 - 1, 1)
                        if u == 2:
                            reduce_pair(k * 2, 0)
                step(0, first=True)
                with pe.Fori(1, H // RING - 1) as k:
                    step(k)
                step(H // RING - 1, last=True)
                reduce_pair(H // 2 - 1, 1)

            @block.scalar
            def _(act):
                act.wait_ge(consts, 2)
                act.wait_ge(cleared, 9)

                def hidden(y, s):
                    act.wait_ge(expanded, y + 1)
                    wait(act, depth_t, 2 * y - 4)
                    wait(act, taps_v, 18 * y - 36)
                    wait(act, rows_lo, 2 * y - 2)

                    def relu(dst, g, b0, b1, done):
                        nc.scalar.activation(dst, ps1[g][0:GC, b0 * W:b1 * W].rearrange("p (b w) -> p b w", w=W), ACT.Relu,
                                             bias=cs[:, 1, 0, g:g + 1], scale=cs[:, 0, 0, g:g + 1]).then_inc(done, 1)
                    relu(hv0[:, s, :, 1:W + 1], 0, 0, B, rows_v)
                    relu(hv1[:, s, :, 1:W + 1], 1, 0, NV, rows_v)
                    relu(ht1[:, s, 0, :, 1:W + 1], 1, NV, B, rows_hi)
                    relu(ht2[:, s, 0, :, 1:W + 1], 2, 0, B, rows_hi)
                    relu(full1[:, s % 2], 1, NV, B, rows_full)
                    relu(full2[:, s % 2], 2, 0, B, rows_full)

                def squash(y, s, rows_reduced):
                    def relu(dst, src, g):
                        nc.scalar.activation(dst, src, ACT.Relu, bias=cs[:, 1, 1, g:g + 1],
                                             scale=cs[:, 0, 1, g:g + 1]).then_inc(squashed, 1)
                    wait(act, reduced, rows_reduced)
                    act.wait_ge(depth_t, 2 * y + 2)
                    relu(h2[:, s, 1, NV * W:], ps2[0][0:GC, 0:NT * W], 1)
                    relu(h2[:, s, 2, :], ps2[1][0:GC, :], 2)
                    act.wait_ge(taps_v, 18 * y + 18)
                    relu(h2[:, s, 0, :], acc[:, s % 2, 0:BW], 0)
                    relu(h2[:, s, 1, 0:NV * W], acc[:, s % 2, BW:BW + NV * W], 1)

                def affine_rows(j, s):
                    act.wait_ge(reduced, j + 1)
                    wait(act, final, j - 1)
                    nc.scalar.activation(scaled[:, s, :], ps3[s][:, :], ACT.Identity, bias=cso[:, 1:2],
                                         scale=cso[:, 0:1]).then_inc(affine, 1)
                def split_hi(k, s):
                    act.wait_ge(x_in[s], 32 * k + 32)
                    wait(act, expanded, k * RING + (s - RING + 1))
                    nc.scalar.activation(x3[0:K, s, :, 1:W + 1], xs[0:K, s, :].rearrange("p (b w) -> p b w", b=B),
                                         ACT.Copy).then_inc(x_hi, 1)
                for r in range(RING):
                    split_hi(0, r)
                for r in range(2):
                    hidden(r, r)

                def step(k, first=False, last=False):
                    for u in range(RING):
                        if not last or u < 2:
                            hidden(k * RING + (u + 2), (u + 2) % RING)
                        if not last:
                            split_hi(k + 1, u)
                        squash(k * RING + u, u, k * 2 + (u // 2 - 1))
                        if u % 2 == 0 and not (first and u == 0):
                            affine_rows(k * 2 + (u // 2 - 1), (u // 2 - 1) % 2)
                step(0, first=True)
                with act.Fori(1, H // RING - 1) as k:
                    step(k)
                step(H // RING - 1, last=True)
                affine_rows(H // 2 - 1, 1)

            @block.vector
            def _(dve):
                dve.wait_ge(loaded, 80)
                nc.vector.tensor_copy(w1_hi[:, :], w1[:, :]).then_inc(w_split, 1)
                dve.wait_ge(w_split, 1)
                nc.vector.tensor_tensor(w1_lo[:, :], w1[:, :], w1_hi[:, :].bitcast(F32), ALU.subtract).then_inc(w_split, 1)
                dve.wait_ge(cleared, 9)
                for g in range(2):
                    for t in range(9):
                        last_one = nc.vector.tensor_scalar(diag[:, g, t, :], eye[:, :], wd[:, g + 1, t:t + 1], None, ALU.mult)
                        last_one.then_inc(diag_steps, 1)
                dve.wait_ge(diag_steps, 18)

                def flat(t):
                    return t[:, :, :, :].rearrange("p a b n -> p (a b n)")
                nc.vector.tensor_copy(flat(diag_hi), flat(diag)).then_inc(diags, 1)
                dve.wait_ge(diags, 1)
                nc.vector.tensor_tensor(flat(diag_lo), flat(diag), flat(diag_hi).bitcast(F32), ALU.subtract).then_inc(diags, 1)

                def depthwise(y, s):
                    dve.wait_ge(rows_v, 2 * y + 4)
                    wait(dve, squashed, 4 * y - 4)
                    parts = ((hv0, 0, 0, B), (hv1, 1, BW, NV))
                    for t in range(9):
                        dy, dx = t // 3 - 1, t % 3
                        for i, (hv, g, at, n) in enumerate(parts):
                            sums = acc[:, s % 2, at:at + n * W].rearrange("p (b w) -> p b w", w=W)
                            src = hv[:, slot(s + dy), :, dx:dx + W]
                            if t:
                                dve.wait_ge(taps_v, 18 * y + (2 * t - 1 + i))
                                nxt = nc.vector.scalar_tensor_tensor(sums, src, wd[:, g, t:t + 1], sums, ALU.mult, ALU.add)
                            else:
                                nxt = nc.vector.tensor_scalar(sums, src, wd[:, g, t:t + 1], None, ALU.mult)
                            nxt.then_inc(taps_v, 1)

                def finish(j, s, earlier):
                    dve.wait_ge(affine, j + 1)
                    dve.wait_ge(r_in[s], 32 * earlier + 32)
                    wait(dve, stored[s], 32 * earlier)
                    nc.vector.tensor_tensor(o[:, s, :], scaled[:, s, :], res[:, s, :], ALU.add).then_inc(final, 1)

                def step(k):
                    for u in range(RING):
                        depthwise(k * RING + u, u)
                        if u == 1 and not (isinstance(k, int) and k == 0):
                            finish(k * 2 - 1, 1, k - 1)
                        if u == 3:
                            finish(k * 2, 0, k)
                step(0)
                step(1)
                with dve.Fori(2, H // RING) as k:
                    step(k)
                finish(H // 2 - 1, 1, H // RING - 1)


def build(nc, D, out, stop=99):
    ctx = ExitStack()
    with ctx:
        hs_ctx = ctx.enter_context(ExitStack())
        hs = hs_ctx.enter_context(nc.sbuf_tensor("hs", [P, H, BW], F32))
        mixed = nc.dram_tensor("mixed", (PAIRS, P, BW), F32, kind="Internal").ap()
        edged = nc.dram_tensor("edged", (PAIRS, P, BW), F32, kind="Internal").ap()
        D = dict(D, mixed=mixed, edged=edged)
        for q in ("mixed", "edged"):
            D[q + "_c"] = D[q].rearrange("k (a u y) (h n) -> (k a) u y h n", a=2, y=4, h=2)
        rows = [nc.dram_tensor(f"rows{i}", (H, C, BW), F32, kind="Internal").ap() for i in range(3)]
        units = rows[0].rearrange("(u y) c (h n) -> u c y h n", y=4, h=2)
        axial_filters(nc, D, hs)
        if stop >= 2:
            mix_channels(nc, D, hs)
        if stop >= 3:
            coordinate_attention(nc, D, hs, units)
        for n, layer in enumerate(("l1", "l2")):
            if stop >= 4 + n:
                lstm_scans(nc, D, hs, rows[n], layer + "_w", "_" + layer)
                project_and_norm(nc, D, hs, rows[n], rows[n + 1], layer + "_proj_T", layer + "_params", "_" + layer)
        if stop == 99:
            hs_ctx.close()
            inverted_residual(nc, D, rows[2], out)
        if stop < 99:
            d = ctx.enter_context(nc.semaphore("dbg"))
            with nc.Block() as block:
                @block.sync
                def _(sp):
                    if stop == 1:
                        sp.dma_start(out.rearrange("a c b w -> (a c b w)"), mixed.rearrange("a b c -> (a b c)")).then_inc(d, 16)
                    if stop == 2:
                        of = out.rearrange("a c b w -> (a c b w)").rearrange("(c n) -> c n", c=2 * C)
                        for h in range(2):
                            sp.dma_start(of[h * C:(h + 1) * C], hs[h * HALF:h * HALF + C, 0:H // 2, :].rearrange("p a n -> p (a n)")).then_inc(d, 16)
                    if stop >= 3:
                        sp.dma_start(out.rearrange("y c b w -> y c (b w)"), rows[stop - 3]).then_inc(d, 16)
                    sp.wait_ge(d, 32 if stop == 2 else 16)


def halves(rows, n=HALF):
    rows = np.asarray(rows)
    out = np.zeros((P,) + rows.shape[1:], rows.dtype)
    out[0:rows.shape[0]] = rows
    out[HALF:HALF + rows.shape[0]] = rows
    return out


def layout(inputs):
    g = {k: np.asarray(v) for k, v in inputs.items()}
    f = np.float32
    x = g["x"]
    A = {}
    A["x_rows"] = x.reshape(B, PAIRS, 2, H, W).transpose(1, 2, 3, 0, 4).reshape(PAIRS, P, BW)
    A["x_cols"] = x.reshape(HB, 2, PAIRS, 2, H, W).transpose(2, 1, 5, 3, 0, 4).reshape(PAIRS, P, 2 * HB * H)
    L = {k[8:]: v for k, v in g.items() if k.startswith("L0_conv_")}
    table = np.zeros((TAPS, 2, COLS), f)
    for h in range(2):
        ay, ax = slice(0, PAIRS), slice(PAIRS, SETS)
        ey, ex = slice(SETS, SETS + PAIRS), slice(SETS + PAIRS, COLS)
        table[0:5, h, ay] = L["wh_m"][h::2].T
        table[5:10, h, ay] = L["wh_l"][h::2].T
        table[0:5, h, ax] = L["ww_m"].T
        table[5:10, h, ax] = L["ww_l"].T
        table[10, h, ay] = 2.0
        table[10, h, ey] = 1.0
        table[11:14, h, ey] = L["dg_wh"][h::2].T
        table[11:14, h, ex] = L["dg_ww"].T
    A["tap_table"] = table
    consts = np.zeros((TAPS, 2), f)
    consts[:, 0] = OFFSETS
    consts[:, 1] = 1.0
    consts[0:5, 1] = L["r_m"]
    consts[5:10, 1] = L["r_l"]
    A["tap_consts"] = consts
    wf = np.zeros((P, P), f)
    for lo in (0, HALF):
        wf[lo:lo + C, lo:lo + C] = L["w_fuse"].T
    A["w_fuse_T"] = wf
    A["mix_params"] = halves(np.stack([L[k] for k in ("bnf_g", "bnf_b", "bnf_m", "bnf_v", "dg_g", "dg_b", "dg_m", "dg_v", "act_a")], 1))
    w1 = np.zeros((C, HALF), f)
    w1[:, 0:8] = L["ca_w1"].T
    A["ca_w1_T"] = halves(w1)
    wg = np.zeros((8, 2, HALF), f)
    wg[:, 0, 0:C] = L["ca_wh"].T
    wg[:, 1, 0:C] = L["ca_ww"].T
    A["ca_wg_T"] = halves(wg)
    A["ca_params"] = halves(np.stack([L[k] for k in ("ca_g", "ca_b", "ca_m", "ca_v", "ca_a")], 1))
    for layer in ("l1", "l2"):
        Q = {k[8:]: v for k, v in g.items() if k.startswith(layer.upper() + "_conv_")}
        K = HALF + C
        w = np.zeros((K, 2, 2, 3, K), f)
        for d, (wd, bd, near, far) in enumerate(((Q["w_f"], Q["b_f"], 0, HALF), (Q["w_b"], Q["b_b"], HALF, 0))):
            mid = wd[:, :, 1, :].reshape(4, C, 2 * C, 3)
            for m, (a, b) in enumerate(((0, 1), (2, 3))):
                for gate, col in ((a, near), (b, far)):
                    w[near:near + C, d, m, :, col:col + C] = mid[gate, :, C:].transpose(1, 2, 0)
                    w[far:far + C, d, m, :, col:col + C] = mid[gate, :, :C].transpose(1, 2, 0)
                    w[C, d, m, 1, col:col + C] = bd.reshape(4, C)[gate]
        A[layer + "_w"] = w.reshape(K, -1)
        wp = np.zeros((K, HALF), f)
        wp[0:C, 0:C] = Q["w_proj"][:, 0:C].T
        wp[HALF:K, 0:C] = Q["w_proj"][:, C:].T
        A[layer + "_proj_T"] = wp
        A[layer + "_params"] = halves(np.stack([Q["gamma"], Q["beta"]], 1))
    Q = {k[8:]: v for k, v in g.items() if k.startswith("L3_conv_")}
    w1 = np.zeros((HALF + C, HID), f)
    w1[0:C] = w1[HALF:] = Q["w1"].T
    A["b_w1_T"] = w1
    A["b_wd"] = Q["wd"].reshape(GROUPS, GC, 9).transpose(1, 0, 2)
    w2 = np.zeros((GC, GROUPS, HALF), f)
    w2[:, :, 0:C] = Q["w2"].reshape(C, GROUPS, GC).transpose(2, 1, 0)
    A["b_w2_T"] = w2
    A["b_bn_hid"] = np.stack([np.stack([Q[p + n].reshape(GROUPS, GC).T for n in "1d"], 1) for p in "gbmv"], 1)
    A["b_bn_out"] = halves(np.stack([Q[p + "2"] for p in "gbmv"], 1))
    sd = np.zeros((P, 2, P), f)
    for p in range(P):
        sd[p, 0, p] = sd[p, 0, (p + HALF) % P] = 0.5
        sd[p, 1, p], sd[p, 1, (p + HALF) % P] = 0.5, -0.5
    A["sum_dif"] = sd
    return {k: np.ascontiguousarray(v) for k, v in A.items()}


STOP = 99


def kernel(**inputs):
    import concourse.bacc as bacc
    from concourse.bass_utils import run_bass_kernel_spmd

    nc = bacc.Bacc("TRN2", target_bir_lowering=False, num_devices=1)
    arrays = layout(inputs)
    D = {k: nc.dram_tensor("in_" + k, a.shape, mybir.dt.from_np(a.dtype), kind="ExternalInput").ap() for k, a in arrays.items()}
    out = nc.dram_tensor("out_rows", (H, C, B, W), F32, kind="ExternalOutput").ap()
    build(nc, D, out, STOP)
    r = run_bass_kernel_spmd(nc, [{"in_" + k: a for k, a in arrays.items()}], core_ids=[0])
    return np.ascontiguousarray(r.results[0]["out_rows"].transpose(2, 1, 0, 3))
```

```python
import concourse.bass as bass
from concourse import mybir
from contextlib import ExitStack
import numpy as np

F32 = mybir.dt.float32
F32R = mybir.dt.float32r
I32 = mybir.dt.int32
ALU = mybir.AluOpType
ACT = mybir.ActivationFunctionType
AX = mybir.AxisListType

B, C, H, W = 8, 48, 64, 64
P = 128
HALF = 64
HB = B // 2
PAIRS = C // 2
BW = B * W
WP = W + 2
HID = 6 * C
SETS_H = 3
REST = HID - 2 * P
QUARTERS = P // REST
QB = B // QUARTERS
EPS = 1e-5
BANKS = 8

TAPS = 2 * 5 + 1 + 3
OFFSETS = [*range(-2, 3), *range(-2, 3), 0, -1, 0, 1]
SPAN = 2 * H - 1
YCOLS = 2 * PAIRS
COLS = YCOLS + C
PER_BANK = 5


def wait(eng, sem, value):
    if isinstance(value, int) and value <= 0:
        return
    eng.wait_ge(sem, value)


def release(nc, sems):
    nc.clear_and_free_semaphores(sems)
    nc.all_engine_barrier()


def held(eng, value):
    return value if isinstance(value, int) else eng.snap(value)


def peeled(eng, count, body):
    body(0)
    with eng.Fori(1, count) as k:
        body(k)


def axial_filters(nc, D, hs):
    ctx = ExitStack()
    NS = 4
    with ctx:
        sems = []
        ctx.callback(release, nc, sems)

        def sb(name, shape, dt=F32):
            return ctx.enter_context(nc.sbuf_tensor(name, shape, dt))

        def sem(name):
            sems.append(nc.alloc_semaphore(name))
            return sems[-1]

        TR = 2 * 32
        taps = sb("taps", [TR, COLS])
        tapc = sb("tapc", [TR, 2])
        shift = sb("shift", [TR, 1])
        radius = sb("radius", [TR, 1])
        disti = sb("disti", [TR, SPAN], I32)
        dist = sb("dist", [TR, 3, SPAN])
        hat = sb("hat", [TR, SPAN])
        filt = hs[:, 0:COLS * H // BW, :].rearrange("p a n -> p (a n)").rearrange("p (c y) -> p c y", y=H)
        fy = sb("fy", [P, NS, 2, P])
        fx = sb("fx", [P, NS, 2, 2, P])
        xr = sb("xr", [P, NS, BW])
        xc = sb("xc", [P, NS, 2, HB, H])
        stage = sb("stage", [P, NS, 2, 2, BW // 2])
        ps = [ctx.enter_context(nc.psum_tensor(f"axps{i}", [P, BW], F32)) for i in range(BANKS)]

        loaded = sem("a_loaded")
        iota_done = sem("a_iota")
        hat_steps = sem("a_hat_steps")
        hat_ready = sem("a_hat_ready")
        built = sem("a_built")
        kept_a = sem("a_kept_act")
        kept_d = sem("a_kept_dve")
        x_in = [sem(f"a_x_in{s}") for s in range(NS)]
        pair_copied = sem("a_pair_copied")
        filtered = sem("a_filtered")
        staged_a = sem("a_staged_act")
        staged_d = sem("a_staged_dve")
        stored = [sem(f"a_stored{s}") for s in range(NS)]
        zeroed = sem("a_zeroed")

        groups = [list(range(i, min(i + PER_BANK, H))) for i in range(0, H, PER_BANK)]
        NG = len(groups)
        n_act, n_dve = (NG + 1) // 2, NG // 2

        with nc.Block() as block:
            @block.sync
            def _(sp):
                sp.dma_start(taps[:, :], D["tap_table"]).then_inc(loaded, 16)
                sp.dma_start(tapc[:, :], D["tap_consts"]).then_inc(loaded, 16)

                def load(pair, s):
                    sp.dma_start(xr[:, s, :], D["x_rows"][pair]).then_inc(x_in[s], 16)
                    sp.dma_start(xc[:, s], D["x_cols"][pair].rearrange("p (a b y) -> p a b y", a=2, b=HB)
                                 ).then_inc(x_in[s], 16)

                def step(k, last=False):
                    for s in range(NS):
                        pair = held(sp, NS * k + s)
                        ahead = held(sp, NS * k + (s + NS))
                        done = held(sp, NS * k + (s + 1))
                        used = held(sp, 2 * NS * k + (2 * s + 2))
                        if not last:
                            sp.wait_ge(filtered, used)
                            load(ahead, s)
                        sp.wait_ge(staged_a, done)
                        sp.wait_ge(staged_d, done)
                        for q, name in enumerate(("mixed", "edged")):
                            sp.dma_start(D[name][pair], stage[:, s, q].rearrange("p i n -> p (i n)")).then_inc(stored[s], 16)
                for s in range(NS):
                    load(s, s)
                with sp.Fori(0, PAIRS // NS - 1) as k:
                    step(k)
                step(PAIRS // NS - 1, last=True)
                for s in range(NS):
                    sp.wait_ge(stored[s], 32 * (PAIRS // NS))

            @block.gpsimd
            def _(pool):
                pool.iota(disti[:, :], [[1, SPAN]], base=-(H - 1), channel_multiplier=0).then_inc(iota_done, 1)
                pool.wait_ge(iota_done, 1)
                pool.memset(hs[32:64, H // 2:, :], 0.0).then_inc(zeroed, 1)

            @block.scalar
            def _(act):
                for n in range(0, NG, 2):
                    act.wait_ge(built, n + 1)
                    g = groups[n]
                    nc.scalar.activation(filt[:, :, g[0]:g[0] + len(g)],
                                         ps[n % BANKS][:, 0:COLS * len(g)].rearrange("p (i c) -> p c i", c=COLS),
                                         ACT.Copy).then_inc(kept_a, 1)

                def step(k):
                    for s in range(NS):
                        act.wait_ge(filtered, 2 * NS * k + 2 * s + 1)
                        wait(act, stored[s], 32 * k)
                        nc.scalar.activation(stage[:, s, :, 0, :], ps[2 * s][:, :].rearrange("p (q n) -> p q n", q=2),
                                             ACT.Copy).then_inc(staged_a, 1)
                peeled(act, PAIRS // NS, step)

            @block.vector
            def _(dve):
                nc.vector.memset(fy[:, :, :, :], 0.0).then_inc(hat_steps, 1)
                nc.vector.memset(fx[:, :, :, :, :], 0.0).then_inc(hat_steps, 1)
                dve.wait_ge(loaded, 32)
                dve.wait_ge(iota_done, 1)
                nc.vector.tensor_copy(dist[:, 0, :], disti[:, :]).then_inc(hat_steps, 1)
                nc.vector.tensor_scalar(radius[:, :], tapc[:, 1:2], 1.0, None, ALU.max).then_inc(hat_steps, 1)
                dve.wait_ge(hat_steps, 4)
                nc.vector.tensor_tensor(shift[:, :], radius[:, :], tapc[:, 0:1], ALU.mult).then_inc(hat_steps, 1)
                dve.wait_ge(hat_steps, 5)
                nc.vector.tensor_scalar(dist[:, 1, :], dist[:, 0, :], shift[:, 0:1], None, ALU.subtract).then_inc(hat_steps, 1)
                dve.wait_ge(hat_steps, 6)
                nc.vector.tensor_scalar(dist[:, 0, :], dist[:, 1, :], -1.0, 1.0, ALU.mult, ALU.add).then_inc(hat_steps, 1)
                nc.vector.tensor_scalar(dist[:, 2, :], dist[:, 1, :], 1.0, None, ALU.add).then_inc(hat_steps, 1)
                dve.wait_ge(hat_steps, 8)
                nc.vector.tensor_tensor(dist[:, 1, :], dist[:, 0, :], dist[:, 2, :], ALU.min).then_inc(hat_steps, 1)
                dve.wait_ge(hat_steps, 9)
                nc.vector.tensor_scalar(hat[:, :], dist[:, 1, :], 0.0, None, ALU.max).then_inc(hat_ready, 1)
                for n in range(1, NG, 2):
                    dve.wait_ge(built, n + 1)
                    g = groups[n]
                    nc.vector.tensor_copy(filt[:, :, g[0]:g[0] + len(g)],
                                          ps[n % BANKS][:, 0:COLS * len(g)].rearrange("p (i c) -> p c i", c=COLS)
                                          ).then_inc(kept_d, 1)
                dve.wait_ge(kept_a, n_act)
                dve.wait_ge(kept_d, n_dve)

                def copy_pair(pair, s):
                    for q in range(2):
                        for h in range(2):
                            lo = h * HALF
                            nc.vector.tensor_copy(fy[lo:lo + HALF, s, q, lo:lo + HALF].unsqueeze(1),
                                                  filt[lo:lo + HALF, bass.ds(pair + q * PAIRS, 1), :])
                            last = nc.vector.tensor_copy(fx[lo:lo + HALF, s, :, q, lo:lo + HALF],
                                                         filt[q * HALF:(q + 1) * HALF, bass.ds(2 * pair + YCOLS, 2), :])
                    last.then_inc(pair_copied, 1)

                def step(k, last=False):
                    for s in range(NS):
                        dve.wait_ge(filtered, 2 * NS * k + 2 * s + 2)
                        wait(dve, stored[s], 32 * k)
                        nc.vector.tensor_copy(stage[:, s, :, 1, :], ps[2 * s + 1][:, :].rearrange("p (q n) -> p q n", q=2)
                                              ).then_inc(staged_d, 1)
                        if not last:
                            copy_pair(NS * k + (s + NS), s)
                for s in range(NS):
                    copy_pair(s, s)
                step(0)
                with dve.Fori(1, PAIRS // NS - 1) as k:
                    step(k)
                step(PAIRS // NS - 1, last=True)

            @block.tensor
            def _(pe):
                pe.wait_ge(loaded, 32)
                pe.wait_ge(hat_ready, 1)
                for n, g in enumerate(groups):
                    if n >= BANKS:
                        m = n - BANKS
                        pe.wait_ge(kept_d if m % 2 else kept_a, m // 2 + 1)
                    for r, i in enumerate(g):
                        for h in range(2):
                            rows = slice(32 * h, 32 * h + 32)
                            mm = nc.tensor.matmul(ps[n % BANKS][h * HALF:(h + 1) * HALF, r * COLS:(r + 1) * COLS],
                                                  hat[rows, H - 1 - i:2 * H - 1 - i], taps[rows, :], start=(r == 0), stop=True,
                                                  skip_group_check=True)
                    mm.then_inc(built, 1)
                pe.wait_ge(kept_a, n_act)
                pe.wait_ge(kept_d, n_dve)

                def step(k):
                    for s in range(NS):
                        wait(pe, x_in[s], 32 * k + 32)
                        wait(pe, pair_copied, NS * k + s + 1)
                        for i in range(2):
                            bank = ps[2 * s + i]
                            wait(pe, staged_d if i else staged_a, NS * k + s - (NS - 1))
                            for q in range(2):
                                nc.tensor.matmul(bank[:, q * BW // 2:(q + 1) * BW // 2], fy[:, s, q, :],
                                                 xr[:, s, i * BW // 2:(i + 1) * BW // 2],
                                                 start=(q == 0), stop=False, skip_group_check=True)
                            for b in range(HB // 2):
                                for h in range(2):
                                    out = bank[h * HALF:(h + 1) * HALF, :].rearrange("p (q b n) -> p q b n", q=2, n=P)
                                    mm = nc.tensor.matmul(out[:, :, b, :], xc[:, s, h, i * HB // 2 + b, :],
                                                          fx[:, s, h, :, :].rearrange("p q n -> p (q n)"),
                                                          start=False, stop=True, skip_group_check=True)
                            mm.then_inc(filtered, 1)
                peeled(pe, PAIRS // NS, step)


def mix_and_attend(nc, D, hs, out_rows):
    ctx = ExitStack()
    K = HALF + C
    UNIT = 4
    UNITS = H // UNIT
    ROW = HB * W
    UC = UNIT * ROW
    NL = 4
    with ctx:
        sems = []
        ctx.callback(release, nc, sems)

        def sb(name, shape, dt=F32):
            return ctx.enter_context(nc.sbuf_tensor(name, shape, dt))

        def sem(name):
            sems.append(nc.alloc_semaphore(name))
            return sems[-1]

        kept = hs[:, 0:H // 2, :].rearrange("p a n -> p (a n)").rearrange("p (u n) -> p u n", n=UC)
        mixed = sb("mixed_sb", [P, NL, UC])
        edged = sb("edged_sb", [P, NL, UC])
        scaled = sb("scaled", [P, 2, UC])
        total = sb("total", [P, 2, UC])
        wf = sb("wf", [P, P])
        par = sb("par", [P, 9])
        half_power = sb("half_power", [P, 2])
        var = sb("var", [P, 2])
        rs = sb("rs", [P, 2])
        scale = sb("scale", [P, 2])
        shift = sb("shift_bn", [P, 4])
        slope = sb("slope", [P, 1])
        means = sb("means", [P, H * HB])
        w1 = sb("ca_w1", [P, P])
        wg = sb("ca_wg", [P, 2, HALF])
        cpar = sb("ca_par", [P, 5])
        tmp = sb("ca_tmp", [P, 4])
        cs = sb("ca_cs", [P, 3])
        ps = [ctx.enter_context(nc.psum_tensor(f"mxps{i}", [P, BW], F32)) for i in range(4)]
        ps_mean = ctx.enter_context(nc.psum_tensor("ps_mean", [P, BW], F32))
        ps_gate = ctx.enter_context(nc.psum_tensor("ps_gate", [P, BW], F32))
        z = mixed[:, 0:2, :].rearrange("p a n -> p (a n)").rearrange("p (a n) -> p a n", n=BW)
        gate = mixed[:, 2, 0:BW].rearrange("p (a n) -> p a n", a=2)

        loaded = sem("m_loaded")
        steps = sem("m_steps")
        consts = sem("m_consts")
        x_in = [sem(f"m_x_in{s}") for s in range(NL)]
        zero_m, zero_e = sem("m_zero_mixed"), sem("m_zero_edged")
        multiplied = sem("m_multiplied")
        affine = sem("m_affine")
        added = sem("m_added")
        negs = sem("m_negs")
        done = sem("m_done")
        summed = sem("m_summed")
        columns = sem("m_columns")
        squeezed = sem("c_squeezed")
        normed = sem("c_normed")
        zneg = sem("c_zneg")
        zdone = sem("c_zdone")
        widened = sem("c_widened")
        gated = sem("c_gated")
        times_w = sem("c_times_w")
        times_h = sem("c_times_h")
        stored = sem("c_stored")

        def unit_loop(eng, body):
            for u in range(NL):
                body(u, u)
            with eng.Fori(1, UNITS // NL) as k:
                for s in range(NL):
                    body(k * NL + s, s)

        with nc.Block() as block:
            @block.sync
            def _(sp):
                for tile, name in ((wf, "w_fuse_T"), (par, "mix_params"), (w1, "ca_w1_T"), (cpar, "ca_params")):
                    sp.dma_start(tile[:, :], D[name]).then_inc(loaded, 16)
                sp.dma_start(wg[:, :, :], D["ca_wg_T"]).then_inc(loaded, 16)
                def load(u, s):
                    u = held(sp, u)
                    if isinstance(u, int) and u < NL:
                        sp.wait_ge(zero_m, u + 1)
                        sp.wait_ge(zero_e, u + 1)
                    else:
                        sp.wait_ge(added, held(sp, u - (NL - 1)))
                    for q, tile in (("mixed_c", mixed), ("edged_c", edged)):
                        for h in range(2):
                            sp.dma_start(tile[h * HALF:h * HALF + C, s, :].rearrange("p (y n) -> p y n", y=UNIT),
                                         D[q][:, u, :, h, :]).then_inc(x_in[s], 16)
                unit_loop(sp, load)
                for u in range(UNITS):
                    sp.wait_ge(times_h, u + 1)
                    for h in range(2):
                        sp.dma_start(out_rows[u, :, :, h, :],
                                     kept[h * HALF:h * HALF + C, u, :].rearrange("p (y n) -> p y n", y=UNIT)).then_inc(stored, 16)
                sp.wait_ge(stored, 32 * UNITS)

            @block.gpsimd
            def _(pool):
                for s in range(NL):
                    pool.memset(edged[:, s, :], 0.0).then_inc(zero_e, 1)
                pool.memset(half_power[:, :], -0.5).then_inc(steps, 1)
                pool.wait_ge(loaded, 80)
                pool.tensor_scalar(var[:, :], par[:, 3:8:4], EPS, 0.0, ALU.add, ALU.add).then_inc(steps, 1)
                pool.wait_ge(steps, 2)
                pool.tensor_tensor(rs[:, :], var[:, :], half_power[:, :], ALU.pow).then_inc(steps, 1)
                pool.wait_ge(steps, 3)
                pool.tensor_tensor(scale[:, :], rs[:, :], par[:, 0:5:4], ALU.mult).then_inc(steps, 1)
                pool.wait_ge(steps, 4)
                pool.tensor_tensor(shift[:, 0:2], par[:, 2:7:4], scale[:, :], ALU.mult).then_inc(steps, 1)
                pool.wait_ge(steps, 5)
                pool.tensor_tensor(shift[:, 2:4], par[:, 1:6:4], shift[:, 0:2], ALU.subtract).then_inc(steps, 1)
                pool.wait_ge(steps, 6)
                pool.tensor_tensor(shift[:, 0:1], shift[:, 2:3], shift[:, 3:4], ALU.add).then_inc(consts, 1)
                pool.tensor_scalar(slope[:, :], par[:, 8:9], -1.0, 1.0, ALU.mult, ALU.add).then_inc(consts, 1)
                pool.tensor_scalar(tmp[:, 0:1], cpar[:, 3:4], EPS, 0.0, ALU.add, ALU.add).then_inc(steps, 1)
                pool.wait_ge(steps, 7)
                pool.tensor_tensor(tmp[:, 1:2], tmp[:, 0:1], half_power[:, 0:1], ALU.pow).then_inc(steps, 1)
                pool.wait_ge(steps, 8)
                pool.tensor_tensor(tmp[:, 2:3], tmp[:, 1:2], cpar[:, 0:1], ALU.mult).then_inc(steps, 1)
                pool.wait_ge(steps, 9)
                pool.tensor_tensor(tmp[:, 3:4], cpar[:, 2:3], tmp[:, 2:3], ALU.mult).then_inc(steps, 1)
                pool.tensor_scalar(cs[:, 0:1], tmp[:, 2:3], 1.0 / W, 0.0, ALU.mult, ALU.add).then_inc(consts, 1)
                pool.wait_ge(steps, 10)
                pool.tensor_tensor(cs[:, 1:2], cpar[:, 1:2], tmp[:, 3:4], ALU.subtract).then_inc(consts, 1)
                pool.tensor_scalar(cs[:, 2:3], cpar[:, 4:5], -1.0, 0.0, ALU.add, ALU.add).then_inc(consts, 1)

            @block.tensor
            def _(pe):
                pe.wait_ge(loaded, 80)

                def fuse(u, s, k):
                    pe.wait_ge(x_in[s], 64 * k + 64)
                    wait(pe, affine, 2 * u - 2)
                    for j in range(2):
                        nc.tensor.matmul(ps[2 * (s % 2) + j][:, :], wf[0:K, :], mixed[0:K, s, j * BW:(j + 1) * BW],
                                         start=True, stop=True).then_inc(multiplied, 1)

                def add_columns(u, first=False):
                    pe.wait_ge(done, u + 1)
                    for j in range(UNIT):
                        mm = nc.tensor.matmul(ps_mean[:, ROW:2 * ROW], w1[0:K, :],
                                              kept[0:K, bass.ds(u, 1), j * ROW:(j + 1) * ROW].rearrange("p a n -> p (a n)"),
                                              start=(first and j == 0), stop=True, skip_group_check=True)
                    mm.then_inc(columns, 1)
                for u in range(NL):
                    fuse(u, u, 0)
                    if u >= 2:
                        add_columns(u - 2, first=(u == 2))
                with pe.Fori(1, UNITS // NL) as k:
                    for s in range(NL):
                        fuse(k * NL + s, s, k)
                        add_columns(k * NL + (s - 2))
                for u in range(UNITS - 2, UNITS):
                    add_columns(u)
                pe.wait_ge(summed, UNITS)
                nc.tensor.matmul(ps_mean[:, 0:ROW], w1[0:K, :], means[0:K, :], start=False, stop=True,
                                 skip_group_check=True).then_inc(squeezed, 1)
                pe.wait_ge(zdone, 1)
                for a in range(2):
                    for h in range(2):
                        lo = h * HALF
                        mm = nc.tensor.matmul(ps_gate[lo:lo + HALF, a * ROW:(a + 1) * ROW],
                                              wg[lo:lo + HALF, a, :], z[lo:lo + HALF, 2, a * ROW:(a + 1) * ROW],
                                              start=(a == 0), stop=True, skip_group_check=True)
                mm.then_inc(widened, 1)

            @block.scalar
            def _(act):
                act.wait_ge(consts, 5)

                def step(u, s):
                    t = s % 2
                    wait(act, done, u - 1)
                    for j in range(2):
                        act.wait_ge(multiplied, 2 * u + (j + 1))
                        nc.scalar.activation(scaled[:, t, j * BW:(j + 1) * BW], ps[2 * t + j][:, :], ACT.Identity,
                                             bias=shift[:, 0:1], scale=scale[:, 0:1]).then_inc(affine, 1)
                    act.wait_ge(added, u + 1)
                    nc.scalar.activation(scaled[:, t, :], total[:, t, :], ACT.Relu, scale=-1.0).then_inc(negs, 1)
                unit_loop(act, step)
                act.wait_ge(squeezed, 1)
                nc.scalar.activation(z[:, 0, :], ps_mean[:, :], ACT.Identity, bias=cs[:, 1:2], scale=cs[:, 0:1]).then_inc(normed, 1)
                act.wait_ge(widened, 1)
                nc.scalar.activation(gate, ps_gate[:, :].rearrange("p (a n) -> p a n", a=2), ACT.Sigmoid).then_inc(gated, 1)

            @block.vector
            def _(dve):
                for s in range(NL):
                    nc.vector.memset(mixed[:, s, :], 0.0).then_inc(zero_m, 1)
                dve.wait_ge(consts, 2)
                x_sums = means[:, :].rearrange("p (u n) -> p u n", u=UNITS)

                def add_rows(u):
                    dve.wait_ge(done, u + 1)
                    nc.vector.tensor_reduce(x_sums[:, bass.ds(u, 1), :].rearrange("p a n -> p (a n)"),
                                            kept[:, bass.ds(u, 1), :].rearrange("p a (n w) -> p (a n) w", w=W),
                                            AX.X, ALU.add).then_inc(summed, 1)

                def step(u, s, k):
                    t = s % 2
                    dve.wait_ge(affine, 2 * u + 2)
                    dve.wait_ge(x_in[s], 64 * k + 64)
                    nc.vector.scalar_tensor_tensor(total[:, t, :], edged[:, s, :], scale[:, 1:2], scaled[:, t, :],
                                                   ALU.mult, ALU.add).then_inc(added, 1)
                    if not (isinstance(u, int) and u == 0):
                        add_rows(u - 1)
                    dve.wait_ge(negs, u + 1)
                    nc.vector.scalar_tensor_tensor(kept[:, bass.ds(u, 1), :].rearrange("p a n -> p (a n)"), scaled[:, t, :],
                                                   slope[:, 0:1], total[:, t, :], ALU.mult, ALU.add).then_inc(done, 1)
                for u in range(NL):
                    step(u, u, 0)
                with dve.Fori(1, UNITS // NL) as k:
                    for s in range(NL):
                        step(k * NL + s, s, k)
                add_rows(UNITS - 1)
                dve.wait_ge(normed, 1)
                nc.vector.tensor_scalar(z[:, 1, :], z[:, 0, :], 0.0, cs[:, 2:3], ALU.min, ALU.mult).then_inc(zneg, 1)
                dve.wait_ge(zneg, 1)
                nc.vector.tensor_tensor(z[:, 2, :], z[:, 0, :], z[:, 1, :], ALU.add).then_inc(zdone, 1)
                dve.wait_ge(gated, 1)

                def by_column(u):
                    rows = kept[:, bass.ds(u, 1), :].rearrange("p a (y n) -> p (a y) n", y=UNIT)
                    nc.vector.tensor_tensor(rows, rows, gate[:, 1, :].unsqueeze(1).broadcast_to([P, UNIT, ROW]),
                                            ALU.mult).then_inc(times_w, 1)

                def by_row(u):
                    rows = kept[:, bass.ds(u, 1), :].rearrange("p a (n w) -> p (a n) w", w=W)
                    a_h = gate[:, 0, :].rearrange("p (u n) -> p u n", u=UNITS)
                    dve.wait_ge(times_w, u + 1)
                    nc.vector.tensor_tensor(rows, rows, a_h[:, bass.ds(u, 1), :].rearrange("p a n -> p (a n)").unsqueeze(2)
                                            .broadcast_to([P, UNIT * HB, W]), ALU.mult).then_inc(times_h, 1)
                by_column(0)
                with dve.Fori(1, UNITS) as u:
                    by_column(u)
                    by_row(u - 1)
                by_row(UNITS - 1)


def lstm_scans(nc, D, hs, rows_in, weights, tag):
    ctx = ExitStack()
    near, far = (0, HALF), (HALF, 0)
    K = HALF + C
    PART = HB * W
    parts = [slice(j * PART, (j + 1) * PART) for j in range(2)]
    with ctx:
        sems = []
        ctx.callback(release, nc, sems)

        def sb(name, shape, dt=F32):
            return ctx.enter_context(nc.sbuf_tensor(name + tag, shape, dt))

        def sem(name):
            sems.append(nc.alloc_semaphore(name + tag))
            return sems[-1]

        NW = 2 * 2 * 3 * K
        w = sb("w", [K, NW])
        w_hi = sb("w_hi", [K, 2, 2, 3, K], F32R)
        w_lo = sb("w_lo", [K, 2, 2, 3, K], F32R)
        xf = sb("xf", [P, 2, BW])
        xh = sb("xh", [P, 2, 2, 2, B, WP], F32R)
        gate_if = sb("gate_if", [P, 2, BW])
        gate_g = sb("gate_g", [P, 2, BW])
        keep = sb("keep", [P, 2, BW])
        add = sb("add", [P, 2, BW])
        cell = ctx.enter_context(nc.psum_tensor("cell" + tag, [P, 2, BW], F32))
        tanh_c = ctx.enter_context(nc.psum_tensor("tanh_c" + tag, [P, 2, BW], F32))
        ps = [[ctx.enter_context(nc.psum_tensor(f"gates{d}{m}" + tag, [P, BW], F32)) for m in range(2)] for d in range(2)]

        w_loaded = sem("w_loaded")
        w_split = sem("w_split")
        cleared = [sem(f"cleared{d}") for d in range(2)]
        x_in = [[sem(f"x_in{d}{s}") for s in range(2)] for d in range(2)]
        x_hi = [sem(f"x_hi{d}") for d in range(2)]
        x_lo = [sem(f"x_lo{d}") for d in range(2)]
        gates = [[sem(f"gates_if{d}"), sem(f"gates_go{d}")] for d in range(2)]
        sig_if = [sem(f"sig_if{d}") for d in range(2)]
        tanh_g = [sem(f"tanh_g{d}") for d in range(2)]
        tanhs = [sem(f"tanhs{d}") for d in range(2)]
        kept = [sem(f"kept{d}") for d in range(2)]
        added = [sem(f"added{d}") for d in range(2)]
        cells = [sem(f"cells{d}") for d in range(2)]
        h_hi = [sem(f"h_hi{d}") for d in range(2)]
        h_full = [sem(f"h_full{d}") for d in range(2)]
        h_lo = [sem(f"h_lo{d}") for d in range(2)]

        def clear(eng, ops, d):
            ops.memset(xh[:, d].bitcast(F32), 0.0).then_inc(cleared[d], 1)
            eng.wait_ge(cleared[d], 1)
            ops.memset(xh[32:64, d, :, 0].bitcast(F32), 1.0).then_inc(cleared[d], 1)
            eng.wait_ge(cleared[d], 2)
            ops.memset(xh[32:C, d, :, 0].bitcast(F32), 0.0).then_inc(cleared[d], 1)

        with nc.Block() as block:
            @block.sync
            def _(sp):
                sp.dma_start(w[:, :], D[weights]).then_inc(w_loaded, 16)

                def load(row, d, s):
                    sp.dma_start(xf[far[d]:far[d] + C, s, :], rows_in[row]).then_inc(x_in[d][s], 16)
                for s in range(2):
                    load(s, 0, s)
                    load(H - 1 - s, 1, s)
                with sp.Fori(0, H // 2 - 1) as k:
                    for s in range(2):
                        row_f = sp.snap(2 * k + s + 2)
                        row_b = sp.snap(k * -2 + (H - 3 - s))
                        done = sp.snap(2 * k + s + 1)
                        sp.wait_ge(x_lo[0], done)
                        load(row_f, 0, s)
                        sp.wait_ge(x_lo[1], done)
                        load(row_b, 1, s)

            @block.gpsimd
            def _(pool):
                clear(pool, pool, 1)

                def step(k, last=False):
                    for s in range(2):
                        for d in range(2):
                            if d:
                                state_lo(2 * k + s, 2 * k + s, 0, s)
                            elif s:
                                state_lo(2 * k, k * -2 + (H - 1), 1, 0)
                            elif not (isinstance(k, int) and k == 0):
                                state_lo(2 * k - 1, k * -2 + H, 1, 1)
                            if not last:
                                split_lo(2 * k + s + 2, d, s)

                def state_lo(t, row, d, s):
                    n = near[d]
                    pool.wait_ge(h_full[d], t + 1)
                    pool.wait_ge(h_hi[d], t + 2)
                    whole = hs[n:n + C, bass.ds(row, 1), :].rearrange("p a (b w) -> p (a b) w", b=B)
                    pool.tensor_tensor(xh[n:n + C, d, 1 - s, 1, :, 1:W + 1], whole,
                                       xh[n:n + C, d, 1 - s, 0, :, 1:W + 1].bitcast(F32), ALU.subtract).then_inc(h_lo[d], 1)
                def split_lo(t, d, s):
                    pool.wait_ge(x_hi[d], t + 1)
                    pool.tensor_tensor(xh[far[d]:far[d] + C, d, s, 1, :, 1:W + 1],
                                       xf[far[d]:far[d] + C, s, :].rearrange("p (b w) -> p b w", b=B),
                                       xh[far[d]:far[d] + C, d, s, 0, :, 1:W + 1].bitcast(F32),
                                       ALU.subtract).then_inc(x_lo[d], 1)
                for s in range(2):
                    for d in range(2):
                        split_lo(s, d, s)
                step(0)
                with pool.Fori(1, H // 2 - 1) as k:
                    step(k)
                step(H // 2 - 1, last=True)

            @block.tensor
            def _(pe):
                pe.wait_ge(w_split, 2)
                with pe.Fori(0, H // 2) as k:
                    for s in range(2):
                        for d in range(2):
                            pe.wait_ge(x_lo[d], 2 * k + s + 1)
                            pe.wait_ge(h_hi[d], 2 * k + s + 1)

                            def taps(m, weight, part, first, last):
                                for t in range(3):
                                    mm = nc.tensor.matmul(ps[d][m][0:K, :], weight[:, d, m, t, :],
                                                          xh[0:K, d, s, part, :, t:t + W],
                                                          start=(first and t == 0), stop=(last and t == 2))
                                return mm
                            for m in range(2):
                                taps(m, w_hi, 0, True, False)
                                taps(m, w_lo, 0, False, False)
                            pe.wait_ge(h_lo[d], 2 * k + s + 1)
                            for m in range(2):
                                taps(m, w_hi, 1, False, True).then_inc(gates[d][m], 1)

            @block.scalar
            def _(act):
                for d in range(2):
                    act.wait_ge(cleared[d], 3)

                def split_hi(k, d, s):
                    act.wait_ge(x_in[d][s], 16 * k + 16)
                    nc.scalar.activation(xh[far[d]:far[d] + C, d, s, 0, :, 1:W + 1],
                                         xf[far[d]:far[d] + C, s, :].rearrange("p (b w) -> p b w", b=B),
                                         ACT.Copy).then_inc(x_hi[d], 1)
                for s in range(2):
                    for d in range(2):
                        split_hi(0, d, s)

                def step(k, last=False):
                    for s in range(2):
                        for d in range(2):
                            n, f = near[d], far[d]
                            act.wait_ge(gates[d][0], 2 * k + s + 1)
                            nc.scalar.activation(gate_if[0:K, d, :], ps[d][0][0:K, :], ACT.Sigmoid).then_inc(sig_if[d], 1)
                            act.wait_ge(gates[d][1], 2 * k + s + 1)
                            nc.scalar.activation(gate_g[n:n + C, d, :], ps[d][1][n:n + C, :], ACT.Tanh).then_inc(tanh_g[d], 1)
                            nc.scalar.activation(gate_g[f:f + C, d, :], ps[d][1][f:f + C, :], ACT.Sigmoid).then_inc(tanh_g[d], 1)
                            if not last:
                                split_hi(k + 1, d, s)
                            for j, part in enumerate(parts):
                                act.wait_ge(cells[d], 4 * k + 2 * s + (j + 3))
                                nc.scalar.activation(tanh_c[f:f + C, j, 0:PART], cell[f:f + C, j, 0:PART],
                                                     ACT.Tanh).then_inc(tanhs[d], 1)
                with act.Fori(0, H // 2 - 1) as k:
                    step(k)
                step(H // 2 - 1, last=True)

            @block.vector
            def _(dve):
                clear(dve, nc.vector, 0)
                for d in range(2):
                    for j in range(2):
                        nc.vector.memset(cell[far[d]:far[d] + C, j, 0:PART], 0.0).then_inc(cells[d], 1)
                dve.wait_ge(w_loaded, 16)
                flat_hi = w_hi[:, :, :, :, :].rearrange("p a b c n -> p (a b c n)")
                flat_lo = w_lo[:, :, :, :, :].rearrange("p a b c n -> p (a b c n)")
                nc.vector.tensor_copy(flat_hi, w[:, :]).then_inc(w_split, 1)
                dve.wait_ge(w_split, 1)
                nc.vector.tensor_tensor(flat_lo, w[:, :], flat_hi.bitcast(F32), ALU.subtract).then_inc(w_split, 1)
                for d in range(2):
                    dve.wait_ge(cleared[d], 3)
                for d in range(2):
                    nc.vector.memset(keep[:, d, :], 0.0).then_inc(h_hi[d], 1)
                    nc.vector.memset(add[:, d, :], 0.0).then_inc(h_lo[d], 1)

                def step(k, last=False):
                    for s in range(2):
                        for d in range(2):
                            n, f = near[d], far[d]
                            dve.wait_ge(cells[d], 4 * k + 2 * s + 2)
                            dve.wait_ge(sig_if[d], 2 * k + s + 1)
                            nc.vector.tensor_tensor(keep[n:n + C, d, :].rearrange("p (j n) -> p j n", j=2),
                                                    gate_if[f:f + C, d, :].rearrange("p (j n) -> p j n", j=2),
                                                    cell[f:f + C, :, 0:PART], ALU.mult).then_inc(kept[d], 1)
                            dve.wait_ge(tanh_g[d], 4 * k + 2 * s + 1)
                            nc.vector.tensor_tensor(add[n:n + C, d, :], gate_if[n:n + C, d, :], gate_g[n:n + C, d, :],
                                                    ALU.mult).then_inc(added[d], 1)
                            dve.wait_ge(kept[d], 2 * k + s + 1)
                            dve.wait_ge(added[d], 2 * k + s + 1)
                            for j, part in enumerate(parts):
                                nc.vector.tensor_tensor(cell[f:f + C, j, 0:PART], keep[n:n + C, d, part],
                                                        add[n:n + C, d, part], ALU.add).then_inc(cells[d], 1)
                            for j, part in enumerate(parts):
                                dve.wait_ge(tanhs[d], 4 * k + 2 * s + (j + 1))
                                hi = nc.vector.tensor_tensor(xh[n:n + C, d, 1 - s, 0, j * HB:(j + 1) * HB, 1:W + 1],
                                                             gate_g[f:f + C, d, part].rearrange("p (b w) -> p b w", b=HB),
                                                             tanh_c[f:f + C, j, 0:PART].rearrange("p (b w) -> p b w", b=HB),
                                                             ALU.mult)
                            hi.then_inc(h_hi[d], 1)
                            row = 2 * k + s if d == 0 else k * -2 + (H - 1 - s)
                            whole = hs[n:n + C, bass.ds(row, 1), :].rearrange("p a n -> p (a n)")
                            nc.vector.tensor_tensor(whole.rearrange("p (j n) -> p j n", j=2),
                                                    gate_g[f:f + C, d, :].rearrange("p (j n) -> p j n", j=2),
                                                    tanh_c[f:f + C, :, 0:PART],
                                                    ALU.mult).then_inc(h_full[d], 1)
                with dve.Fori(0, H // 2 - 1) as k:
                    step(k)
                step(H // 2 - 1, last=True)


def project_and_norm(nc, D, hs, rows_in, rows_out, weights, params, tag):
    ctx = ExitStack()
    K = HALF + C
    HH = H // 2
    UNIT = 4
    with ctx:
        sems = []
        ctx.callback(release, nc, sems)

        def sb(name, shape, dt=F32):
            return ctx.enter_context(nc.sbuf_tensor(name + tag, shape, dt))

        def sem(name):
            sems.append(nc.alloc_semaphore(name + tag))
            return sems[-1]

        w = sb("pw", [K, HALF])
        par = sb("ppar", [P, 2])
        sumdif = sb("sumdif", [P, 2, P])
        stats = sb("stats", [P, HH, 6])
        mv = sb("mv", [P, 2])
        tot = sb("tot", [P, 4])
        tmp = sb("ptmp", [P, 6])
        cs = sb("pcs", [P, 2])
        ps = [ctx.enter_context(nc.psum_tensor(f"pps{i}" + tag, [P, BW], F32)) for i in range(BANKS - 1)]
        ps_stat = ctx.enter_context(nc.psum_tensor("ps_stat" + tag, [P, BW], F32))
        NB = BANKS - 1

        loaded = sem("p_loaded")
        cleared = sem("p_cleared")
        projected = sem("projected")
        kept = sem("y_kept")
        counted = sem("counted")
        aggregated = sem("aggregated")
        shared = sem("shared")
        steps = sem("p_steps")
        consts = sem("p_consts")
        r_in = sem("r_in")
        normed = sem("p_normed")
        valued = sem("valued")
        stored = sem("p_stored")

        with nc.Block() as block:
            @block.sync
            def _(sp):
                sp.dma_start(w[:, :], D[weights]).then_inc(loaded, 16)
                sp.dma_start(par[:, :], D[params]).then_inc(loaded, 16)
                sp.dma_start(sumdif[:, :, :], D["sum_dif"]).then_inc(loaded, 16)

                for y in range(0, HH, UNIT):
                    sp.wait_ge(projected, y + UNIT)
                    for h in range(2):
                        sp.dma_start(hs[h * HALF:h * HALF + C, HH + y:HH + y + UNIT, :],
                                     rows_in[h * HH + y:h * HH + y + UNIT].rearrange("y c n -> c y n")).then_inc(r_in, 16)
                for y in range(0, HH, UNIT):
                    sp.wait_ge(valued, y + UNIT)
                    for h in range(2):
                        sp.dma_start(rows_out[h * HH + y:h * HH + y + UNIT].rearrange("y c n -> c y n"),
                                     hs[h * HALF:h * HALF + C, y:y + UNIT, :]).then_inc(stored, 16)
                sp.wait_ge(stored, 32 * (HH // UNIT))

            @block.gpsimd
            def _(pool):
                pool.memset(tmp[:, 5:6], -0.5).then_inc(cleared, 1)
                pool.wait_ge(cleared, 1)
                pool.wait_ge(steps, 2)
                pool.tensor_tensor(tmp[:, 1:2], tmp[:, 0:1], tmp[:, 5:6], ALU.pow).then_inc(steps, 1)
                pool.wait_ge(steps, 3)
                pool.tensor_tensor(cs[:, 0:1], tmp[:, 1:2], par[:, 0:1], ALU.mult).then_inc(steps, 1)
                pool.wait_ge(steps, 4)
                pool.tensor_tensor(tmp[:, 2:3], tot[:, 0:1], cs[:, 0:1], ALU.mult).then_inc(steps, 1)
                pool.wait_ge(steps, 5)
                pool.tensor_tensor(cs[:, 1:2], par[:, 1:2], tmp[:, 2:3], ALU.subtract).then_inc(consts, 1)

            @block.tensor
            def _(pe):
                pe.wait_ge(loaded, 48)
                for y in range(HH):
                    if y >= NB:
                        pe.wait_ge(kept, y - NB + 1)
                    for h in range(2):
                        mm = nc.tensor.matmul(ps[y % NB][h * HALF:(h + 1) * HALF, :], w[:, :], hs[0:K, y + h * HH, :],
                                              start=True, stop=True)
                    mm.then_inc(projected, 1)
                pe.wait_ge(aggregated, 1)
                for a in range(2):
                    mm = nc.tensor.matmul(ps_stat[:, 2 * a:2 * a + 2], sumdif[:, a, :], mv[:, :],
                                          start=(a == 0), stop=True, skip_group_check=True)
                mm.then_inc(shared, 1)

            @block.scalar
            def _(act):
                for y in range(HH):
                    act.wait_ge(projected, y + 1)
                    nc.scalar.activation(hs[:, y, :], ps[y % NB][:, :], ACT.Copy).then_inc(kept, 1)
                act.wait_ge(consts, 1)

                def step(y):
                    row = hs[0:K, bass.ds(y, 1), :].rearrange("p a n -> p (a n)")
                    nc.scalar.activation(row, row, ACT.Relu, bias=cs[0:K, 1:2], scale=cs[0:K, 0:1]).then_inc(normed, 1)
                with act.Fori(0, HH) as y:
                    step(y)

            @block.vector
            def _(dve):
                for y in range(HH):
                    dve.wait_ge(kept, y + 1)
                    nc.vector.bn_stats(stats[:, y, :], hs[:, y, :]).then_inc(counted, 1)
                dve.wait_ge(counted, HH)
                nc.vector.bn_aggr(mv[:, :], stats[:, :, :].rearrange("p a n -> p (a n)")).then_inc(aggregated, 1)
                dve.wait_ge(shared, 1)
                nc.vector.tensor_copy(tot[:, :], ps_stat[:, 0:4]).then_inc(shared, 1)
                dve.wait_ge(shared, 2)
                nc.vector.scalar_tensor_tensor(tmp[:, 3:4], tot[:, 2:3], tot[:, 2:3], tot[:, 1:2], ALU.mult, ALU.add).then_inc(steps, 1)
                dve.wait_ge(steps, 1)
                nc.vector.tensor_scalar(tmp[:, 0:1], tmp[:, 3:4], EPS, None, ALU.add).then_inc(steps, 1)

                dve.wait_ge(r_in, 32 * (HH // UNIT))

                def step(y):
                    row, x = (hs[0:K, bass.ds(y + n, 1), :].rearrange("p a n -> p (a n)") for n in (0, HH))
                    dve.wait_ge(normed, y + 1)
                    nc.vector.tensor_tensor(row, row, x, ALU.add).then_inc(valued, 1)
                with dve.Fori(0, HH) as y:
                    step(y)


def inverted_residual(nc, D, rows_in, out):
    ctx = ExitStack()
    K = HALF + C
    RING = 4
    with ctx:
        sems = []
        ctx.callback(release, nc, sems)

        def sb(name, shape, dt=F32):
            return ctx.enter_context(nc.sbuf_tensor(name, shape, dt))

        def sem(name):
            sems.append(nc.alloc_semaphore(name))
            return sems[-1]

        w1 = sb("b_w1", [K, HID])
        w1_hi = sb("b_w1_hi", [K, 2 * P], F32R)
        w1_lo = sb("b_w1_lo", [K, 2 * P], F32R)
        wd = sb("b_wd", [P, SETS_H, 9])
        w2 = sb("b_w2", [P, 2 + QUARTERS, HALF])
        bn_hid = sb("b_bn_hid", [P, 4, 2, SETS_H])
        bn_out = sb("b_bn_out", [P, 4])
        eye = sb("b_eye", [P, P])
        diag = sb("b_diag", [P, 9, P])
        diag_hi = sb("b_diag_hi", [P, 9, P], F32R)
        diag_lo = sb("b_diag_lo", [P, 9, P], F32R)
        cs = sb("b_cs", [P, 2, 2, SETS_H])
        cso = sb("b_cso", [P, 2])
        tmp = sb("b_tmp", [P, 4, 2 * SETS_H])
        xs = sb("b_xs", [P, RING, BW])
        x3 = sb("b_x3", [P, RING, B, WP], F32R)
        hidden_v = sb("b_hidden_v", [P, RING, B, WP])
        hidden_r = sb("b_hidden_r", [P, RING, QB, WP])
        hidden_t = sb("b_hidden_t", [P, RING, 2, B, WP], F32R)
        whole_t = sb("b_whole_t", [P, 2, B, W])
        acc_v = [ctx.enter_context(nc.psum_tensor(f"b_acc_v{i}", [P, BW], F32)) for i in range(2)]
        acc_r = sb("b_acc_r", [P, 2, QB * W])
        h2 = sb("b_h2", [P, RING, 2, BW])
        h2_r = sb("b_h2_r", [P, RING, QB * W])
        res = sb("b_res", [P, 2, BW])
        scaled = sb("b_scaled", [P, 2, BW])
        o = sb("b_o", [P, 2, BW])
        ps1 = [ctx.enter_context(nc.psum_tensor(f"b_ps1{i}", [P, BW], F32)) for i in range(SETS_H)]
        ps2 = [ctx.enter_context(nc.psum_tensor(f"b_ps2{i}", [P, BW], F32)) for i in range(2)]
        ps3 = ctx.enter_context(nc.psum_tensor("b_ps3", [P, BW], F32))

        loaded = sem("b_loaded")
        cleared = sem("b_cleared")
        rows_cleared = sem("b_rows_cleared")
        steps = sem("b_steps")
        consts = sem("b_consts")
        diags = sem("b_diags")
        w_split = sem("b_w_split")
        x_in = [sem(f"b_x_in{s}") for s in range(RING)]
        r_in = [sem(f"b_r_in{s}") for s in range(2)]
        expanded = sem("b_expanded")
        rows_v = sem("b_rows_v")
        rows_hi = sem("b_rows_hi")
        rows_whole = sem("b_rows_whole")
        rows_lo = sem("b_rows_lo")
        depth_t = sem("b_depth_t")
        first_tap = sem("b_first_tap")
        taps_v = sem("b_taps_v")
        diag_steps = sem("b_diag_steps")
        squashed = sem("b_squashed")
        reduced = sem("b_reduced")
        affine = sem("b_affine")
        x_hi = sem("b_x_hi")
        x_lo = sem("b_x_lo")
        final = sem("b_final")
        stored = [sem(f"b_stored{s}") for s in range(2)]

        def slot(y):
            return y % RING

        with nc.Block() as block:
            @block.sync
            def _(sp):
                for tile, name in ((w1, "b_w1_T"), (wd, "b_wd"), (w2, "b_w2_T"), (bn_hid, "b_bn_hid"), (bn_out, "b_bn_out")):
                    ap = tile[tuple(slice(None) for _ in tile.shape)]
                    sp.dma_start(ap, D[name]).then_inc(loaded, 16)
                def load_x(row, s):
                    for part in range(2):
                        sp.dma_start(xs[part * HALF:part * HALF + C, s, :], rows_in[row]).then_inc(x_in[s], 16)

                def load_r(y, y1, s):
                    for h, row in enumerate((y, y1)):
                        sp.dma_start(res[h * HALF:h * HALF + C, s, :], rows_in[row]).then_inc(r_in[s], 16)

                sp.wait_ge(cleared, 1)
                for y in range(RING):
                    load_x(y, y)
                sp.wait_ge(cleared, 5)
                for s in range(2):
                    load_r(2 * s, 2 * s + 1, s)

                def store(y, y1, s):
                    for h, row in enumerate((y, y1)):
                        sp.dma_start(out[row].rearrange("c b w -> c (b w)"),
                                     o[h * HALF:h * HALF + C, s, :]).then_inc(stored[s], 16)

                def step(k, last=False):
                    for u in range(RING):
                        s = u // 2
                        ahead = held(sp, k * RING + (u + RING))
                        used = held(sp, k * RING + (u + 1))
                        done = held(sp, k * 2 + (s - 1))
                        y, y1 = held(sp, k * RING + (2 * s - 4)), held(sp, k * RING + (2 * s - 3))
                        r, r1 = held(sp, k * RING + 2 * s), held(sp, k * RING + (2 * s + 1))
                        if not last:
                            sp.wait_ge(x_lo, used)
                            load_x(ahead, u)
                        if u % 2 and not (isinstance(k, int) and k == 0):
                            sp.wait_ge(final, done)
                            store(y, y1, s)
                            load_r(r, r1, s)
                step(0)
                with sp.Fori(1, H // RING - 1) as k:
                    step(k)
                step(H // RING - 1, last=True)
                for s in range(2):
                    sp.wait_ge(final, H // 2 - 1 + s)
                    store(H - 4 + 2 * s, H - 3 + 2 * s, s)
                for s in range(2):
                    sp.wait_ge(stored[s], 32 * (H // RING))

            @block.gpsimd
            def _(pool):
                pool.memset(xs[:, :, :], 0.0).then_inc(cleared, 1)
                pool.memset(eye[:, :], 0.0).then_inc(cleared, 1)
                pool.wait_ge(cleared, 2)
                pool.affine_select(out=eye[:, :], in_=eye[:, :], compare_op=ALU.not_equal, fill=1.0, base=0,
                                   pattern=[[-1, P]], channel_multiplier=1).then_inc(cleared, 1)
                pool.memset(x3[:, :, :, :].bitcast(F32), 0.0).then_inc(cleared, 1)
                pool.memset(res[:, :, :], 0.0).then_inc(cleared, 1)
                pool.memset(hidden_r[:, :, :, :], 0.0).then_inc(cleared, 1)
                pool.memset(tmp[:, 3, :], -0.5).then_inc(steps, 1)
                pool.wait_ge(loaded, 80)
                pool.wait_ge(steps, 1)

                def flat(i):
                    return bn_hid[:, i].rearrange("p a g -> p (a g)")
                pool.tensor_scalar(tmp[:, 0, :], flat(3), EPS, 0.0, ALU.add, ALU.add).then_inc(steps, 1)
                pool.wait_ge(steps, 2)
                pool.tensor_tensor(tmp[:, 1, :], tmp[:, 0, :], tmp[:, 3, :], ALU.pow).then_inc(steps, 1)
                pool.wait_ge(steps, 3)
                pool.tensor_tensor(cs[:, 0].rearrange("p a g -> p (a g)"), tmp[:, 1, :], flat(0), ALU.mult).then_inc(steps, 1)
                pool.wait_ge(steps, 4)
                pool.tensor_tensor(tmp[:, 2, :], flat(2), cs[:, 0].rearrange("p a g -> p (a g)"), ALU.mult).then_inc(steps, 1)
                pool.wait_ge(steps, 5)
                pool.tensor_tensor(cs[:, 1].rearrange("p a g -> p (a g)"), flat(1), tmp[:, 2, :], ALU.subtract).then_inc(consts, 1)
                pool.tensor_scalar(tmp[:, 0, 0:1], bn_out[:, 3:4], EPS, 0.0, ALU.add, ALU.add).then_inc(steps, 1)
                pool.wait_ge(steps, 6)
                pool.tensor_tensor(tmp[:, 1, 0:1], tmp[:, 0, 0:1], tmp[:, 3, 0:1], ALU.pow).then_inc(steps, 1)
                pool.wait_ge(steps, 7)
                pool.tensor_tensor(cso[:, 0:1], tmp[:, 1, 0:1], bn_out[:, 0:1], ALU.mult).then_inc(steps, 1)
                pool.wait_ge(steps, 8)
                pool.tensor_tensor(tmp[:, 2, 0:1], bn_out[:, 2:3], cso[:, 0:1], ALU.mult).then_inc(steps, 1)
                pool.wait_ge(steps, 9)
                pool.tensor_tensor(cso[:, 1:2], bn_out[:, 1:2], tmp[:, 2, 0:1], ALU.subtract).then_inc(consts, 1)

                def low_parts(s, count, splits):
                    pool.wait_ge(x_lo, splits)
                    pool.wait_ge(rows_whole, count)
                    pool.tensor_tensor(hidden_t[:, s, 1, :, 1:W + 1], whole_t[:, s % 2],
                                       hidden_t[:, s, 0, :, 1:W + 1].bitcast(F32), ALU.subtract).then_inc(rows_lo, 1)

                def split_lo(count, s, lows=0):
                    pool.wait_ge(x_hi, count)
                    wait(pool, rows_lo, lows)
                    half = slice(HALF, K)
                    pool.tensor_tensor(x3[half, s, :, 1:W + 1], xs[half, s, :].rearrange("p (b w) -> p b w", b=B),
                                       x3[half, s, :, 1:W + 1].bitcast(F32), ALU.subtract).then_inc(x_lo, 1)
                pool.wait_ge(consts, 2)
                for r in range(RING):
                    split_lo(r + 1, r)
                for r in range(2):
                    low_parts(r, r + 1, RING)

                def step(k, last=False):
                    for u in range(RING):
                        if last and u == 2:
                            pool.wait_ge(depth_t, H - 2)
                            pool.wait_ge(taps_v, 17 * (H - 2))
                            for t in (hidden_v, hidden_r):
                                pool.memset(t[:, 0], 0.0).then_inc(rows_v, 1)
                            pool.memset(hidden_t[:, 0, 0].bitcast(F32), 0.0).then_inc(rows_hi, 1)
                            pool.memset(hidden_t[:, 0, 1].bitcast(F32), 0.0).then_inc(rows_lo, 1)
                        elif not last or u < 2:
                            low_parts((u + 2) % RING, k * RING + (u + 3), H if last else k * RING + (u + RING))
                        if not last:
                            split_lo(k * RING + (u + RING + 1), u, k * RING + (u + 3))
                step(0)
                with pool.Fori(1, H // RING - 1) as k:
                    step(k)
                step(H // RING - 1, last=True)

            @block.tensor
            def _(pe):
                pe.wait_ge(w_split, 2)
                pe.wait_ge(cleared, 6)
                pe.wait_ge(rows_cleared, 2)

                def expand(y, s):
                    pe.wait_ge(x_lo, y + 1)
                    wait(pe, rows_whole, y)
                    for g in range(2):
                        for n, w in enumerate((w1_hi, w1_lo)):
                            nc.tensor.matmul(ps1[g][:, :], w[:, g * P:(g + 1) * P],
                                             x3[0:K, s, :, 1:W + 1], start=(n == 0), stop=(n == 1))
                    for q in range(QUARTERS):
                        mm = nc.tensor.matmul(ps1[2][q * REST:(q + 1) * REST, 0:QB * W], w1[:, 2 * P:2 * P + REST],
                                              x3[0:K, s, q * QB:(q + 1) * QB, 1:W + 1].bitcast(F32), start=True, stop=True,
                                              skip_group_check=True)
                    mm.then_inc(expanded, 1)

                def depthwise(y, s):
                    pe.wait_ge(rows_hi, y + 2)
                    wait(pe, squashed, 3 * y - 5)
                    for part, d in ((0, diag_hi), (0, diag_lo), (1, diag_hi)):
                        if part:
                            pe.wait_ge(rows_lo, y + 2)
                        for t in range(9):
                            dy, dx = t // 3 - 1, t % 3
                            mm = nc.tensor.matmul(ps2[s % 2][:, :], d[:, t, :],
                                                  hidden_t[:, slot(s + dy), part, :, dx:dx + W],
                                                  start=(d is diag_hi and part == 0 and t == 0), stop=(part == 1 and t == 8))
                    mm.then_inc(depth_t, 1)

                def reduce_pair(j, s):
                    pe.wait_ge(squashed, j * 6 + 6)
                    wait(pe, affine, j)
                    for g in range(2):
                        for h in range(2):
                            nc.tensor.matmul(ps3[h * HALF:(h + 1) * HALF, :], w2[:, g, :], h2[:, 2 * s + h, g, :],
                                             start=(g == 0), stop=False, skip_group_check=True)
                    for q in range(QUARTERS):
                        for h in range(2):
                            mm = nc.tensor.matmul(ps3[h * HALF:(h + 1) * HALF, q * QB * W:(q + 1) * QB * W],
                                                  w2[:, 2 + q, :], h2_r[:, 2 * s + h, :], start=False, stop=True,
                                                  skip_group_check=True)
                    mm.then_inc(reduced, 1)
                for r in range(2):
                    expand(r, r)
                pe.wait_ge(diags, 2)

                def step(k, first=False, last=False):
                    for u in range(RING):
                        if not last or u < 2:
                            expand(k * RING + (u + 2), (u + 2) % RING)
                        depthwise(k * RING + u, u)
                        if u == 0 and not first:
                            reduce_pair(k * 2 - 1, 1)
                        if u == 2:
                            reduce_pair(k * 2, 0)
                step(0, first=True)
                with pe.Fori(1, H // RING - 1) as k:
                    step(k)
                step(H // RING - 1, last=True)
                reduce_pair(H // 2 - 1, 1)

            @block.scalar
            def _(act):
                act.wait_ge(cleared, 4)

                def hidden(y, s):
                    act.wait_ge(expanded, y + 1)
                    wait(act, depth_t, y - 2)
                    wait(act, taps_v, 17 * y - 34)
                    wait(act, rows_lo, y - 1)

                    def relu(dst, g, n, done):
                        nc.scalar.activation(dst, ps1[g][:, 0:n * W].rearrange("p (b w) -> p b w", w=W), ACT.Relu,
                                             bias=cs[:, 1, 0, g:g + 1], scale=cs[:, 0, 0, g:g + 1]).then_inc(done, 1)
                    relu(hidden_t[:, s, 0, :, 1:W + 1], 1, B, rows_hi)
                    relu(hidden_v[:, s, :, 1:W + 1], 0, B, rows_v)
                    relu(hidden_r[:, s, :, 1:W + 1], 2, QB, rows_v)
                    relu(whole_t[:, s % 2], 1, B, rows_whole)

                def squash(y, s, rows_reduced):
                    def relu(dst, src, g):
                        nc.scalar.activation(dst, src, ACT.Relu, bias=cs[:, 1, 1, g:g + 1],
                                             scale=cs[:, 0, 1, g:g + 1]).then_inc(squashed, 1)
                    wait(act, reduced, rows_reduced)
                    act.wait_ge(depth_t, y + 1)
                    relu(h2[:, s, 1, :], ps2[s % 2][:, :], 1)
                    act.wait_ge(taps_v, 17 * y + 17)
                    relu(h2[:, s, 0, :], acc_v[s % 2][:, :], 0)
                    relu(h2_r[:, s, :], acc_r[:, s % 2, :], 2)

                def begin_sums(y, s):
                    wait(act, rows_v, 2 * y)
                    wait(act, squashed, 3 * y - 4)
                    nc.scalar.activation(acc_v[s % 2][:, :].rearrange("p (b w) -> p b w", w=W),
                                         hidden_v[:, slot(s - 1), :, 0:W], ACT.Copy, scale=wd[:, 0, 0:1]).then_inc(first_tap, 1)

                def affine_rows(j, s):
                    act.wait_ge(reduced, j + 1)
                    wait(act, final, j - 1)
                    nc.scalar.activation(scaled[:, s, :], ps3[:, :], ACT.Identity, bias=cso[:, 1:2],
                                         scale=cso[:, 0:1]).then_inc(affine, 1)

                def split_hi(k, s):
                    act.wait_ge(x_in[s], 32 * k + 32)
                    wait(act, expanded, k * RING + (s - RING + 1))
                    nc.scalar.activation(x3[0:K, s, :, 1:W + 1], xs[0:K, s, :].rearrange("p (b w) -> p b w", b=B),
                                         ACT.Copy).then_inc(x_hi, 1)
                for r in range(RING):
                    split_hi(0, r)
                act.wait_ge(consts, 2)
                act.wait_ge(cleared, 6)
                act.wait_ge(rows_cleared, 2)
                for r in range(2):
                    hidden(r, r)
                    begin_sums(r, r)

                def step(k, first=False, last=False):
                    for u in range(RING):
                        if not last or u < 2:
                            hidden(k * RING + (u + 2), (u + 2) % RING)
                        if not last:
                            split_hi(k + 1, u)
                        squash(k * RING + u, u, k * 2 + (u // 2 - 1))
                        if not last or u < 2:
                            begin_sums(k * RING + (u + 2), (u + 2) % RING)
                        if u % 2 == 0 and not (first and u == 0):
                            affine_rows(k * 2 + (u // 2 - 1), (u // 2 - 1) % 2)
                step(0, first=True)
                with act.Fori(1, H // RING - 1) as k:
                    step(k)
                step(H // RING - 1, last=True)
                affine_rows(H // 2 - 1, 1)

            @block.vector
            def _(dve):
                nc.vector.memset(hidden_t[:, :, :, :, :].bitcast(F32), 0.0).then_inc(rows_cleared, 1)
                nc.vector.memset(hidden_v[:, :, :, :], 0.0).then_inc(rows_cleared, 1)
                dve.wait_ge(loaded, 80)
                nc.vector.tensor_copy(w1_hi[:, :], w1[:, 0:2 * P]).then_inc(w_split, 1)
                dve.wait_ge(w_split, 1)
                nc.vector.tensor_tensor(w1_lo[:, :], w1[:, 0:2 * P], w1_hi[:, :].bitcast(F32), ALU.subtract).then_inc(w_split, 1)
                dve.wait_ge(cleared, 3)
                for t in range(9):
                    nc.vector.tensor_scalar(diag[:, t, :], eye[:, :], wd[:, 1, t:t + 1], None, ALU.mult).then_inc(diag_steps, 1)
                dve.wait_ge(diag_steps, 9)

                def flat(t):
                    return t[:, :, :].rearrange("p a n -> p (a n)")
                nc.vector.tensor_copy(flat(diag_hi), flat(diag)).then_inc(diags, 1)
                dve.wait_ge(diags, 1)
                nc.vector.tensor_tensor(flat(diag_lo), flat(diag), flat(diag_hi).bitcast(F32), ALU.subtract).then_inc(diags, 1)

                def depthwise(y, s):
                    dve.wait_ge(rows_v, 2 * y + 4)
                    wait(dve, squashed, 3 * y - 3)
                    for t in range(9):
                        dy, dx = t // 3 - 1, t % 3
                        for i, (rows, total, g) in enumerate(((hidden_v, acc_v[s % 2][:, :], 0),
                                                             (hidden_r, acc_r[:, s % 2, :], 2))):
                            sums = total.rearrange("p (b w) -> p b w", w=W)
                            src = rows[:, slot(s + dy), :, dx:dx + W]
                            if g == 0 and t == 0:
                                continue
                            if t:
                                if g == 0 and t == 1:
                                    dve.wait_ge(first_tap, y + 1)
                                else:
                                    dve.wait_ge(taps_v, 17 * y + (2 * t - 2 + i))
                                nxt = nc.vector.scalar_tensor_tensor(sums, src, wd[:, g, t:t + 1], sums, ALU.mult, ALU.add)
                            else:
                                nxt = nc.vector.tensor_scalar(sums, src, wd[:, g, t:t + 1], None, ALU.mult)
                            nxt.then_inc(taps_v, 1)

                def finish(j, s, earlier):
                    dve.wait_ge(affine, j + 1)
                    dve.wait_ge(r_in[s], 32 * earlier + 32)
                    wait(dve, stored[s], 32 * earlier)
                    nc.vector.tensor_tensor(o[:, s, :], scaled[:, s, :], res[:, s, :], ALU.add).then_inc(final, 1)

                def step(k):
                    for u in range(RING):
                        depthwise(k * RING + u, u)
                        if u == 1 and not (isinstance(k, int) and k == 0):
                            finish(k * 2 - 1, 1, k - 1)
                        if u == 3:
                            finish(k * 2, 0, k)
                step(0)
                step(1)
                with dve.Fori(2, H // RING) as k:
                    step(k)
                finish(H // 2 - 1, 1, H // RING - 1)


def build(nc, D, out):
    ctx = ExitStack()
    with ctx:
        hs_ctx = ctx.enter_context(ExitStack())
        hs = hs_ctx.enter_context(nc.sbuf_tensor("hs", [P, H, BW], F32))
        mixed = nc.dram_tensor("mixed", (PAIRS, P, BW), F32, kind="Internal").ap()
        edged = nc.dram_tensor("edged", (PAIRS, P, BW), F32, kind="Internal").ap()
        D = dict(D, mixed=mixed, edged=edged)
        for q in ("mixed", "edged"):
            D[q + "_c"] = D[q].rearrange("k (a u y) (h n) -> (k a) u y h n", a=2, y=4, h=2)
        rows = [nc.dram_tensor(f"rows{i}", (H, C, BW), F32, kind="Internal").ap() for i in range(3)]
        axial_filters(nc, D, hs)
        mix_and_attend(nc, D, hs, rows[0].rearrange("(u y) c (h n) -> u c y h n", y=4, h=2))
        for n, layer in enumerate(("l1", "l2")):
            lstm_scans(nc, D, hs, rows[n], layer + "_w", "_" + layer)
            project_and_norm(nc, D, hs, rows[n], rows[n + 1], layer + "_proj_T", layer + "_params", "_" + layer)
        hs_ctx.close()
        inverted_residual(nc, D, rows[2], out)


def halves(rows, n=HALF):
    rows = np.asarray(rows)
    out = np.zeros((P,) + rows.shape[1:], rows.dtype)
    out[0:rows.shape[0]] = rows
    out[HALF:HALF + rows.shape[0]] = rows
    return out


def layout(inputs):
    g = {k: np.asarray(v) for k, v in inputs.items()}
    f = np.float32
    x = g["x"]
    A = {}
    A["x_rows"] = x.reshape(B, PAIRS, 2, H, W).transpose(1, 2, 3, 0, 4).reshape(PAIRS, P, BW)
    A["x_cols"] = x.reshape(HB, 2, PAIRS, 2, H, W).transpose(2, 1, 5, 3, 0, 4).reshape(PAIRS, P, 2 * HB * H)
    L = {k[8:]: v for k, v in g.items() if k.startswith("L0_conv_")}
    table = np.zeros((2 * 32, COLS), f)
    for h in range(2):
        ay, ey, x_cols = slice(0, PAIRS), slice(PAIRS, YCOLS), slice(YCOLS, COLS)
        rows = table[32 * h:32 * h + TAPS]
        rows[0:5, ay] = L["wh_m"][h::2].T
        rows[5:10, ay] = L["wh_l"][h::2].T
        rows[10, ay] = 2.0
        rows[10, ey] = 1.0
        rows[11:14, ey] = L["dg_wh"][h::2].T
        if h == 0:
            rows[0:5, x_cols] = L["ww_m"].T
            rows[5:10, x_cols] = L["ww_l"].T
        else:
            rows[11:14, x_cols] = L["dg_ww"].T
    A["tap_table"] = table
    consts = np.zeros((2 * 32, 2), f)
    for lo in (0, 32):
        consts[lo:lo + TAPS, 0] = OFFSETS
        consts[lo:lo + TAPS, 1] = 1.0
        consts[lo:lo + 5, 1] = L["r_m"]
        consts[lo + 5:lo + 10, 1] = L["r_l"]
    A["tap_consts"] = consts
    wf = np.zeros((P, P), f)
    for lo in (0, HALF):
        wf[lo:lo + C, lo:lo + C] = L["w_fuse"].T
    A["w_fuse_T"] = wf
    A["mix_params"] = halves(np.stack([L[k] for k in ("bnf_g", "bnf_b", "bnf_m", "bnf_v", "dg_g", "dg_b", "dg_m", "dg_v", "act_a")], 1))
    w1 = np.zeros((P, P), f)
    for lo in (0, HALF):
        w1[lo:lo + C, lo:lo + 8] = L["ca_w1"].T
    A["ca_w1_T"] = w1
    wg = np.zeros((8, 2, HALF), f)
    wg[:, 0, 0:C] = L["ca_wh"].T
    wg[:, 1, 0:C] = L["ca_ww"].T
    A["ca_wg_T"] = halves(wg)
    A["ca_params"] = halves(np.stack([L[k] for k in ("ca_g", "ca_b", "ca_m", "ca_v", "ca_a")], 1))
    for layer in ("l1", "l2"):
        Q = {k[8:]: v for k, v in g.items() if k.startswith(layer.upper() + "_conv_")}
        K = HALF + C
        w = np.zeros((K, 2, 2, 3, K), f)
        for d, (wd, bd, near, far) in enumerate(((Q["w_f"], Q["b_f"], 0, HALF), (Q["w_b"], Q["b_b"], HALF, 0))):
            mid = wd[:, :, 1, :].reshape(4, C, 2 * C, 3)
            for m, (a, b) in enumerate(((0, 1), (2, 3))):
                for gate, col in ((a, near), (b, far)):
                    w[near:near + C, d, m, :, col:col + C] = mid[gate, :, C:].transpose(1, 2, 0)
                    w[far:far + C, d, m, :, col:col + C] = mid[gate, :, :C].transpose(1, 2, 0)
                    w[C, d, m, 1, col:col + C] = bd.reshape(4, C)[gate]
        A[layer + "_w"] = w.reshape(K, -1)
        wp = np.zeros((K, HALF), f)
        wp[0:C, 0:C] = Q["w_proj"][:, 0:C].T
        wp[HALF:K, 0:C] = Q["w_proj"][:, C:].T
        A[layer + "_proj_T"] = wp
        A[layer + "_params"] = halves(np.stack([Q["gamma"], Q["beta"]], 1))
    Q = {k[8:]: v for k, v in g.items() if k.startswith("L3_conv_")}
    def sets(rows):
        return np.stack([rows[0:P], rows[P:2 * P], np.concatenate([rows[2 * P:]] * QUARTERS)], 1)
    w1 = np.zeros((HALF + C, HID), f)
    w1[0:C] = w1[HALF:] = Q["w1"].T
    w2 = np.zeros((P, 2 + QUARTERS, HALF), f)
    for g in range(2):
        w2[:, g, 0:C] = Q["w2"][:, g * P:(g + 1) * P].T
    for q in range(QUARTERS):
        own = slice(q * REST, (q + 1) * REST)
        w2[own, 2 + q, 0:C] = Q["w2"][:, 2 * P:].T
    A["b_w1_T"] = w1
    A["b_w2_T"] = w2
    A["b_wd"] = sets(Q["wd"].reshape(HID, 9))
    A["b_bn_hid"] = np.stack([np.stack([sets(Q[p + n]) for n in "1d"], 1) for p in "gbmv"], 1)
    A["b_bn_out"] = halves(np.stack([Q[p + "2"] for p in "gbmv"], 1))
    sd = np.zeros((P, 2, P), f)
    for p in range(P):
        sd[p, 0, p] = sd[p, 0, (p + HALF) % P] = 0.5
        sd[p, 1, p], sd[p, 1, (p + HALF) % P] = 0.5, -0.5
    A["sum_dif"] = sd
    return {k: np.ascontiguousarray(v) for k, v in A.items()}


def kernel(**inputs):
    import concourse.bacc as bacc
    from concourse.bass_utils import run_bass_kernel_spmd

    nc = bacc.Bacc("TRN2", target_bir_lowering=False, num_devices=1)
    arrays = layout(inputs)
    D = {k: nc.dram_tensor("in_" + k, a.shape, mybir.dt.from_np(a.dtype), kind="ExternalInput").ap() for k, a in arrays.items()}
    out = nc.dram_tensor("out_rows", (H, C, B, W), F32, kind="ExternalOutput").ap()
    build(nc, D, out)
    r = run_bass_kernel_spmd(nc, [{"in_" + k: a for k, a in arrays.items()}], core_ids=[0])
    return np.ascontiguousarray(r.results[0]["out_rows"].transpose(2, 1, 0, 3))
```
